# Optimizing a Trainium2 kernel written in Bass

```python
import numpy as np
import jax
import jax.numpy as jnp

def _softmax(x, axis=-1):
    return jax.nn.softmax(x, axis=axis)

def _gelu(x):
    return jax.nn.gelu(x, approximate=True)

def _silu(x):
    return jax.nn.silu(x)

def _sigmoid(x):
    return jax.nn.sigmoid(x)

def _layernorm(x, axis=-1, eps=1e-05):
    m = jnp.mean(x, axis=axis, keepdims=True)
    v = jnp.var(x, axis=axis, keepdims=True)
    return (x - m) / jnp.sqrt(v + eps)

def _scatter_add(tgt, idx, src, axis=0):
    return tgt.at[idx].add(src)

def _segment_sum(src, seg, n):
    return jax.ops.segment_sum(src, seg, n)
kernel_name = 'mk_gps_d1_gnn_r8_7812ac'

def setup_inputs(seed: int=0):
    np.random.seed(seed)
    _w = jnp.asarray

    def _rec_inputs():
        import jax
        import jax.numpy as jnp
        _gk = jax.random.key(seed)
        x = -0.0003713 + 1 * jax.random.normal(jax.random.fold_in(_gk, 1), (6250, 256), jnp.float32)
        _s = jax.random.randint(jax.random.fold_in(_gk, 2), (100000,), 0, 6250, jnp.int32)
        _d = jax.random.randint(jax.random.fold_in(_gk, 3), (100000,), 0, 6250, jnp.int32)
        _loop = jnp.arange(6250, dtype=jnp.int32)
        src = jnp.concatenate([_s, _d, _loop])
        dst = jnp.concatenate([_d, _s, _loop])
        _o = jnp.argsort(dst, stable=True)
        src = src[_o]
        dst = dst[_o]
        return (x, src, dst)
    x, src, dst = _rec_inputs()

    def _L0_gnn_setup():
        import jax, jax.numpy as jnp
        import numpy as np
        N_NODES = 6250
        N_EDGES = 100000
        F_IN = 256
        HEADS = 4
        C_OUT = 64
        NEG_SLOPE = 0.2
        key = jax.random.key(seed)
        k0, k1, k2, k3, k4, k5 = jax.random.split(key, 6)
        x = jax.random.normal(k0, (N_NODES, F_IN), dtype=jnp.float32)
        edge_index = jax.random.randint(k1, (2, N_EDGES), 0, N_NODES, dtype=jnp.int64)
        s = 1.0 / np.sqrt(F_IN)
        W = jax.random.uniform(k2, (HEADS * C_OUT, F_IN), minval=-s, maxval=s, dtype=jnp.float32)
        att_src = jax.random.normal(k3, (HEADS, C_OUT), dtype=jnp.float32) * 0.1
        att_dst = jax.random.normal(k4, (HEADS, C_OUT), dtype=jnp.float32) * 0.1
        bias = jnp.zeros((HEADS * C_OUT,), dtype=jnp.float32)
        return {'x': x, 'edge_index': edge_index, 'W': W, 'att_src': att_src, 'att_dst': att_dst, 'bias': bias}
    _L0_gnn_all = _L0_gnn_setup()
    _L0_gnn_in = {k: v for k, v in _L0_gnn_all.items() if k in ('W', 'att_src', 'att_dst', 'bias')}
    del _L0_gnn_all

    def _L0_mix_setup():
        import jax, jax.numpy as jnp
        import numpy as np
        HEADS = 8
        DIM_HEAD = 64
        EPS = 1e-05

        def _inst_norm(t):
            mu = jnp.mean(t, axis=-1, keepdims=True)
            var = jnp.var(t, axis=-1, keepdims=True)
            return (t - mu) / jnp.sqrt(var + EPS)
        key = jax.random.key(seed)
        k1, k2, k3, k4 = jax.random.split(key, 4)
        b, n, dim = (4, 1024, 256)
        inner = HEADS * DIM_HEAD
        x = jax.random.normal(k1, (b, n, dim), dtype=jnp.float32)
        w_qkv = jax.random.normal(k2, (dim, 3 * inner), dtype=jnp.float32) * (1.0 / DIM_HEAD)
        w_out = jax.random.normal(k3, (inner, dim), dtype=jnp.float32) * dim ** (-0.5)
        b_out = jax.random.normal(k4, (dim,), dtype=jnp.float32) * 0.01
        return {'x': x, 'w_qkv': w_qkv, 'w_out': w_out, 'b_out': b_out}
    _L0_mix_all = _L0_mix_setup()
    _L0_mix_in = {k: v for k, v in _L0_mix_all.items() if k in ('w_qkv', 'w_out', 'b_out')}
    del _L0_mix_all

    def _L0_ffn_setup():
        import jax, jax.numpy as jnp
        import numpy as np
        BN_EPS = 0.001

        def _bn(h, g, b, m, v):
            return g * (h - m) * jax.lax.rsqrt(v + BN_EPS) + b
        key = jax.random.key(seed)
        ks = jax.random.split(key, 8)
        B, F, Df = (256, 64, 256)
        E, H, D = (8, 256, 256)
        s1 = 1.0 / np.sqrt(Df)
        s2 = 1.0 / np.sqrt(H)
        return {'x': jax.random.normal(ks[0], (B, F, Df), jnp.float32), 'Wr': jax.random.normal(ks[1], (Df, E), jnp.float32) * s1, 'br': jnp.zeros((E,), jnp.float32), 'W1': jax.random.normal(ks[2], (E, Df, H), jnp.float32) * s1, 'b1': jnp.zeros((E, H), jnp.float32), 'g1': jnp.ones((E, H), jnp.float32), 'be1': jnp.zeros((E, H), jnp.float32), 'm1': jnp.zeros((E, H), jnp.float32), 'v1': jnp.ones((E, H), jnp.float32), 'W2': jax.random.normal(ks[3], (E, H, H), jnp.float32) * s2, 'b2': jnp.zeros((E, H), jnp.float32), 'g2': jnp.ones((E, H), jnp.float32), 'be2': jnp.zeros((E, H), jnp.float32), 'm2': jnp.zeros((E, H), jnp.float32), 'v2': jnp.ones((E, H), jnp.float32), 'Wo': jax.random.normal(ks[4], (E, H, D), jnp.float32) * s2, 'bo': jnp.zeros((E, D), jnp.float32)}
    _L0_ffn_all = _L0_ffn_setup()
    _L0_ffn_in = {k: v for k, v in _L0_ffn_all.items() if k in ('Wr', 'br', 'W1', 'b1', 'g1', 'be1', 'm1', 'v1', 'W2', 'b2', 'g2', 'be2', 'm2', 'v2', 'Wo', 'bo')}
    del _L0_ffn_all
    return {'x': x, 'src': src, 'dst': dst, 'L0_gnn_W': _L0_gnn_in['W'], 'L0_gnn_att_src': _L0_gnn_in['att_src'], 'L0_gnn_att_dst': _L0_gnn_in['att_dst'], 'L0_gnn_bias': _L0_gnn_in['bias'], 'L0_mix_w_qkv': _L0_mix_in['w_qkv'], 'L0_mix_w_out': _L0_mix_in['w_out'], 'L0_mix_b_out': _L0_mix_in['b_out'], 'L0_ffn_Wr': _L0_ffn_in['Wr'], 'L0_ffn_br': _L0_ffn_in['br'], 'L0_ffn_W1': _L0_ffn_in['W1'], 'L0_ffn_b1': _L0_ffn_in['b1'], 'L0_ffn_g1': _L0_ffn_in['g1'], 'L0_ffn_be1': _L0_ffn_in['be1'], 'L0_ffn_m1': _L0_ffn_in['m1'], 'L0_ffn_v1': _L0_ffn_in['v1'], 'L0_ffn_W2': _L0_ffn_in['W2'], 'L0_ffn_b2': _L0_ffn_in['b2'], 'L0_ffn_g2': _L0_ffn_in['g2'], 'L0_ffn_be2': _L0_ffn_in['be2'], 'L0_ffn_m2': _L0_ffn_in['m2'], 'L0_ffn_v2': _L0_ffn_in['v2'], 'L0_ffn_Wo': _L0_ffn_in['Wo'], 'L0_ffn_bo': _L0_ffn_in['bo']}

def reference(x, src, dst, L0_gnn_W, L0_gnn_att_src, L0_gnn_att_dst, L0_gnn_bias, L0_mix_w_qkv, L0_mix_w_out, L0_mix_b_out, L0_ffn_Wr, L0_ffn_br, L0_ffn_W1, L0_ffn_b1, L0_ffn_g1, L0_ffn_be1, L0_ffn_m1, L0_ffn_v1, L0_ffn_W2, L0_ffn_b2, L0_ffn_g2, L0_ffn_be2, L0_ffn_m2, L0_ffn_v2, L0_ffn_Wo, L0_ffn_bo):
    import jax
    import jax.numpy as jnp

    def _L0_gnn_ref(x, edge_index, W, att_src, att_dst, bias):
        import jax, jax.numpy as jnp
        import numpy as np
        N_NODES = 6250
        N_EDGES = 100000
        F_IN = 256
        HEADS = 4
        C_OUT = 64
        NEG_SLOPE = 0.2
        N = x.shape[0]
        H, C = att_src.shape
        loops = jnp.arange(N, dtype=edge_index.dtype)
        src = jnp.concatenate([edge_index[0], loops])
        dst = jnp.concatenate([edge_index[1], loops])
        h = (x @ W.T).reshape(N, H, C)
        a_s = jnp.einsum('nhc,hc->nh', h, att_src)
        a_d = jnp.einsum('nhc,hc->nh', h, att_dst)
        e = jax.nn.leaky_relu(a_s[src] + a_d[dst], NEG_SLOPE)
        m = jax.ops.segment_max(e, dst, num_segments=N)
        m = jnp.where(jnp.isfinite(m), m, 0.0)
        p = jnp.exp(e - m[dst])
        denom = jax.ops.segment_sum(p, dst, num_segments=N)
        alpha = p / (denom[dst] + 1e-16)
        msg = alpha[:, :, None] * h[src]
        out = jax.ops.segment_sum(msg, dst, num_segments=N)
        out = out.reshape(N, H * C) + bias
        out = jax.nn.elu(out) + x
        return out

    def _L0_mix_ref(x, w_qkv, w_out, b_out):
        import jax, jax.numpy as jnp
        import numpy as np
        HEADS = 8
        DIM_HEAD = 64
        EPS = 1e-05

        def _inst_norm(t):
            mu = jnp.mean(t, axis=-1, keepdims=True)
            var = jnp.var(t, axis=-1, keepdims=True)
            return (t - mu) / jnp.sqrt(var + EPS)
        b, n, dim = x.shape
        qkv = x @ w_qkv
        q, k, v = jnp.split(qkv, 3, axis=-1)
        to_heads = lambda t: t.reshape(b, n, HEADS, DIM_HEAD).transpose(0, 2, 1, 3)
        q, k, v = (to_heads(q), to_heads(k), to_heads(v))
        k = _inst_norm(k)
        v = _inst_norm(v)
        dots = jnp.einsum('bhnd,bhne->bhde', k, v)
        out = jnp.einsum('bhnd,bhde->bhne', q, dots) * (1.0 / n)
        out = out.transpose(0, 2, 1, 3).reshape(b, n, HEADS * DIM_HEAD)
        return out @ w_out + b_out

    def _L0_ffn_ref(x, Wr, br, W1, b1, g1, be1, m1, v1, W2, b2, g2, be2, m2, v2, Wo, bo):
        import jax, jax.numpy as jnp
        import numpy as np
        BN_EPS = 0.001

        def _bn(h, g, b, m, v):
            return g * (h - m) * jax.lax.rsqrt(v + BN_EPS) + b
        feat = jnp.mean(x, axis=0)
        w = jax.nn.softmax(feat @ Wr + br, axis=-1)
        h = jnp.einsum('bfd,edh->bfeh', x, W1) + b1
        h = jax.nn.relu(_bn(h, g1, be1, m1, v1))
        h = jnp.einsum('bfeh,ehk->bfek', h, W2) + b2
        h = jax.nn.relu(_bn(h, g2, be2, m2, v2))
        y = jnp.einsum('bfeh,ehd->bfed', h, Wo) + bo
        return jnp.einsum('bfed,fe->bfd', y, w)
    edge_index = jnp.stack([src, dst])
    xn = _layernorm(x, axis=-1)
    x = x + _L0_gnn_ref(xn, edge_index, L0_gnn_W, L0_gnn_att_src, L0_gnn_att_dst, L0_gnn_bias) + _L0_mix_ref(xn[None], L0_mix_w_qkv, L0_mix_w_out, L0_mix_b_out)[0]
    x = x + _L0_ffn_ref(_layernorm(x, axis=-1)[None], L0_ffn_Wr, L0_ffn_br, L0_ffn_W1, L0_ffn_b1, L0_ffn_g1, L0_ffn_be1, L0_ffn_m1, L0_ffn_v1, L0_ffn_W2, L0_ffn_b2, L0_ffn_g2, L0_ffn_be2, L0_ffn_m2, L0_ffn_v2, L0_ffn_Wo, L0_ffn_bo)[0]
    return x

_drawn_inputs = setup_inputs


def setup_inputs(seed=0):
    import zlib

    import numpy as np

    out = dict(_drawn_inputs(seed))
    spreads = {'L0_gnn_bias': (0.0, 0.1),
     'L0_ffn_br': (0.0, 0.461),
     'L0_ffn_b1': (0.0, 0.627),
     'L0_ffn_g1': (1.0, 0.6),
     'L0_ffn_be1': (0.0, 0.635),
     'L0_ffn_m1': (0.0, 0.618),
     'L0_ffn_v1': (1.0, 0.6),
     'L0_ffn_b2': (0.0, 0.446),
     'L0_ffn_g2': (1.0, 0.576),
     'L0_ffn_be2': (0.0, 0.468),
     'L0_ffn_m2': (0.0, 0.46),
     'L0_ffn_v2': (1.0, 0.6),
     'L0_ffn_bo': (0.0, 0.333)}
    factors = {'L0_gnn_att_src': 3.136, 'L0_gnn_att_dst': 8.0, 'L0_mix_b_out': 8.0}
    for name, (base, spread) in spreads.items():
        noise = np.random.default_rng([zlib.crc32(name.encode()), seed]).standard_normal(out[name].shape)
        drawn = base * np.exp(spread * noise) if base else spread * noise
        out[name] = jnp.asarray(drawn.astype(out[name].dtype))
    for name, factor in factors.items():
        out[name] = (out[name] * factor).astype(out[name].dtype)
    return out
```

```python
from contextlib import ExitStack

import concourse.bass as bass
from concourse import mybir

F32 = mybir.dt.float32
BF16 = mybir.dt.bfloat16
I32 = mybir.dt.int32
ALU = mybir.AluOpType
ACT = mybir.ActivationFunctionType
AX_X = mybir.AxisListType.X

P = 128
D = 256
KC = D // P
HEADS = 4
C = D // HEADS
HG = C + 1
ROW = HEADS * HG + HEADS
MH = 8
MD = 64
INNER = MH * MD
EXPERTS = 8
SUP = 4
TPS = 4
STEP = P * TPS
RING = 8
MAX_STEPS = 512
EPS = 1e-5
BN_EPS = 1e-3


class Chain:

    def __init__(self, eng, sem, base, per):
        self.eng, self.sem, self.base, self.per, self.n = eng, sem, base, per, 0

    def link(self, ins):
        self.n += 1
        ins.then_inc(self.sem, 1)
        self.eng.wait_ge(self.sem, self.base + self.n)

    def end(self):
        assert self.n == self.per, (self.n, self.per)


def gps_layer(nc, x, sd, dsts, att, w_gnn, w_gnn_t, rows, w_kv, w_q_t, w_out, w_r, bn, w1, w2, wo, bo, out, n_nodes, n_edges):
    NT = x.shape[0] // P
    NSUP = (NT - 1) // SUP
    LAST = NSUP * SUP
    assert NT == LAST + 1 and LAST % 2 == 0
    DCOLS = -(-n_edges // P)
    EMAX = sd.shape[0] - STEP
    h_rows = nc.dram_tensor("h_rows", [NT * P, ROW], F32).ap()

    ctx = ExitStack()
    with ctx:
        def sb(name, shape, dt=F32):
            return ctx.enter_context(nc.sbuf_tensor(name, shape, dt))

        def sem(name):
            return ctx.enter_context(nc.semaphore(name))

        bank = [ctx.enter_context(nc.psum_tensor(f"bank{i}", [P, 512], F32)) for i in range(8)]

        ident = sb("ident", [P, P])
        iota_i = sb("iota_i", [P, MAX_STEPS], I32)
        iota_f = sb("iota_f", [P, MAX_STEPS])
        node_i = sb("node_i", [P, NT], I32)
        node_pf = sb("node_pf", [P, NT])
        base_f = sb("base_f", [P, NT + 1])
        ones = sb("ones", [P, P])
        zeros = sb("zeros", [P, 512], BF16)
        wkv = sb("wkv", [P, KC, 2 * INNER])
        wh = sb("wh", [P, KC, D + 2 * HEADS])
        wg = sb("wg", [P, KC, D])
        attb = sb("attb", [P, KC, 2 * HEADS])
        wqt = sb("wqt", [P, INNER // P, D])
        wout = sb("wout", [P, INNER // P, D])
        wr = sb("wr", [P, KC, EXPERTS])
        rowsb = sb("rowsb", [P, 2 * D + EXPERTS])
        bnp = sb("bnp", [P, 10, 2 * EXPERTS])
        bns = sb("bns", [P, 2, 2 * EXPERTS])
        bnt = sb("bnt", [P, 2, 2 * EXPERTS])
        bob = sb("bob", [EXPERTS, D])
        w1b = sb("w1b", [P, EXPERTS, KC, D])
        w2b = sb("w2b", [P, EXPERTS, KC, D])
        wob = sb("wob", [P, EXPERTS, KC, D])
        mean16 = sb("mean16", [P, KC, 16])
        mean_n = sb("mean_n", [P, NT])
        rstd_n = sb("rstd_n", [P, NT])
        keep_a = sb("keep_a", [P, NT])
        keep_b = sb("keep_b", [P, NT])
        asad = sb("asad", [P, NT, 2 * HEADS])
        adc = sb("adc", [P, NT, 2 * HEADS])
        pself = sb("pself", [P, NT, HEADS])
        gmax = sb("gmax", [P, 2, HEADS])
        msb = sb("msb", [P, KC, D])
        cnt = sb("cnt", [P, NT])
        sched = sb("sched", [1, 8, 64])
        sched_i = sb("sched_i", [1, 4, 64], I32)
        meta = sb("meta", [1, 192], I32)
        steps_i = sb("steps_i", [1, MAX_STEPS], I32)
        steps_f = sb("steps_f", [64, MAX_STEPS])
        cols = sb("cols", [64, 2])
        stats = sb("stats", [P, 6])
        mv = sb("mv", [P, 2])
        small = sb("small", [P, 64])
        rsq = sb("rsq", [P, 8])
        ve1 = sb("ve1", [P, 1])
        rs1 = sb("rs1", [P, 1])
        ve2 = sb("ve2", [P, MH])
        rs2 = sb("rs2", [P, MH])
        rs3 = sb("rs3", [P, MH])
        small2 = sb("small2", [P, NT, HEADS])

        big = sb("big", [P, 26400])
        at = [0]

        def part(n, dt=F32):
            words = -(-n * (2 if dt == BF16 else 4) // 4)
            view = big[:, at[0]:at[0] + words]
            at[0] += words + (-words) % 8
            return view if dt == F32 else view.bitcast(dt)

        dst_all = part(DCOLS, I32)
        below = part(DCOLS, BF16)
        xt = [part(D) for _ in range(2)]
        xn = [part(D) for _ in range(2)]
        xnT = [part(KC * P) for _ in range(2)]
        ksb = [part(INNER) for _ in range(2)]
        vsb = [part(INNER) for _ in range(2)]
        sq = [part(2 * INNER) for _ in range(2)]
        hst = [part(ROW) for _ in range(2)]
        dtb = part(4 * P)
        zsb = part(4 * D)
        at1 = at[0]
        at[0] = 0
        ring = part(RING * TPS * ROW).rearrange("p (u j c) -> p u j c", u=RING, j=TPS)
        idx = part(RING * TPS * 2, I32).rearrange("p (u j c) -> p u j c", u=RING, j=TPS)
        dstrow = part(RING * STEP, I32).rearrange("p (u e) -> p u e", u=RING)
        window = part(P)
        oh = [part(2 * P).rearrange("p (j n) -> p j n", j=2) for _ in range(2)]
        msg = [part(2 * HEADS * HG).rearrange("p (j h c) -> p j h c", j=2, h=HEADS) for _ in range(2)]
        oht = part(TPS * P).rearrange("p (j e) -> p j e", j=TPS)
        prob = part(TPS * HEADS).rearrange("p (j h) -> p j h", j=TPS)
        sc = part(TPS * HEADS).rearrange("p (j h) -> p j h", j=TPS)
        sc2 = part(TPS * HEADS).rearrange("p (j h) -> p j h", j=TPS)
        xin = [part(D) for _ in range(2)]
        hself = [part(ROW) for _ in range(2)]
        mself = part(HEADS * HG)
        xnb = part(D)
        xnTb = part(KC * P)
        kept = part(D)
        gat = part(D)
        neg = part(D)
        zb = part(D)
        zTb = part(KC * SUP * P).rearrange("p (k n) -> p k n", k=KC)
        zTf = part(KC * SUP * P).rearrange("p (k n) -> p k n", k=KC)
        x1b = part(SUP * D).rearrange("p (t c) -> p t c", t=SUP)
        acc = part(SUP * D).rearrange("p (t c) -> p t c", t=SUP)
        wgt = part(SUP * EXPERTS).rearrange("p (t e) -> p t e", t=SUP)
        wgf = part(SUP * EXPERTS).rearrange("p (t e) -> p t e", t=SUP)
        wT = part(P)
        h1 = [part(KC * SUP * P).rearrange("p (k n) -> p k n", k=KC) for _ in range(2)]
        h2 = [part(KC * SUP * P).rearrange("p (k n) -> p k n", k=KC) for _ in range(2)]
        at2 = at[0]
        assert max(at1, at2) <= 26400, (at1, at2)

        acc_ps, small_ps, tp_ps, mix_ps = bank[:4]
        ff_ps = bank[4:]
        k_ps, v_ps = bank[4:6], bank[6:8]
        adg_ps = small_ps[:, 0:TPS * 2 * HEADS].rearrange("p (j c) -> p j c", j=TPS)
        rt_ps = small_ps[:, 64:64 + EXPERTS]
        wT_ps = small_ps[0:EXPERTS, 128:256]

        weights_in = sem("weights_in")
        wgnn_in = sem("wgnn_in")
        experts_in = sem("experts_in")
        dst_in = sem("dst_in")
        const_made = sem("const_made")
        setup_chain = sem("setup_chain")
        was_done = sem("was_done")
        wh_ready = sem("wh_ready")
        weights_ready = sem("weights_ready")
        phase2_ready = sem("phase2_ready")
        x_in = [sem(f"x_in{i}") for i in range(2)]
        normed = sem("normed")
        ln_chain = sem("ln_chain")
        xT_done = sem("xT_done")
        xT_copied = sem("xT_copied")
        k_done = sem("k_done")
        v_done = sem("v_done")
        h_done = sem("h_done")
        squared = sem("squared")
        h_staged = sem("h_staged")
        h_stored = [sem(f"h_stored{i}") for i in range(2)]
        kv_chain = sem("kv_chain")
        v_scaled = sem("v_scaled")
        bn_var = sem("bn_var")
        bn_rooted = sem("bn_rooted")
        x_var = sem("x_var")
        x_rooted = sem("x_rooted")
        kv_var = sem("kv_var")
        kv_rooted = sem("kv_rooted")
        w_recip = sem("w_recip")
        z_done = sem("z_done")
        dt_done = sem("dt_done")
        mid_chain = sem("mid_chain")
        dt_copied = sem("dt_copied")
        z_copied = sem("z_copied")
        m_done = sem("m_done")
        m_copied = sem("m_copied")
        counts_summed = sem("counts_summed")
        sched_rows = sem("sched_rows")
        sched_cols = sem("sched_cols")
        steps_masked = sem("steps_masked")
        steps_summed = sem("steps_summed")
        gmax_local = sem("gmax_local")
        gmax_all = sem("gmax_all")
        self_scores = sem("self_scores")
        self_probs = sem("self_probs")
        idx_in = [sem(f"idx_in{i}") for i in range(RING)]
        gathered = [sem(f"gathered{i}") for i in range(RING)]
        step_begun = sem("step_begun")
        rows_ready = sem("rows_ready")
        oht_ready = sem("oht_ready")
        adg_ready = sem("adg_ready")
        score_chain = sem("score_chain")
        scores_ready = sem("scores_ready")
        probs_ready = sem("probs_ready")
        msg_ready = [sem("msg_a_ready"), sem("msg_b_ready")]
        half_summed = [sem("half_a_summed"), sem("half_b_summed")]
        xin_in = [sem(f"xin_in{i}") for i in range(2)]
        xn_ready = sem("xn_ready")
        xnT2_done = sem("xnT2_done")
        xnT2_copied = sem("xnT2_copied")
        mix_done = sem("mix_done")
        tile_chain = sem("tile_chain")
        self_ready = sem("self_ready")
        tile_summed = sem("tile_summed")
        neg_ready = sem("neg_ready")
        neg_exped = sem("neg_exped")
        z_ready = sem("z_ready")
        zT_done = sem("zT_done")
        zT_copied = sem("zT_copied")
        router_done = sem("router_done")
        logits_ready = sem("logits_ready")
        wexp_done = sem("wexp_done")
        w_ready = sem("w_ready")
        wT_done = sem("wT_done")
        wT_copied = sem("wT_copied")
        bo_done = sem("bo_done")
        tile_done = sem("tile_done")
        ff_done = sem("ff_done")
        relu_done = sem("relu_done")
        acc_done = sem("acc_done")
        handed = sem("handed")
        out_stored = sem("out_stored")

        def part_bases(g, q):
            return (g - 1) * (12 * SUP) + 12 * q, (g - 1) * (8 * SUP) + 8 * q, (g - 1) * (4 * SUP) + 4 * q

        def last_bases(q):
            return NSUP * 12 * SUP + 10 * q, NSUP * 8 * SUP + 8 * q, NSUP * 4 * SUP + 2 * q

        block = ctx.enter_context(nc.Block())

        @block.sync
        def _(sp):
            sp.dma_start(wg[:, :, :], w_gnn.rearrange("(k p) n -> p k n", p=P)).then_inc(wgnn_in, 16)
            sp.dma_start(attb[:, :, :], att.rearrange("(k p) n -> p k n", p=P)).then_inc(wgnn_in, 16)
            sp.dma_start(wh[:, :, 0:D], w_gnn_t.rearrange("(k p) n -> p k n", p=P)).then_inc(wgnn_in, 16)

            def load_x(n, par):
                sp.dma_start(xt[par], x[bass.ds(n * P, P), :]).then_inc(x_in[par], 16)

            def store_h(n, par):
                sp.wait_ge(h_staged, n + 1)
                sp.dma_start(h_rows[bass.ds(n * P, P), :], hst[par]).then_inc(h_stored[par], 16)

            load_x(0, 0)
            load_x(1, 1)
            sp.dma_start(dst_all, dsts[0:P * DCOLS].rearrange("(p c) -> p c", p=P)).then_inc(dst_in, 16)
            for n in range(2):
                sp.wait_ge(normed, n + 1)
                load_x(n + 2, n % 2)
                store_h(n, n % 2)
            with sp.Fori(2, LAST - 2, 2) as n0:
                for par in range(2):
                    sp.wait_ge(normed, n0 + (par + 1))
                    load_x(n0 + (par + 2), par)
                    store_h(n0 + par, par)
            sp.wait_ge(normed, LAST - 1)
            load_x(LAST, 0)
            for n in range(LAST - 2, NT):
                store_h(n, n % 2)

            sp.wait_ge(phase2_ready, 1)

            def edges(s, u, first):
                if not first:
                    sp.wait_ge(msg_ready[1], s - (RING - 1))
                e0 = sp.value_load(steps_i[0:1, bass.ds(s, 1)], min_val=0, max_val=EMAX)
                sp.dma_start(idx[:, u, :, :], sd[bass.ds(e0, STEP), :].rearrange("(p j) c -> p j c", p=P))\
                    .then_inc(idx_in[u], 16)
                sp.dma_start(dstrow[:, u, :], dsts[bass.ds(e0, STEP)].partition_broadcast(P))\
                    .then_inc(idx_in[u], 16)

            for u in range(RING):
                edges(u, u, True)
            rounds = sp.value_load(meta[0:1, 128:129], min_val=2, max_val=MAX_STEPS // RING)
            with sp.Fori(1, rounds) as r:
                for u in range(RING):
                    edges(r * RING + u, u, False)

        @block.gpsimd
        def _(pool):
            pool.memset(ident[:, :], 0.0).then_inc(const_made, 1)
            pool.memset(ones[:, :], 1.0)
            pool.memset(zeros[:, :], 0.0)
            pool.memset(hst[0].rearrange("p (c) -> p c"), 1.0)
            pool.memset(hst[1].rearrange("p (c) -> p c"), 1.0)
            pool.iota(iota_i[:, :], [[1, MAX_STEPS]], base=0, channel_multiplier=0)
            pool.iota(node_i[:, :], [[P, NT]], base=0, channel_multiplier=1).then_inc(const_made, 1)
            pool.wait_ge(const_made, 2)
            pool.affine_select(out=ident[:, :], in_=ident[:, :], compare_op=ALU.not_equal, fill=1.0, base=0,
                               pattern=[[-1, P]], channel_multiplier=1).then_inc(const_made, 1)
            pool.wait_ge(gmax_local, 1)
            pool.partition_all_reduce(gmax[:, 1, :], gmax[:, 0, :], P, bass.bass_isa.ReduceOp.max).then_inc(gmax_all, 1)

            pool.wait_ge(phase2_ready, 1)

            def gather(s, u, first, turn):
                if not first:
                    pool.wait_ge(msg_ready[1], s - (RING - 1))
                pool.wait_ge(idx_in[u], 32 * turn)
                pool.sem_inc(step_begun, 1)
                for j in range(TPS):
                    pool.indirect_dma_start(ring[:, u, j, :], None, h_rows[:, :],
                                            bass.IndirectOffsetOnAxis(ap=idx[:, u, j, 0:1], axis=0))\
                        .then_inc(gathered[u], 16)

            def landed(u, turn):
                pool.wait_ge(gathered[u], 16 * TPS * turn)
                pool.sem_inc(rows_ready, 1)

            for u in range(RING):
                gather(u, u, True, 1)
                if u:
                    landed(u - 1, 1)
            rounds = pool.value_load(meta[0:1, 128:129], min_val=2, max_val=MAX_STEPS // RING)
            with pool.Fori(1, rounds) as r:
                for u in range(RING):
                    gather(r * RING + u, u, False, r + 1)
                    landed((u - 1) % RING, r + 1 if u else r)
            landed(RING - 1, rounds)

        @block.scalar
        def _(act):
            act.dma_start(wkv[:, :, :], w_kv.rearrange("(k p) n -> p k n", p=P)).then_inc(weights_in, 16)
            act.dma_start(bnp[:, :, :], bn).then_inc(weights_in, 16)
            act.dma_start(rowsb[:, :], rows).then_inc(weights_in, 16)
            act.dma_start(wqt[:, :, :], w_q_t.rearrange("(k p) n -> p k n", p=P)).then_inc(weights_in, 16)
            act.dma_start(wout[:, :, :], w_out.rearrange("(k p) n -> p k n", p=P)).then_inc(weights_in, 16)
            act.dma_start(wr[:, :, :], w_r.rearrange("(k p) n -> p k n", p=P)).then_inc(weights_in, 16)
            act.dma_start(bob[:, :], bo).then_inc(weights_in, 16)
            for dst, src in ((w1b, w1), (w2b, w2), (wob, wo)):
                act.dma_start(dst[:, :, :, :], src.rearrange("e (k p) n -> p e k n", p=P)).then_inc(experts_in, 16)
            act.wait_ge(was_done, 1)
            act.wait_ge(wgnn_in, 48)
            act.activation(wh[:, :, D:D + 2 * HEADS],
                           small_ps[:, 0:KC * 2 * HEADS].rearrange("p (k c) -> p k c", k=KC), ACT.Copy)\
                .then_inc(wh_ready, 1)

            def copy_xT(n, par):
                act.wait_ge(xT_done, n + 1)
                act.activation(xnT[par], tp_ps[:, 0:KC * P], ACT.Copy).then_inc(xT_copied, 1)

            def evacuate(n, par, first):
                act.wait_ge(k_done, n + 1)
                act.activation(ksb[par], k_ps[par][:, :], ACT.Copy)
                act.activation(sq[par][:, 0:INNER], k_ps[par][:, :], ACT.Square)
                act.wait_ge(v_done, n + 1)
                act.activation(sq[par][:, INNER:2 * INNER], v_ps[par][:, :], ACT.Square).then_inc(squared, 1)
                act.wait_ge(h_done, n + 1)
                if first is None:
                    act.wait_ge(h_stored[par], ((n - par) // 2) * 16 if isinstance(n, int) else (n - par) * 8)
                act.activation(hst[par][:, 0:HEADS * HG].rearrange("p (h c) -> p h c", h=HEADS)[:, :, 0:C],
                               mix_ps[:, 0:D].rearrange("p (h c) -> p h c", h=HEADS), ACT.Copy)
                act.activation(asad[:, bass.ds(n, 1), :].rearrange("p a c -> p (a c)"),
                               mix_ps[:, D:D + 2 * HEADS], ACT.Copy)
                act.activation(hst[par][:, HEADS * HG:ROW], mix_ps[:, D:D + HEADS], ACT.Copy)\
                    .then_inc(h_staged, 1)

            def x_std(n):
                act.wait_ge(x_var, n + 1)
                act.activation(rs1[:, :], ve1[:, :], ACT.Sqrt).then_inc(x_rooted, 1)

            def kv_std(n):
                act.wait_ge(kv_var, n + 1)
                act.activation(rs2[:, :], ve2[:, :], ACT.Sqrt).then_inc(kv_rooted, 1)

            act.wait_ge(bn_var, 1)
            act.activation(bns[:, :, :], bns[:, :, :], ACT.Sqrt).then_inc(bn_rooted, 1)
            act.wait_ge(const_made, 3)
            x_std(0)
            x_std(1)
            copy_xT(0, 0)
            evacuate(0, 0, True)
            kv_std(0)
            x_std(2)
            copy_xT(1, 1)
            evacuate(1, 1, True)
            kv_std(1)
            x_std(3)
            copy_xT(2, 0)
            with act.Fori(2, LAST - 2, 2) as n0:
                for par in range(2):
                    evacuate(n0 + par, par, None)
                    kv_std(n0 + par)
                    x_std(n0 + (par + 2))
                    copy_xT(n0 + (par + 1), 1 - par)
            evacuate(LAST - 2, 0, None)
            kv_std(LAST - 2)
            x_std(LAST)
            copy_xT(LAST - 1, 1)
            evacuate(LAST - 1, 1, None)
            kv_std(LAST - 1)
            copy_xT(LAST, 0)
            evacuate(LAST, 0, None)
            kv_std(LAST)

            act.wait_ge(self_scores, 1)
            act.activation(pself[:, :, :], small2[:, :, :], ACT.Exp).then_inc(self_probs, 1)
            act.wait_ge(z_done, 1)
            for j in range(2):
                act.activation(zsb[:, j * 512:(j + 1) * 512], k_ps[j][:, :], ACT.Copy).then_inc(z_copied, 1)
            act.wait_ge(m_done, 1)
            act.activation(msb[:, :, :], v_ps[0][:, :].rearrange("p (k n) -> p k n", k=KC), ACT.Copy,
                           scale=1.0 / n_nodes).then_inc(m_copied, 1)
            act.wait_ge(phase2_ready, 1)

            def load_tile(n, par):
                act.dma_start(xin[par], x[bass.ds(n * P, P), :]).then_inc(xin_in[par], 16)
                act.dma_start(hself[par], h_rows[bass.ds(n * P, P), :]).then_inc(xin_in[par], 16)

            def exp_step(s):
                act.wait_ge(scores_ready, s + 1)
                act.activation(prob, sc, ACT.Exp).then_inc(probs_ready, 1)

            def tile(n, q, bases, last=False):
                first = act.value_load(meta[0:1, bass.ds(n, 1)], min_val=0, max_val=MAX_STEPS)
                count = act.value_load(meta[0:1, bass.ds(n + 64, 1)], min_val=2, max_val=MAX_STEPS)
                if not (isinstance(n, int) and n == 0):
                    act.wait_ge(tile_done, n)
                if not last:
                    load_tile(n + 1, (q + 1) % 2)
                act.wait_ge(xnT2_done, n + 1)
                act.activation(xnTb, tp_ps[:, 0:KC * P], ACT.Copy).then_inc(xnT2_copied, 1)
                with act.Fori(0, count) as k:
                    exp_step(first + k)
                act.wait_ge(neg_ready, n + 1)
                act.activation(neg, neg, ACT.Exp).then_inc(neg_exped, 1)
                if bases is not None:
                    expert_relus(q, bases, 0, SUP * P)
                act.wait_ge(zT_done, n + 1)
                act.activation(zTb[:, :, q * P:(q + 1) * P], tp_ps[:, 0:KC * P].rearrange("p (k n) -> p k n", k=KC),
                               ACT.Copy).then_inc(zT_copied, 1)
                if bases is not None:
                    expert_relus(q, bases, 1, SUP * P)
                act.wait_ge(logits_ready, n + 1)
                act.activation(small[:, 16:24], small[:, 8:16], ACT.Exp, accum_out=small[:, 24:25]).then_inc(wexp_done, 1)
                act.wait_ge(wT_done, n + 1)
                act.activation(wT[0:EXPERTS, :], wT_ps, ACT.Copy).then_inc(wT_copied, 1)

            def expert_relus(q, bases, layer, width):
                fbase, _, _ = bases
                for i in range(4):
                    act.wait_ge(ff_done, fbase + (4 * layer + i + 1))
                    col = 2 * (2 * q + i // 2) + i % 2
                    act.activation((h1, h2)[layer][i // 2][:, i % 2, 0:width], ff_ps[i][:, 0:width], ACT.Relu,
                                   bias=bnt[:, layer, col:col + 1], scale=bns[:, layer, col:col + 1])\
                        .then_inc(relu_done, 1)

            load_tile(0, 0)
            for q in range(SUP):
                tile(q, q, None)
            with act.Fori(1, NSUP) as g:
                for q in range(SUP):
                    tile(g * SUP + q, q, part_bases(g, q))
                act.wait_ge(acc_done, g * (4 * SUP))
                act.dma_start(out[bass.ds((g - 1) * (SUP * P), SUP * P), :].rearrange("(t p) c -> p t c", p=P),
                              acc).then_inc(out_stored, 16)
            tile(LAST, 0, None, last=True)
            for q in range(SUP):
                for layer in range(2):
                    expert_relus(q, part_bases(NSUP, q), layer, SUP * P)
            act.wait_ge(acc_done, NSUP * 4 * SUP)
            act.dma_start(out[(NSUP - 1) * SUP * P:NSUP * SUP * P, :].rearrange("(t p) c -> p t c", p=P),
                          acc).then_inc(out_stored, 16)
            for q in range(SUP):
                for layer in range(2):
                    expert_relus(q, last_bases(q), layer, P)
            act.wait_ge(acc_done, NSUP * 4 * SUP + 2 * SUP)
            act.dma_start(out[LAST * P:NT * P, :], acc[:, 0, :]).then_inc(out_stored, 16)
            act.wait_ge(out_stored, 16 * (NSUP + 1))

        @block.vector
        def _(dve):
            dve.wait_ge(const_made, 3)
            prep = Chain(dve, setup_chain, 0, 9)
            dve.memset(base_f[:, 0:1], 0.0)
            dve.tensor_copy(node_pf[:, :], node_i[:, :])
            prep.link(dve.tensor_copy(iota_f[:, :], iota_i[:, :]))
            prep.link(dve.tensor_scalar(base_f[:, 1:NT + 1], iota_f[:, 0:NT], 1.0, float(P), ALU.add, ALU.mult))
            dve.wait_ge(weights_in, 112)
            for k in range(KC):
                prep.link(dve.tensor_reduce(mean16[:, k, :], wkv[:, k, :].rearrange("p (h c) -> p h c", c=MD), axis=AX_X,
                                            op=ALU.add))
            prep.link(dve.tensor_scalar(mean16[:, :, :], mean16[:, :, :], 1.0 / MD, None, ALU.mult))
            for k in range(KC):
                dve.tensor_tensor(wkv[:, k, :].rearrange("p (h c) -> p h c", c=MD),
                                  wkv[:, k, :].rearrange("p (h c) -> p h c", c=MD),
                                  mean16[:, k, :].unsqueeze(2).broadcast_to([P, 16, MD]), ALU.subtract)
            par10 = bnp[:, :, :].rearrange("p (l f) c -> p l f c", l=2)
            dve.tensor_scalar(bns[:, :, :], par10[:, :, 4, :], BN_EPS, None, ALU.add).then_inc(bn_var, 1)
            dve.wait_ge(bn_rooted, 1)
            prep.link(dve.reciprocal(bns[:, :, :], bns[:, :, :]))
            prep.link(dve.tensor_tensor(bns[:, :, :], bns[:, :, :], par10[:, :, 1, :], ALU.mult))
            prep.link(dve.tensor_tensor(bnt[:, :, :], par10[:, :, 0, :], par10[:, :, 3, :], ALU.subtract))
            prep.link(dve.tensor_tensor(bnt[:, :, :], bnt[:, :, :], bns[:, :, :], ALU.mult))
            dve.tensor_tensor(bnt[:, :, :], bnt[:, :, :], par10[:, :, 2, :], ALU.add)
            dve.tensor_scalar(rowsb[:, D:2 * D], rowsb[:, D:2 * D], -1.0, None, ALU.add).then_inc(weights_ready, 1)
            dve.wait_ge(weights_ready, 1)
            prep.end()
            dve.wait_ge(dst_in, 16)

            def norm(n, par, first=None):
                c = Chain(dve, ln_chain, n * 4, 4)
                dve.wait_ge(x_in[par], (n - par) * 8 + 16)
                c.link(dve.bn_stats(stats[:, :], xt[par]))
                c.link(dve.tensor_scalar(below, dst_all, base_f[:, bass.ds(n + 1, 1)], 0.0, ALU.is_lt, ALU.add,
                                         accum_out=cnt[:, bass.ds(n, 1)]))
                dve.memset(small[:, 63:64], 0.0)
                c.link(dve.bn_aggr(mv[:, :], stats[:, :]))
                dve.tensor_scalar(ve1[:, :], mv[:, 1:2], EPS, None, ALU.add).then_inc(x_var, 1)
                dve.tensor_copy(mean_n[:, bass.ds(n, 1)], mv[:, 0:1])
                if first is None:
                    dve.wait_ge(xT_done, n - 1)
                dve.wait_ge(x_rooted, n + 1)
                c.link(dve.reciprocal(rstd_n[:, bass.ds(n, 1)], rs1[:, 0:1]))
                dve.tensor_scalar(xn[par], xt[par], mv[:, 0:1], rstd_n[:, bass.ds(n, 1)], ALU.subtract, ALU.mult)\
                    .then_inc(normed, 1)
                c.end()

            def scale_v(n, par):
                c = Chain(dve, kv_chain, n * 3, 3)
                dve.wait_ge(squared, n + 1)
                c.link(dve.tensor_reduce(small[:, 0:16], sq[par].rearrange("p (h c) -> p h c", c=MD), axis=AX_X, op=ALU.add))
                c.link(dve.tensor_scalar(small[:, 16:32], small[:, 0:16], 1.0 / MD, EPS, ALU.mult, ALU.add))
                dve.tensor_tensor(ve2[:, :], small[:, 16:24], small[:, 24:32], ALU.mult).then_inc(kv_var, 1)
                dve.wait_ge(kv_rooted, n + 1)
                c.link(dve.reciprocal(rs3[:, :], rs2[:, :]))
                c.end()
                dve.tensor_tensor(vsb[par].rearrange("p (h c) -> p h c", c=MD),
                                  v_ps[par][:, :].rearrange("p (h c) -> p h c", c=MD),
                                  rs3[:, :].unsqueeze(2).broadcast_to([P, MH, MD]), ALU.mult).then_inc(v_scaled, 1)

            norm(0, 0, True)
            norm(1, 1, True)
            scale_v(0, 0)
            with dve.Fori(2, LAST, 2) as n0:
                norm(n0, 0)
                scale_v(n0 - 1, 1)
                norm(n0 + 1, 1)
                scale_v(n0, 0)
            norm(LAST, 0)
            scale_v(LAST - 1, 1)
            scale_v(LAST, 0)

            mid = Chain(dve, mid_chain, 0, 30)
            link = mid.link
            link(dve.memset(dtb, 0.0))
            dve.wait_ge(dt_done, NT + 1)
            dt_v = acc_ps[:, :].rearrange("p (j c) -> p j c", j=4)
            dt_b = dtb.rearrange("p (j c) -> p j c", j=4)
            dve.tensor_copy(dt_b[0:MD, :, 0:MD], dt_v[0:MD, :, 0:MD])
            dve.tensor_copy(dt_b[MD:P, :, MD:P], dt_v[MD:P, :, MD:P]).then_inc(dt_copied, 1)
            dve.wait_ge(h_staged, NT)
            dve.tensor_reduce(gmax[:, 0, :], asad[:, :, 0:HEADS].rearrange("p n h -> p h n"), axis=AX_X, op=ALU.max)\
                .then_inc(gmax_local, 1)
            dve.wait_ge(counts_summed, 1)
            rp, k_f, k_sum, t0, tmp = (sched[:, i, :] for i in range(5))
            link(dve.memset(sched[:, :, :], 0.0))
            link(dve.tensor_copy(rp[:, 1:NT + 1], small_ps[0:1, 0:NT]))
            link(dve.tensor_tensor(tmp[:, 0:NT], rp[:, 1:NT + 1], rp[:, 0:NT], ALU.subtract))
            link(dve.tensor_scalar(sched_i[:, 0, 0:NT], tmp[:, 0:NT], float(STEP - 1), None, ALU.add))
            link(dve.tensor_scalar(sched_i[:, 1, 0:NT], sched_i[:, 0, 0:NT], STEP.bit_length() - 1, None, ALU.arith_shift_right))
            link(dve.tensor_scalar(k_f[:, 0:NT], sched_i[:, 1, 0:NT], 2.0, None, ALU.max))
            zero_row = sched[:, 7, 0:NT]
            link(dve.tensor_tensor_scan(k_sum[:, 0:NT], k_f[:, 0:NT], zero_row, 0.0, ALU.add, ALU.add))
            link(dve.tensor_tensor(t0[:, 0:NT], k_sum[:, 0:NT], k_f[:, 0:NT], ALU.subtract))
            link(dve.tensor_scalar(sched_i[:, 2, 0:1], k_sum[:, NT - 1:NT], float(RING - 1), None, ALU.add))
            link(dve.tensor_scalar(sched_i[:, 3, 0:1], sched_i[:, 2, 0:1], RING.bit_length() - 1, None, ALU.arith_shift_right))
            link(dve.tensor_copy(meta[:, 128:129], sched_i[:, 3, 0:1]))
            link(dve.tensor_scalar(tmp[:, 0:1], sched_i[:, 3, 0:1], float(RING), None, ALU.mult))
            link(dve.tensor_tensor(k_f[:, NT - 1:NT], tmp[:, 0:1], t0[:, NT - 1:NT], ALU.subtract))
            link(dve.tensor_copy(meta[:, 0:NT], t0[:, 0:NT]))
            link(dve.tensor_copy(meta[:, 64:64 + NT], k_f[:, 0:NT]))
            base_n, dif = sched[:, 5, :], sched[:, 6, :]
            link(dve.scalar_tensor_tensor(base_n[:, 1:NT + 1], t0[:, 0:NT], -float(STEP), rp[:, 0:NT], ALU.mult, ALU.add))
            dve.tensor_tensor(dif[:, 0:NT], base_n[:, 1:NT + 1], base_n[:, 0:NT], ALU.subtract).then_inc(sched_rows, 1)
            dve.wait_ge(sched_cols, 1)
            link(dve.tensor_copy(cols[0:NT, :], small_ps[0:NT, 64:66]))
            dve.tensor_scalar(steps_f[0:NT, :], iota_f[0:NT, :], cols[0:NT, 0:1], cols[0:NT, 1:2], ALU.is_ge, ALU.mult)\
                .then_inc(steps_masked, 1)
            dve.wait_ge(steps_summed, 1)
            link(dve.scalar_tensor_tensor(steps_i[:, :], iota_f[0:1, :], float(STEP), mix_ps[0:1, :], ALU.mult, ALU.add))
            dve.wait_ge(gmax_all, 1)
            link(dve.tensor_copy(adc[:, :, 0:HEADS], asad[:, :, HEADS:2 * HEADS]))
            link(dve.tensor_tensor(small2[:, :, :], asad[:, :, HEADS:2 * HEADS],
                                   gmax[:, 1, :].unsqueeze(1).broadcast_to([P, NT, HEADS]), ALU.add))
            link(dve.scalar_tensor_tensor(adc[:, :, HEADS:2 * HEADS], small2[:, :, :], 0.2, small2[:, :, :], ALU.mult, ALU.max))
            link(dve.tensor_tensor(small2[:, :, :], asad[:, :, 0:HEADS], asad[:, :, HEADS:2 * HEADS], ALU.add))
            link(dve.scalar_tensor_tensor(pself[:, :, :], small2[:, :, :], 0.2, small2[:, :, :], ALU.mult, ALU.max))
            link(dve.tensor_tensor(small2[:, :, :], pself[:, :, :], adc[:, :, HEADS:2 * HEADS], ALU.subtract))
            dve.tensor_scalar(small2[:, :, :], small2[:, :, :], 0.0, None, ALU.min).then_inc(self_scores, 1)
            link(dve.tensor_scalar(keep_a[:, :], rstd_n[:, :], 1.0, None, ALU.add))
            link(dve.scalar_tensor_tensor(keep_b[:, :], mean_n[:, :], -1.0, rstd_n[:, :], ALU.mult, ALU.mult))
            dve.wait_ge(self_probs, 1)
            dve.wait_ge(m_copied, 1)
            dve.wait_ge(h_stored[0], 16 * ((NT + 1) // 2))
            dve.wait_ge(h_stored[1], 16 * (NT // 2))
            link(dve.tensor_copy(small[:, 0:1], keep_a[:, 0:1]))
            link(dve.tensor_copy(small[:, 1:2], keep_b[:, 0:1]))
            mid.per = mid.n
            dve.tensor_copy(small[:, 2:3], keep_b[:, 0:1]).then_inc(phase2_ready, 1)

            def slot(s):
                return bass.ds(s % RING, 1)

            def onehot_t(n, s):
                dve.wait_ge(rows_ready, s + 1)
                src = dstrow[:, slot(s), :].rearrange("p a (e j) -> p (a j) e", j=TPS)
                dve.tensor_scalar(oht, src, node_pf[:, bass.ds(n, 1)], None, ALU.is_equal).then_inc(oht_ready, 1)

            def scores(s):
                c = Chain(dve, score_chain, s * 3, 3)
                dve.wait_ge(adg_ready, s + 1)
                a_src = ring[:, slot(s), :, HEADS * HG:ROW].rearrange("p a j c -> p (a j) c")
                c.link(dve.tensor_tensor(sc2, adg_ps[:, :, 0:HEADS], a_src, ALU.add))
                c.link(dve.scalar_tensor_tensor(sc, sc2, 0.2, sc2, ALU.mult, ALU.max))
                c.link(dve.tensor_tensor(sc2, sc, adg_ps[:, :, HEADS:2 * HEADS], ALU.subtract))
                dve.tensor_scalar(sc, sc2, 0.0, None, ALU.min).then_inc(scores_ready, 1)
                c.end()

            def messages(s, half):
                js = slice(2 * half, 2 * half + 2)
                dve.wait_ge(half_summed[half], s + 1)
                d = idx[:, slot(s), js, 1].rearrange("p a j -> p (a j)")
                dve.tensor_tensor(oh[half], window.unsqueeze(1).broadcast_to([P, 2, P]),
                                  d.unsqueeze(2).broadcast_to([P, 2, P]), ALU.is_equal)
                if half == 0:
                    dve.wait_ge(probs_ready, s + 1)
                rows_ = ring[:, slot(s), js, 0:HEADS * HG].rearrange("p a j (h c) -> p (a j) h c", h=HEADS)
                dve.tensor_tensor(msg[half], rows_, prob[:, js, :].unsqueeze(3).broadcast_to([P, 2, HEADS, HG]), ALU.mult)\
                    .then_inc(msg_ready[half], 1)

            def rsqrt(c, out_, var):
                v, y, t = rsq[:, 0:1], rsq[:, 1:2], rsq[:, 2:3]
                c.link(dve.tensor_scalar(v, var, EPS, None, ALU.add))
                c.link(dve.tensor_scalar(y.bitcast(I32), v.bitcast(I32), -0.5, float(0x5f3759df), ALU.mult, ALU.add))
                for i in range(3):
                    c.link(dve.scalar_tensor_tensor(t, y, v, y, ALU.mult, ALU.mult))
                    c.link(dve.tensor_scalar(t, t, -0.5, 1.5, ALU.mult, ALU.add))
                    c.link(dve.tensor_tensor(out_ if i == 2 else y, y, t, ALU.mult))

            def tile(n, q, bases, handoff=None):
                par = q % 2
                c = Chain(dve, tile_chain, n * 24, 24)
                first = dve.value_load(meta[0:1, bass.ds(n, 1)], min_val=0, max_val=MAX_STEPS)
                count = dve.value_load(meta[0:1, bass.ds(n + 64, 1)], min_val=2, max_val=MAX_STEPS)
                col = bass.ds(n, 1)
                dve.wait_ge(xin_in[par], (n - par) * 16 + 32)
                dve.tensor_scalar(xnb, xin[par], mean_n[:, col], rstd_n[:, col], ALU.subtract, ALU.mult).then_inc(xn_ready, 1)
                c.link(dve.tensor_scalar(kept, xin[par], keep_a[:, col], keep_b[:, col], ALU.mult, ALU.add))
                dve.tensor_tensor(kept, kept, rowsb[:, D:2 * D], ALU.add)
                dve.tensor_tensor(mself.rearrange("p (h c) -> p h c", h=HEADS),
                                  hself[par][:, 0:HEADS * HG].rearrange("p (h c) -> p h c", h=HEADS),
                                  pself[:, col, :].rearrange("p a h -> p (a h)").unsqueeze(2).broadcast_to([P, HEADS, HG]),
                                  ALU.mult).then_inc(self_ready, 1)
                c.link(dve.tensor_scalar(window, iota_f[:, 0:P], base_f[:, col], None, ALU.add))
                onehot_t(n, first)
                scores(first)
                with dve.Fori(0, count - 1) as k:
                    messages(first + k, 0)
                    onehot_t(n, first + k + 1)
                    messages(first + k, 1)
                    scores(first + k + 1)
                messages(first + count - 1, 0)
                messages(first + count - 1, 1)

                dve.wait_ge(tile_summed, n + 1)
                sums = acc_ps[:, 0:HEADS * HG].rearrange("p (h c) -> p h c", h=HEADS)
                c.link(dve.tensor_scalar(small[:, 0:4], sums[:, :, C], 1e-16, None, ALU.add))
                c.link(dve.reciprocal(small[:, 4:8], small[:, 0:4]))
                c.link(dve.tensor_tensor(gat.rearrange("p (h c) -> p h c", h=HEADS), sums[:, :, 0:C],
                                         small[:, 4:8].unsqueeze(2).broadcast_to([P, HEADS, C]), ALU.mult))
                c.link(dve.tensor_tensor(gat, gat, rowsb[:, 0:D], ALU.add))
                dve.tensor_scalar(neg, gat, 0.0, None, ALU.min).then_inc(neg_ready, 1)
                dve.wait_ge(mix_done, n + 1)
                c.link(dve.tensor_tensor(kept, kept, mix_ps[:, 0:D], ALU.add))
                dve.wait_ge(neg_exped, n + 1)
                c.link(dve.scalar_tensor_tensor(gat, gat, 0.0, neg, ALU.max, ALU.add))
                x1 = x1b[:, q, :]
                c.link(dve.tensor_tensor(x1, gat, kept, ALU.add))
                c.link(dve.bn_stats(stats[:, :], x1))
                dve.memset(small[:, 63:64], 0.0)
                c.link(dve.bn_aggr(mv[:, :], stats[:, :]))
                rsqrt(c, small[:, 40:41], mv[:, 1:2])
                dve.tensor_scalar(zb, x1, mv[:, 0:1], small[:, 40:41], ALU.subtract, ALU.mult).then_inc(z_ready, 1)

                dve.wait_ge(router_done, n + 1)
                c.link(dve.tensor_tensor(small[:, 8:16], rt_ps, rowsb[:, 2 * D:2 * D + EXPERTS], ALU.add))
                c.link(dve.tensor_reduce(small[:, 41:42], small[:, 8:16], axis=AX_X, op=ALU.max))
                dve.tensor_scalar(small[:, 8:16], small[:, 8:16], small[:, 41:42], None, ALU.subtract).then_inc(logits_ready, 1)
                dve.wait_ge(wexp_done, n + 1)
                c.end()
                dve.reciprocal(small[:, 42:43], small[:, 24:25]).then_inc(w_recip, 1)
                dve.wait_ge(w_recip, n + 1)
                dve.tensor_scalar(wgt[:, q, :], small[:, 16:24], small[:, 42:43], None, ALU.mult).then_inc(w_ready, 1)
                if bases is not None:
                    expert_sums(q, bases, SUP, handoff)
                dve.wait_ge(bo_done, n + 1)
                dve.tensor_tensor(x1, x1, mix_ps[:, D:2 * D], ALU.add).then_inc(tile_done, 1)

            def expert_sums(q, bases, tiles, handoff):
                fbase, _, abase = bases
                pairs = max(1, tiles // 2)
                for i in range(2 * pairs):
                    e = 2 * q + i // pairs
                    t0_ = 2 * (i % pairs)
                    dve.wait_ge(ff_done, fbase + (9 + i))
                    if q == 0 and i < pairs:
                        dve.wait_ge(handed, handoff)
                    else:
                        dve.wait_ge(acc_done, abase + (i - pairs + 1))
                    for t in range(t0_, min(t0_ + 2, tiles)):
                        ins = dve.scalar_tensor_tensor(acc[:, t, :], ff_ps[i][:, (t - t0_) * D:(t - t0_ + 1) * D],
                                                       wgf[:, t, e:e + 1], acc[:, t, :], ALU.mult, ALU.add)
                    ins.then_inc(acc_done, 1)

            def hand_over(n_done, stored, tiles):
                dve.wait_ge(tile_done, n_done)
                if stored is not None:
                    dve.wait_ge(out_stored, stored)
                dve.tensor_copy(acc[:, 0:tiles, :], x1b[:, 0:tiles, :])
                dve.tensor_copy(wgf[:, 0:tiles, :], wgt[:, 0:tiles, :])
                dve.tensor_copy(zTf[:, :, 0:tiles * P], zTb[:, :, 0:tiles * P]).then_inc(handed, 1)

            for q in range(SUP):
                tile(q, q, None)
            hand_over(SUP, None, SUP)
            with dve.Fori(1, NSUP) as g:
                for q in range(SUP):
                    tile(g * SUP + q, q, part_bases(g, q), g)
                hand_over(g * SUP + SUP, g * 16, SUP)
            tile(LAST, 0, None)
            for q in range(SUP):
                expert_sums(q, part_bases(NSUP, q), SUP, NSUP)
            hand_over(LAST + 1, NSUP * 16, 1)
            for q in range(SUP):
                expert_sums(q, last_bases(q), 1, NSUP + 1)

        @block.tensor
        def _(pe):
            def product(out_, pairs, sem_=None, start=True, stop=True):
                for i, (lhsT, rhs) in enumerate(pairs):
                    ins = pe.matmul(out_, lhsT, rhs, start=start and i == 0, stop=stop and i == len(pairs) - 1)
                if sem_ is not None:
                    ins.then_inc(sem_, 1)

            pe.wait_ge(const_made, 3)
            pe.wait_ge(wgnn_in, 48)
            for k in range(KC):
                product(small_ps[:, k * 2 * HEADS:(k + 1) * 2 * HEADS],
                        [(wg[:, o, k * P:(k + 1) * P], attb[:, o, :]) for o in range(KC)],
                        was_done if k == KC - 1 else None)
            product(acc_ps[:, :], [(zeros[:, 0:P], zeros[:, :])], stop=False)

            def transpose_x(n, par):
                pe.wait_ge(normed, n + 1)
                for k in range(KC):
                    ins = pe.transpose(tp_ps[:, k * P:(k + 1) * P], xn[par][:, k * P:(k + 1) * P], ident[:, :])
                ins.then_inc(xT_done, 1)

            def sum_dt(n, par):
                pe.wait_ge(v_scaled, n + 1)
                for j in range(4):
                    ins = pe.matmul(acc_ps[:, j * P:(j + 1) * P], vsb[par][:, j * P:(j + 1) * P],
                                    ksb[par][:, j * P:(j + 1) * P], start=False, stop=False)
                ins.then_inc(dt_done, 1)

            def project(n, par):
                pe.wait_ge(xT_copied, n + 1)
                xT = [xnT[par][:, k * P:(k + 1) * P] for k in range(KC)]
                product(k_ps[par][:, :], [(xT[k], wkv[:, k, 0:INNER]) for k in range(KC)], k_done)
                product(v_ps[par][:, :], [(xT[k], wkv[:, k, INNER:2 * INNER]) for k in range(KC)], v_done)
                if not (isinstance(n, int) and n == 0):
                    pe.wait_ge(h_staged, n)
                product(mix_ps[:, 0:D + 2 * HEADS], [(xT[k], wh[:, k, :]) for k in range(KC)], h_done)

            pe.wait_ge(weights_ready, 1)
            pe.wait_ge(wh_ready, 1)
            for n in range(2):
                transpose_x(n, n)
                project(n, n)
            with pe.Fori(2, LAST, 2) as n0:
                for par in range(2):
                    transpose_x(n0 + par, par)
                    sum_dt(n0 + (par - 2), par)
                    project(n0 + par, par)
            transpose_x(LAST, 0)
            sum_dt(LAST - 2, 0)
            project(LAST, 0)
            sum_dt(LAST - 1, 1)
            sum_dt(LAST, 0)
            product(acc_ps[:, :], [(zeros[:, 0:P], zeros[:, :])], dt_done, start=False)

            product(small_ps[0:1, 0:NT], [(ones[:, 0:1], cnt[:, 0:NT])], counts_summed)
            pe.wait_ge(dt_copied, 1)
            for j in range(4):
                product(k_ps[j // 2][:, (j % 2) * D:(j % 2 + 1) * D], [(dtb[:, j * P:(j + 1) * P], wout[:, j, :])],
                        z_done if j == 3 else None)
            pe.wait_ge(sched_rows, 1)
            product(small_ps[0:NT, 64:65], [(sched[0:1, 3, 0:NT], ones[0:1, 0:1])])
            product(small_ps[0:NT, 65:66], [(sched[0:1, 6, 0:NT], ones[0:1, 0:1])], sched_cols)
            pe.wait_ge(steps_masked, 1)
            product(mix_ps[0:1, :], [(ones[0:NT, 0:1], steps_f[0:NT, :])], steps_summed)
            pe.wait_ge(z_copied, 2)
            for f in range(KC):
                product(v_ps[0][:, f * D:(f + 1) * D],
                        [(wqt[:, j, f * P:(f + 1) * P], zsb[:, j * D:(j + 1) * D]) for j in range(4)],
                        m_done if f == KC - 1 else None)

            pe.wait_ge(phase2_ready, 1)
            for half in range(2):
                pe.sem_inc(half_summed[half], 1)

            def target_scores(n, s):
                pe.wait_ge(oht_ready, s + 1)
                for j in range(TPS):
                    ins = pe.matmul(adg_ps[:, j, :], oht[:, j, :],
                                    adc[:, bass.ds(n, 1), :].rearrange("p a c -> p (a c)"), start=True, stop=True)
                ins.then_inc(adg_ready, 1)

            def sum_half(s, half):
                pe.wait_ge(msg_ready[half], s + 1)
                for j in range(2):
                    ins = pe.matmul(acc_ps[:, 0:HEADS * HG], oh[half][:, j, :],
                                    msg[half][:, j, :, :].rearrange("p h c -> p (h c)"), start=False, stop=False)
                ins.then_inc(half_summed[half], 1)

            def layer1(q, bases, width, handoff):
                _, _, abase = bases
                for i in range(4):
                    if q == 0:
                        if i == 0:
                            pe.wait_ge(handed, handoff)
                    else:
                        pe.wait_ge(acc_done, abase + ((i - 3) if width > P else min(0, i - 1)))
                    e, m = 2 * q + i // 2, i % 2
                    product(ff_ps[i][:, 0:width],
                            [(w1b[:, e, k, m * P:(m + 1) * P], zTf[:, k, 0:width]) for k in range(KC)], ff_done)

            def layer2(q, bases, width):
                _, rbase, _ = bases
                for i in range(4):
                    if i % 2 == 0:
                        pe.wait_ge(relu_done, rbase + (i + 2))
                    e, m = 2 * q + i // 2, i % 2
                    product(ff_ps[i][:, 0:width],
                            [(w2b[:, e, k, m * P:(m + 1) * P], h1[i // 2][:, k, 0:width]) for k in range(KC)], ff_done)

            def layer3(q, bases, tiles, which):
                _, rbase, _ = bases
                pairs = max(1, tiles // 2)
                pe.wait_ge(relu_done, rbase + (6 + 2 * which))
                for i in range(which * pairs, (which + 1) * pairs):
                    e = 2 * q + which
                    t0_ = 2 * (i % pairs)
                    for t in range(t0_, min(t0_ + 2, tiles)):
                        end = t == min(t0_ + 2, tiles) - 1
                        product(ff_ps[i][:, (t - t0_) * D:(t - t0_ + 1) * D],
                                [(h2[which][:, k, t * P:(t + 1) * P], wob[:, e, k, :]) for k in range(KC)],
                                ff_done if end else None)

            def tile(n, q, bases, handoff=None):
                first = pe.value_load(meta[0:1, bass.ds(n, 1)], min_val=0, max_val=MAX_STEPS)
                count = pe.value_load(meta[0:1, bass.ds(n + 64, 1)], min_val=2, max_val=MAX_STEPS)
                product(acc_ps[:, 0:HEADS * HG], [(zeros[:, 0:P], zeros[:, 0:HEADS * HG])], stop=False)
                pe.wait_ge(xn_ready, n + 1)
                for k in range(KC):
                    ins = pe.transpose(tp_ps[:, k * P:(k + 1) * P], xnb[:, k * P:(k + 1) * P], ident[:, :])
                ins.then_inc(xnT2_done, 1)
                target_scores(n, first)
                pe.wait_ge(xnT2_copied, n + 1)
                product(mix_ps[:, 0:D], [(xnTb[:, k * P:(k + 1) * P], msb[:, k, :]) for k in range(KC)], mix_done)
                with pe.Fori(0, count - 1) as k:
                    sum_half(first + k, 0)
                    target_scores(n, first + k + 1)
                    sum_half(first + k, 1)
                sum_half(first + count - 1, 0)
                sum_half(first + count - 1, 1)
                pe.wait_ge(self_ready, n + 1)
                product(acc_ps[:, 0:HEADS * HG], [(ident[:, :], mself)], tile_summed, start=False)
                if bases is not None:
                    layer1(q, bases, SUP * P, handoff)
                pe.wait_ge(z_ready, n + 1)
                for k in range(KC):
                    ins = pe.transpose(tp_ps[:, k * P:(k + 1) * P], zb[:, k * P:(k + 1) * P], ident[:, :])
                ins.then_inc(zT_done, 1)
                if bases is not None:
                    layer2(q, bases, SUP * P)
                pe.wait_ge(zT_copied, n + 1)
                product(rt_ps, [(zTb[:, k, q * P:(q + 1) * P], wr[:, k, :]) for k in range(KC)], router_done)
                if bases is not None:
                    layer3(q, bases, SUP, 0)
                pe.wait_ge(w_ready, n + 1)
                pe.transpose(wT_ps, wgt[:, q, :], ident[:, :]).then_inc(wT_done, 1)
                if bases is not None:
                    layer3(q, bases, SUP, 1)
                pe.wait_ge(wT_copied, n + 1)
                product(mix_ps[:, D:2 * D], [(wT[0:EXPERTS, :], bob[:, :])], bo_done)

            for q in range(SUP):
                tile(q, q, None)
            pe.wait_ge(experts_in, 48)
            with pe.Fori(1, NSUP) as g:
                for q in range(SUP):
                    tile(g * SUP + q, q, part_bases(g, q), g)
            tile(LAST, 0, None)
            for q in range(SUP):
                layer1(q, part_bases(NSUP, q), SUP * P, NSUP)
                layer2(q, part_bases(NSUP, q), SUP * P)
                for which in range(2):
                    layer3(q, part_bases(NSUP, q), SUP, which)
            for q in range(SUP):
                layer1(q, last_bases(q), P, NSUP + 1)
                layer2(q, last_bases(q), P)
                for which in range(2):
                    layer3(q, last_bases(q), 1, which)


def kernel(x, src, dst, L0_gnn_W, L0_gnn_att_src, L0_gnn_att_dst, L0_gnn_bias, L0_mix_w_qkv, L0_mix_w_out, L0_mix_b_out,
           L0_ffn_Wr, L0_ffn_br, L0_ffn_W1, L0_ffn_b1, L0_ffn_g1, L0_ffn_be1, L0_ffn_m1, L0_ffn_v1, L0_ffn_W2, L0_ffn_b2,
           L0_ffn_g2, L0_ffn_be2, L0_ffn_m2, L0_ffn_v2, L0_ffn_Wo, L0_ffn_bo):
    import numpy as np
    import concourse.bacc as bacc
    from concourse.bass_utils import run_bass_kernel_spmd

    f = np.ascontiguousarray
    n, e = x.shape[0], src.shape[0]
    rows_pad = -(-n // P) * P - n
    edge_pad = -(-e // P) * P - e + STEP * (RING + 4)
    srcp = np.concatenate([np.asarray(src), np.zeros(edge_pad, np.int32)])
    dstp = np.concatenate([np.asarray(dst), np.full(edge_pad, 1 << 20, np.int32)])
    att = np.zeros((D, 2 * HEADS), np.float32)
    for h in range(HEADS):
        att[h * C:(h + 1) * C, h] = np.asarray(L0_gnn_att_src)[h]
        att[h * C:(h + 1) * C, HEADS + h] = np.asarray(L0_gnn_att_dst)[h]
    rows = np.tile(np.concatenate([np.asarray(L0_gnn_bias), np.asarray(L0_mix_b_out), np.asarray(L0_ffn_br)])[None], (P, 1))
    params = [L0_ffn_b1, L0_ffn_g1, L0_ffn_be1, L0_ffn_m1, L0_ffn_v1, L0_ffn_b2, L0_ffn_g2, L0_ffn_be2, L0_ffn_m2, L0_ffn_v2]
    bn = np.stack([np.asarray(a).reshape(2 * EXPERTS, P).T for a in params], axis=1)
    qkv = np.asarray(L0_mix_w_qkv)
    ins = {
        "in_x": f(np.pad(np.asarray(x), ((0, rows_pad), (0, 0)))),
        "in_sd": f(np.stack([srcp, dstp], axis=1)),
        "in_dst": f(dstp),
        "in_att": att,
        "in_w_gnn": f(L0_gnn_W),
        "in_w_gnn_t": f(np.asarray(L0_gnn_W).T),
        "in_rows": f(rows),
        "in_w_kv": f(qkv[:, INNER:]),
        "in_w_q_t": f(qkv[:, :INNER].T),
        "in_w_out": f(L0_mix_w_out),
        "in_w_r": f(L0_ffn_Wr),
        "in_bn": f(bn),
        "in_w1": f(L0_ffn_W1),
        "in_w2": f(L0_ffn_W2),
        "in_wo": f(L0_ffn_Wo),
        "in_bo": f(L0_ffn_bo),
    }
    nc = bacc.Bacc("TRN2", target_bir_lowering=False, num_devices=1)
    args = [nc.dram_tensor(k, a.shape, mybir.dt.from_np(a.dtype), kind="ExternalInput").ap() for k, a in ins.items()]
    out = nc.dram_tensor("out_x", (n + rows_pad, D), F32, kind="ExternalOutput").ap()
    gps_layer(nc, *args, out, n, e)
    r = run_bass_kernel_spmd(nc, [ins], core_ids=[0])
    return r.results[0]["out_x"][:n]
```

```python
from contextlib import ExitStack

import concourse.bass as bass
from concourse import mybir

F32 = mybir.dt.float32
BF16 = mybir.dt.bfloat16
I32 = mybir.dt.int32
ALU = mybir.AluOpType
ACT = mybir.ActivationFunctionType
AX_X = mybir.AxisListType.X

P = 128
D = 256
KC = D // P
HEADS = 4
C = D // HEADS
HG = C + 1
ROW = HEADS * HG + HEADS
MH = 8
MD = 64
INNER = MH * MD
EXPERTS = 8
SUP = 4
TPS = 4
STEP = P * TPS
RING = 8
MAX_STEPS = 640
EPS = 1e-5
BN_EPS = 1e-3


class Chain:

    def __init__(self, eng, sem, base, per):
        self.eng, self.sem, self.base, self.per, self.n = eng, sem, base, per, 0

    def link(self, ins):
        self.n += 1
        ins.then_inc(self.sem, 1)
        self.eng.wait_ge(self.sem, self.base + self.n)

    def end(self):
        assert self.n == self.per, (self.n, self.per)


def gps_layer(nc, x, sd, dsts, att, w_gnn, w_gnn_t, rows, w_kv, w_q_t, w_out, w_r, bn, w1, w2, wo, bo, out, n_nodes, n_edges):
    NT = x.shape[0] // P
    NSUP = (NT - 1) // SUP
    LAST = NSUP * SUP
    assert NT == LAST + 1 and LAST % 2 == 0
    DCOLS = -(-n_edges // P)
    EMAX = sd.shape[0] - STEP
    h_rows = nc.dram_tensor("h_rows", [NT * P, ROW], F32).ap()

    ctx = ExitStack()
    with ctx:
        def sb(name, shape, dt=F32):
            return ctx.enter_context(nc.sbuf_tensor(name, shape, dt))

        def sem(name):
            return ctx.enter_context(nc.semaphore(name))

        bank = [ctx.enter_context(nc.psum_tensor(f"bank{i}", [P, 512], F32)) for i in range(8)]

        ident = sb("ident", [P, P])
        iota_i = sb("iota_i", [P, MAX_STEPS], I32)
        iota_f = sb("iota_f", [P, MAX_STEPS])
        node_i = sb("node_i", [P, NT], I32)
        node_pf = sb("node_pf", [P, NT])
        base_f = sb("base_f", [P, NT + 1])
        ones = sb("ones", [P, P])
        zeros = sb("zeros", [P, 512], BF16)
        wkv = sb("wkv", [P, KC, 2 * INNER])
        wh = sb("wh", [P, KC, D + 2 * HEADS])
        wg = sb("wg", [P, KC, D])
        attb = sb("attb", [P, KC, 2 * HEADS])
        wqt = sb("wqt", [P, INNER // P, D])
        wout = sb("wout", [P, INNER // P, D])
        wr = sb("wr", [P, KC, EXPERTS])
        rowsb = sb("rowsb", [P, 2 * D + EXPERTS])
        bnp = sb("bnp", [P, 10, 2 * EXPERTS])
        bns = sb("bns", [P, 2, 2 * EXPERTS])
        bnt = sb("bnt", [P, 2, 2 * EXPERTS])
        bob = sb("bob", [EXPERTS, D])
        w1b = sb("w1b", [P, EXPERTS, KC, D])
        w2b = sb("w2b", [P, EXPERTS, KC, D])
        wob = sb("wob", [P, EXPERTS, KC, D])
        mean16 = sb("mean16", [P, KC, 16])
        mean_n = sb("mean_n", [P, NT])
        rstd_n = sb("rstd_n", [P, NT])
        keep_a = sb("keep_a", [P, NT])
        keep_b = sb("keep_b", [P, NT])
        asad = sb("asad", [P, NT, 2 * HEADS])
        adc = sb("adc", [P, NT, 2 * HEADS])
        adc3 = sb("adc3", [P, NT, 3, 2 * HEADS], BF16)
        adc_r = sb("adc_r", [P, NT, 2 * HEADS])
        pself = sb("pself", [P, NT, HEADS])
        gmax = sb("gmax", [P, 2, HEADS])
        msb = sb("msb", [P, KC, D])
        cnt = sb("cnt", [P, NT])
        sched = sb("sched", [1, 8, 64])
        sched_i = sb("sched_i", [1, 4, 64], I32)
        meta = sb("meta", [1, 192], I32)
        steps_i = sb("steps_i", [1, MAX_STEPS], I32)
        steps_f = sb("steps_f", [64, MAX_STEPS])
        cols = sb("cols", [64, 2])
        stats = sb("stats", [P, 6])
        mv = sb("mv", [P, 2])
        small = sb("small", [P, 64])
        rsq = sb("rsq", [P, 8])
        ve1 = sb("ve1", [P, 1])
        rs1 = sb("rs1", [P, 1])
        ve2 = sb("ve2", [P, MH])
        rs2 = sb("rs2", [P, MH])
        rs3 = sb("rs3", [P, MH])
        small2 = sb("small2", [P, NT, HEADS])

        big = sb("big", [P, 26400])
        at = [0]

        def part(n, dt=F32):
            words = -(-n * (2 if dt == BF16 else 4) // 4)
            view = big[:, at[0]:at[0] + words]
            at[0] += words + (-words) % 8
            return view if dt == F32 else view.bitcast(dt)

        dst_all = part(DCOLS, I32)
        below = part(DCOLS, BF16)
        xt = [part(D) for _ in range(2)]
        xn = [part(D) for _ in range(2)]
        xnT = [part(KC * P) for _ in range(2)]
        ksb = [part(INNER) for _ in range(2)]
        vsb = [part(INNER) for _ in range(2)]
        sq = [part(2 * INNER) for _ in range(2)]
        hst = [part(ROW) for _ in range(2)]
        dtb = part(4 * P)
        zsb = part(4 * D)
        at1 = at[0]
        at[0] = 0
        ring = part(RING * TPS * ROW).rearrange("p (u j c) -> p u j c", u=RING, j=TPS)
        idx = part(RING * TPS * 2, I32).rearrange("p (u j c) -> p u j c", u=RING, j=TPS)
        dstrow = part(RING * STEP, I32).rearrange("p (u e) -> p u e", u=RING)
        window = part(P)
        oh = [part(2 * P).rearrange("p (j n) -> p j n", j=2) for _ in range(2)]
        msg = [part(2 * HEADS * HG).rearrange("p (j h c) -> p j h c", j=2, h=HEADS) for _ in range(2)]
        oht = part(TPS * P, BF16).rearrange("p (j e) -> p j e", j=TPS)
        prob = part(2 * TPS * HEADS).rearrange("p (b j h) -> p b j h", b=2, j=TPS)
        outb = part(SUP * D).rearrange("p (t c) -> p t c", t=SUP)
        sc = part(TPS * HEADS).rearrange("p (j h) -> p j h", j=TPS)
        sc2 = part(TPS * HEADS).rearrange("p (j h) -> p j h", j=TPS)
        xin = [part(D) for _ in range(2)]
        hself = [part(ROW) for _ in range(2)]
        mself = part(HEADS * HG)
        xnb = part(D)
        xnTb = part(KC * P)
        kept = part(D)
        gat = part(D)
        neg = part(D)
        zb = part(D)
        zTb = part(KC * SUP * P).rearrange("p (k n) -> p k n", k=KC)
        zTf = part(KC * SUP * P).rearrange("p (k n) -> p k n", k=KC)
        x1b = part(SUP * D).rearrange("p (t c) -> p t c", t=SUP)
        acc = part(SUP * D).rearrange("p (t c) -> p t c", t=SUP)
        wgt = part(SUP * EXPERTS).rearrange("p (t e) -> p t e", t=SUP)
        wgf = part(SUP * EXPERTS).rearrange("p (t e) -> p t e", t=SUP)
        wT = part(P)
        h1 = [wkv[:, i, :].rearrange("p (k n) -> p k n", k=KC) for i in range(2)]
        h2 = [w.rearrange("p j n -> p (j n)").rearrange("p (k n) -> p k n", k=KC) for w in (wqt[:, :, :], wout[:, :, :])]
        at2 = at[0]
        assert max(at1, at2) <= 26400, (at1, at2)

        acc_ps, small_ps, tp_ps, mix_ps = bank[:4]
        ff_ps = bank[4:]
        k_ps, v_ps = bank[4:6], bank[6:8]
        adg_ps = small_ps[:, 0:TPS * 2 * HEADS].rearrange("p (j c) -> p j c", j=TPS)
        rt_ps = mix_ps[:, D:D + EXPERTS]
        wT_ps = tp_ps[0:EXPERTS, KC * P:KC * P + P]

        weights_in = sem("weights_in")
        wgnn_in = sem("wgnn_in")
        experts_in = sem("experts_in")
        dst_in = sem("dst_in")
        const_made = sem("const_made")
        setup_chain = sem("setup_chain")
        was_done = sem("was_done")
        wh_ready = sem("wh_ready")
        weights_ready = sem("weights_ready")
        phase2_ready = sem("phase2_ready")
        x_in = [sem(f"x_in{i}") for i in range(2)]
        normed = sem("normed")
        ln_chain = sem("ln_chain")
        xT_done = sem("xT_done")
        xT_copied = sem("xT_copied")
        k_done = sem("k_done")
        v_done = sem("v_done")
        h_done = sem("h_done")
        squared = sem("squared")
        h_staged = sem("h_staged")
        h_stored = [sem(f"h_stored{i}") for i in range(2)]
        kv_chain = sem("kv_chain")
        v_scaled = sem("v_scaled")
        bn_var = sem("bn_var")
        bn_rooted = sem("bn_rooted")
        x_var = sem("x_var")
        x_rooted = sem("x_rooted")
        kv_var = sem("kv_var")
        kv_rooted = sem("kv_rooted")
        w_recip = sem("w_recip")
        z_done = sem("z_done")
        dt_done = sem("dt_done")
        mid_chain = sem("mid_chain")
        dt_copied = sem("dt_copied")
        z_copied = sem("z_copied")
        m_done = sem("m_done")
        m_copied = sem("m_copied")
        counts_summed = sem("counts_summed")
        sched_rows = sem("sched_rows")
        sched_cols = sem("sched_cols")
        steps_masked = sem("steps_masked")
        steps_summed = sem("steps_summed")
        gmax_local = sem("gmax_local")
        gmax_all = sem("gmax_all")
        self_scores = sem("self_scores")
        self_probs = sem("self_probs")
        idx_in = [sem(f"idx_in{i}") for i in range(RING)]
        gathered = [sem(f"gathered{i}") for i in range(RING)]
        step_begun = sem("step_begun")
        rows_ready = sem("rows_ready")
        oht_ready = sem("oht_ready")
        adg_ready = sem("adg_ready")
        score_chain = sem("score_chain")
        scores_ready = sem("scores_ready")
        probs_ready = sem("probs_ready")
        msg_ready = [sem("msg_a_ready"), sem("msg_b_ready")]
        half_summed = [sem("half_a_summed"), sem("half_b_summed")]
        xin_in = [sem(f"xin_in{i}") for i in range(2)]
        xn_ready = sem("xn_ready")
        xnT2_done = sem("xnT2_done")
        xnT2_copied = sem("xnT2_copied")
        mix_done = sem("mix_done")
        tile_chain = sem("tile_chain")
        router_chain = sem("router_chain")
        self_ready = sem("self_ready")
        tile_summed = sem("tile_summed")
        neg_ready = sem("neg_ready")
        neg_exped = sem("neg_exped")
        z_ready = sem("z_ready")
        zT_done = sem("zT_done")
        zT_copied = sem("zT_copied")
        router_done = sem("router_done")
        logits_ready = sem("logits_ready")
        wexp_done = sem("wexp_done")
        w_ready = sem("w_ready")
        wT_done = sem("wT_done")
        wT_copied = sem("wT_copied")
        bo_done = sem("bo_done")
        tile_done = sem("tile_done")
        ff_done = sem("ff_done")
        relu_done = sem("relu_done")
        acc_done = sem("acc_done")
        handed = sem("handed")
        out_stored = sem("out_stored")

        def part_bases(g, q):
            return (g - 1) * (12 * SUP) + 12 * q, (g - 1) * (8 * SUP) + 8 * q, (g - 1) * (4 * SUP) + 4 * q

        def last_bases(q):
            return NSUP * 12 * SUP + 10 * q, NSUP * 8 * SUP + 8 * q, NSUP * 4 * SUP + 2 * q

        block = ctx.enter_context(nc.Block())

        @block.sync
        def _(sp):
            sp.dma_start(wg[:, :, :], w_gnn.rearrange("(k p) n -> p k n", p=P)).then_inc(wgnn_in, 16)
            sp.dma_start(attb[:, :, :], att.rearrange("(k p) n -> p k n", p=P)).then_inc(wgnn_in, 16)
            sp.dma_start(wh[:, :, 0:D], w_gnn_t.rearrange("(k p) n -> p k n", p=P)).then_inc(wgnn_in, 16)

            def load_x(n, par):
                sp.dma_start(xt[par], x[bass.ds(n * P, P), :]).then_inc(x_in[par], 16)

            def store_h(n, par):
                sp.wait_ge(h_staged, n + 1)
                sp.dma_start(h_rows[bass.ds(n * P, P), :], hst[par]).then_inc(h_stored[par], 16)

            load_x(0, 0)
            load_x(1, 1)
            sp.dma_start(dst_all, dsts[0:P * DCOLS].rearrange("(p c) -> p c", p=P)).then_inc(dst_in, 16)
            for n in range(2):
                sp.wait_ge(normed, n + 1)
                load_x(n + 2, n % 2)
                store_h(n, n % 2)
            with sp.Fori(2, LAST - 2, 2) as n0:
                for par in range(2):
                    sp.wait_ge(normed, n0 + (par + 1))
                    load_x(n0 + (par + 2), par)
                    store_h(n0 + par, par)
            sp.wait_ge(normed, LAST - 1)
            load_x(LAST, 0)
            for n in range(LAST - 2, NT):
                store_h(n, n % 2)

            sp.wait_ge(phase2_ready, 1)

            def edges(s, u, first):
                if not first:
                    sp.wait_ge(msg_ready[1], s - (RING - 1))
                e0 = sp.value_load(steps_i[0:1, bass.ds(s, 1)], min_val=0, max_val=EMAX)
                sp.dma_start(idx[:, u, :, :], sd[bass.ds(e0, STEP), :].rearrange("(p j) c -> p j c", p=P))\
                    .then_inc(idx_in[u], 16)
                sp.dma_start(dstrow[:, u, :], dsts[bass.ds(e0, STEP)].partition_broadcast(P))\
                    .then_inc(idx_in[u], 16)

            for u in range(RING):
                edges(u, u, True)
            rounds = sp.value_load(meta[0:1, 128:129], min_val=2, max_val=MAX_STEPS // RING)
            with sp.Fori(1, rounds) as r:
                for u in range(RING):
                    edges(r * RING + u, u, False)

        @block.gpsimd
        def _(pool):
            pool.memset(ident[:, :], 0.0).then_inc(const_made, 1)
            pool.memset(ones[:, :], 1.0)
            pool.memset(zeros[:, :], 0.0)
            pool.memset(hst[0].rearrange("p (c) -> p c"), 1.0)
            pool.memset(hst[1].rearrange("p (c) -> p c"), 1.0)
            pool.iota(iota_i[:, :], [[1, MAX_STEPS]], base=0, channel_multiplier=0)
            pool.iota(node_i[:, :], [[P, NT]], base=0, channel_multiplier=1).then_inc(const_made, 1)
            pool.wait_ge(const_made, 2)
            pool.affine_select(out=ident[:, :], in_=ident[:, :], compare_op=ALU.not_equal, fill=1.0, base=0,
                               pattern=[[-1, P]], channel_multiplier=1).then_inc(const_made, 1)
            pool.wait_ge(gmax_local, 1)
            pool.partition_all_reduce(gmax[:, 1, :], gmax[:, 0, :], P, bass.bass_isa.ReduceOp.max).then_inc(gmax_all, 1)

            pool.wait_ge(phase2_ready, 1)

            def gather(s, u, first, turn):
                if not first:
                    pool.wait_ge(msg_ready[1], s - (RING - 1))
                pool.wait_ge(idx_in[u], 32 * turn)
                pool.sem_inc(step_begun, 1)
                for j in range(TPS):
                    pool.indirect_dma_start(ring[:, u, j, :], None, h_rows[:, :],
                                            bass.IndirectOffsetOnAxis(ap=idx[:, u, j, 0:1], axis=0))\
                        .then_inc(gathered[u], 16)

            def landed(u, turn):
                pool.wait_ge(gathered[u], 16 * TPS * turn)
                pool.sem_inc(rows_ready, 1)

            for u in range(RING):
                gather(u, u, True, 1)
                if u:
                    landed(u - 1, 1)
            rounds = pool.value_load(meta[0:1, 128:129], min_val=2, max_val=MAX_STEPS // RING)
            with pool.Fori(1, rounds) as r:
                for u in range(RING):
                    gather(r * RING + u, u, False, r + 1)
                    landed((u - 1) % RING, r + 1 if u else r)
            landed(RING - 1, rounds)

        @block.scalar
        def _(act):
            act.dma_start(wkv[:, :, :], w_kv.rearrange("(k p) n -> p k n", p=P)).then_inc(weights_in, 16)
            act.dma_start(bnp[:, :, :], bn).then_inc(weights_in, 16)
            act.dma_start(rowsb[:, :], rows).then_inc(weights_in, 16)
            act.dma_start(wqt[:, :, :], w_q_t.rearrange("(k p) n -> p k n", p=P)).then_inc(weights_in, 16)
            act.dma_start(wout[:, :, :], w_out.rearrange("(k p) n -> p k n", p=P)).then_inc(weights_in, 16)
            act.dma_start(wr[:, :, :], w_r.rearrange("(k p) n -> p k n", p=P)).then_inc(weights_in, 16)
            act.dma_start(bob[:, :], bo).then_inc(weights_in, 16)
            for dst, src in ((w1b, w1), (w2b, w2), (wob, wo)):
                act.dma_start(dst[:, :, :, :], src.rearrange("e (k p) n -> p e k n", p=P)).then_inc(experts_in, 16)
            act.wait_ge(was_done, 1)
            act.wait_ge(wgnn_in, 48)
            act.activation(wh[:, :, D:D + 2 * HEADS],
                           small_ps[:, 0:KC * 2 * HEADS].rearrange("p (k c) -> p k c", k=KC), ACT.Copy)\
                .then_inc(wh_ready, 1)

            def copy_xT(n, par):
                act.wait_ge(xT_done, n + 1)
                act.activation(xnT[par], tp_ps[:, 0:KC * P], ACT.Copy).then_inc(xT_copied, 1)

            def evacuate_kv(n, par):
                act.wait_ge(k_done, n + 1)
                act.activation(ksb[par], k_ps[par][:, :], ACT.Copy)
                act.activation(sq[par][:, 0:INNER], k_ps[par][:, :], ACT.Square)
                act.wait_ge(v_done, n + 1)
                act.activation(sq[par][:, INNER:2 * INNER], v_ps[par][:, :], ACT.Square).then_inc(squared, 1)

            def evacuate_h(n, par):
                act.wait_ge(h_done, n + 1)
                if not (isinstance(n, int) and n < 2):
                    act.wait_ge(h_stored[par], (n - par) * 8)
                act.activation(hst[par][:, 0:HEADS * HG].rearrange("p (h c) -> p h c", h=HEADS)[:, :, 0:C],
                               mix_ps[:, 0:D].rearrange("p (h c) -> p h c", h=HEADS), ACT.Copy)
                act.activation(asad[:, bass.ds(n, 1), :].rearrange("p a c -> p (a c)"),
                               mix_ps[:, D:D + 2 * HEADS], ACT.Copy)
                act.activation(hst[par][:, HEADS * HG:ROW], mix_ps[:, D:D + HEADS], ACT.Copy)\
                    .then_inc(h_staged, 1)

            def x_std(n):
                act.wait_ge(x_var, n + 1)
                act.activation(rs1[:, :], ve1[:, :], ACT.Sqrt).then_inc(x_rooted, 1)

            def kv_std(n):
                act.wait_ge(kv_var, n + 1)
                act.activation(rs2[:, :], ve2[:, :], ACT.Sqrt).then_inc(kv_rooted, 1)

            def tile1(n, par, left):
                evacuate_kv(n, par)
                if left > 0:
                    copy_xT(n + 1, 1 - par)
                evacuate_h(n, par)
                kv_std(n)
                if left > 1:
                    x_std(n + 2)

            act.wait_ge(bn_var, 1)
            act.activation(bns[:, :, :], bns[:, :, :], ACT.Sqrt).then_inc(bn_rooted, 1)
            act.wait_ge(const_made, 3)
            x_std(0)
            x_std(1)
            copy_xT(0, 0)
            tile1(0, 0, 2)
            tile1(1, 1, 2)
            with act.Fori(2, LAST - 2, 2) as n0:
                for par in range(2):
                    tile1(n0 + par, par, 2)
            for n in range(LAST - 2, NT):
                tile1(n, n % 2, LAST - n)

            act.wait_ge(self_scores, 1)
            act.activation(pself[:, :, :], small2[:, :, :], ACT.Exp).then_inc(self_probs, 1)
            act.wait_ge(z_done, 1)
            for j in range(2):
                act.activation(zsb[:, j * 512:(j + 1) * 512], k_ps[j][:, :], ACT.Copy).then_inc(z_copied, 1)
            act.wait_ge(m_done, 1)
            act.activation(msb[:, :, :], v_ps[0][:, :].rearrange("p (k n) -> p k n", k=KC), ACT.Copy,
                           scale=1.0 / n_nodes).then_inc(m_copied, 1)
            act.wait_ge(phase2_ready, 1)

            def load_tile(n, par):
                act.dma_start(xin[par], x[bass.ds(n * P, P), :]).then_inc(xin_in[par], 16)
                act.dma_start(hself[par], h_rows[bass.ds(n * P, P), :]).then_inc(xin_in[par], 16)

            def exp_step(s):
                act.wait_ge(scores_ready, s + 1)
                act.activation(prob[:, bass.ds(s % 2, 1), :, :].rearrange("p b j h -> p (b j h)"),
                               sc.rearrange("p j h -> p (j h)"), ACT.Exp).then_inc(probs_ready, 1)

            def late_zT(n, q):
                act.wait_ge(zT_done, n + 1)
                act.activation(zTb[:, :, q * P:(q + 1) * P], tp_ps[:, 0:KC * P].rearrange("p (k n) -> p k n", k=KC),
                               ACT.Copy).then_inc(zT_copied, 1)

            def late_router(n):
                act.wait_ge(logits_ready, n + 1)
                act.activation(small[:, 16:24], small[:, 8:16], ACT.Exp, accum_out=small[:, 24:25]).then_inc(wexp_done, 1)
                act.wait_ge(wT_done, n + 1)
                act.activation(wT[0:EXPERTS, :], wT_ps, ACT.Copy).then_inc(wT_copied, 1)

            def section(n, q, bases=None, first_tile=False):
                late = None if first_tile else n - 1
                part_no = (q - 1) % SUP
                if not first_tile:
                    act.wait_ge(self_ready, n)
                load_tile((n + 1) % NT, (q + 1) % 2)
                if bases is not None:
                    expert_relus(part_no, bases, 0, SUP * P)
                first = act.value_load(meta[0:1, bass.ds(n, 1)], min_val=0, max_val=MAX_STEPS)
                body = act.value_load(meta[0:1, bass.ds(n + 64, 1)], min_val=1, max_val=MAX_STEPS)
                if late is not None:
                    late_zT(late, part_no)
                exp_step(first)
                if bases is not None:
                    expert_relus(part_no, bases, 1, SUP * P)
                act.wait_ge(xnT2_done, n + 1)
                act.activation(xnTb, tp_ps[:, 0:KC * P], ACT.Copy).then_inc(xnT2_copied, 1)
                if late is not None:
                    late_router(late)
                if bases is not None and part_no == SUP - 1:
                    store_out(n)
                with act.Fori(1, body + 2) as k:
                    exp_step(first + k)
                act.wait_ge(neg_ready, n + 1)
                act.activation(neg, neg, ACT.Exp).then_inc(neg_exped, 1)

            def store_out(n):
                act.wait_ge(acc_done, n * 4 - 4 * SUP)
                act.dma_start(out[bass.ds(n * P - 2 * SUP * P, SUP * P), :].rearrange("(t p) c -> p t c", p=P),
                              outb).then_inc(out_stored, 16)

            def expert_relus(q, bases, layer, width):
                fbase, _, _ = bases
                for i in range(4):
                    act.wait_ge(ff_done, fbase + (4 * layer + i + 1))
                    col = 2 * (2 * q + i // 2) + i % 2
                    act.activation((h1, h2)[layer][i // 2][:, i % 2, 0:width], ff_ps[i][:, 0:width], ACT.Relu,
                                   bias=bnt[:, layer, col:col + 1], scale=bns[:, layer, col:col + 1])\
                        .then_inc(relu_done, 1)

            act.sem_inc(out_stored, 16)
            load_tile(0, 0)
            for n in range(SUP + 1):
                section(n, n % SUP, first_tile=n == 0)
            with act.Fori(1, NSUP) as g:
                for q in range(1, SUP + 1):
                    section(g * SUP + q, q % SUP, part_bases(g, q - 1))
            expert_relus(0, part_bases(NSUP, 0), 0, SUP * P)
            late_zT(LAST, 0)
            expert_relus(0, part_bases(NSUP, 0), 1, SUP * P)
            late_router(LAST)
            for q in range(1, SUP):
                for layer in range(2):
                    expert_relus(q, part_bases(NSUP, q), layer, SUP * P)
            store_out(LAST + SUP)
            for q in range(SUP):
                for layer in range(2):
                    expert_relus(q, last_bases(q), layer, P)
            act.wait_ge(acc_done, NSUP * 4 * SUP + 2 * SUP)
            act.dma_start(out[LAST * P:NT * P, :], outb[:, 0, :]).then_inc(out_stored, 16)
            act.wait_ge(out_stored, 16 * (NSUP + 2))

        @block.vector
        def _(dve):
            dve.wait_ge(const_made, 3)
            prep = Chain(dve, setup_chain, 0, 9)
            dve.memset(base_f[:, 0:1], 0.0)
            dve.tensor_copy(node_pf[:, :], node_i[:, :])
            prep.link(dve.tensor_copy(iota_f[:, :], iota_i[:, :]))
            prep.link(dve.tensor_scalar(base_f[:, 1:NT + 1], iota_f[:, 0:NT], 1.0, float(P), ALU.add, ALU.mult))
            dve.wait_ge(weights_in, 112)
            for k in range(KC):
                prep.link(dve.tensor_reduce(mean16[:, k, :], wkv[:, k, :].rearrange("p (h c) -> p h c", c=MD), axis=AX_X,
                                            op=ALU.add))
            prep.link(dve.tensor_scalar(mean16[:, :, :], mean16[:, :, :], 1.0 / MD, None, ALU.mult))
            for k in range(KC):
                dve.tensor_tensor(wkv[:, k, :].rearrange("p (h c) -> p h c", c=MD),
                                  wkv[:, k, :].rearrange("p (h c) -> p h c", c=MD),
                                  mean16[:, k, :].unsqueeze(2).broadcast_to([P, 16, MD]), ALU.subtract)
            par10 = bnp[:, :, :].rearrange("p (l f) c -> p l f c", l=2)
            dve.tensor_scalar(bns[:, :, :], par10[:, :, 4, :], BN_EPS, None, ALU.add).then_inc(bn_var, 1)
            dve.wait_ge(bn_rooted, 1)
            prep.link(dve.reciprocal(bns[:, :, :], bns[:, :, :]))
            prep.link(dve.tensor_tensor(bns[:, :, :], bns[:, :, :], par10[:, :, 1, :], ALU.mult))
            prep.link(dve.tensor_tensor(bnt[:, :, :], par10[:, :, 0, :], par10[:, :, 3, :], ALU.subtract))
            prep.link(dve.tensor_tensor(bnt[:, :, :], bnt[:, :, :], bns[:, :, :], ALU.mult))
            dve.tensor_tensor(bnt[:, :, :], bnt[:, :, :], par10[:, :, 2, :], ALU.add)
            dve.tensor_scalar(rowsb[:, D:2 * D], rowsb[:, D:2 * D], -1.0, None, ALU.add).then_inc(weights_ready, 1)
            dve.wait_ge(weights_ready, 1)
            prep.end()
            dve.wait_ge(dst_in, 16)

            def norm(n, par, first=None):
                c = Chain(dve, ln_chain, n * 4, 4)
                dve.wait_ge(x_in[par], (n - par) * 8 + 16)
                c.link(dve.bn_stats(stats[:, :], xt[par]))
                c.link(dve.tensor_scalar(below, dst_all, base_f[:, bass.ds(n + 1, 1)], 0.0, ALU.is_lt, ALU.add,
                                         accum_out=cnt[:, bass.ds(n, 1)]))
                dve.memset(small[:, 63:64], 0.0)
                c.link(dve.bn_aggr(mv[:, :], stats[:, :]))
                dve.tensor_scalar(ve1[:, :], mv[:, 1:2], EPS, None, ALU.add).then_inc(x_var, 1)
                dve.tensor_copy(mean_n[:, bass.ds(n, 1)], mv[:, 0:1])
                if first is None:
                    dve.wait_ge(xT_done, n - 1)
                dve.wait_ge(x_rooted, n + 1)
                c.link(dve.reciprocal(rstd_n[:, bass.ds(n, 1)], rs1[:, 0:1]))
                dve.tensor_scalar(xn[par], xt[par], mv[:, 0:1], rstd_n[:, bass.ds(n, 1)], ALU.subtract, ALU.mult)\
                    .then_inc(normed, 1)
                c.end()

            def scale_v(n, par):
                c = Chain(dve, kv_chain, n * 3, 3)
                dve.wait_ge(squared, n + 1)
                c.link(dve.tensor_reduce(small[:, 0:16], sq[par].rearrange("p (h c) -> p h c", c=MD), axis=AX_X, op=ALU.add))
                c.link(dve.tensor_scalar(small[:, 16:32], small[:, 0:16], 1.0 / MD, EPS, ALU.mult, ALU.add))
                dve.tensor_tensor(ve2[:, :], small[:, 16:24], small[:, 24:32], ALU.mult).then_inc(kv_var, 1)
                dve.wait_ge(kv_rooted, n + 1)
                c.link(dve.reciprocal(rs3[:, :], rs2[:, :]))
                c.end()
                dve.tensor_tensor(vsb[par].rearrange("p (h c) -> p h c", c=MD),
                                  v_ps[par][:, :].rearrange("p (h c) -> p h c", c=MD),
                                  rs3[:, :].unsqueeze(2).broadcast_to([P, MH, MD]), ALU.mult).then_inc(v_scaled, 1)

            norm(0, 0, True)
            norm(1, 1, True)
            scale_v(0, 0)
            with dve.Fori(2, LAST, 2) as n0:
                norm(n0, 0)
                scale_v(n0 - 1, 1)
                norm(n0 + 1, 1)
                scale_v(n0, 0)
            norm(LAST, 0)
            scale_v(LAST - 1, 1)
            scale_v(LAST, 0)

            mid = Chain(dve, mid_chain, 0, 30)
            link = mid.link
            link(dve.memset(dtb, 0.0))
            dve.wait_ge(dt_done, NT + 1)
            dt_v = acc_ps[:, :].rearrange("p (j c) -> p j c", j=4)
            dt_b = dtb.rearrange("p (j c) -> p j c", j=4)
            dve.tensor_copy(dt_b[0:MD, :, 0:MD], dt_v[0:MD, :, 0:MD])
            dve.tensor_copy(dt_b[MD:P, :, MD:P], dt_v[MD:P, :, MD:P]).then_inc(dt_copied, 1)
            dve.wait_ge(h_staged, NT)
            dve.tensor_reduce(gmax[:, 0, :], asad[:, :, 0:HEADS].rearrange("p n h -> p h n"), axis=AX_X, op=ALU.max)\
                .then_inc(gmax_local, 1)
            dve.wait_ge(counts_summed, 1)
            rp, k_f, k_sum, t0, tmp = (sched[:, i, :] for i in range(5))
            link(dve.memset(sched[:, :, :], 0.0))
            link(dve.tensor_copy(rp[:, 1:NT + 1], small_ps[0:1, 0:NT]))
            link(dve.tensor_tensor(tmp[:, 0:NT], rp[:, 1:NT + 1], rp[:, 0:NT], ALU.subtract))
            link(dve.tensor_scalar(sched_i[:, 0, 0:NT], tmp[:, 0:NT], float(STEP - 1), None, ALU.add))
            link(dve.tensor_scalar(sched_i[:, 1, 0:NT], sched_i[:, 0, 0:NT], STEP.bit_length() - 1, None, ALU.arith_shift_right))
            link(dve.tensor_scalar(k_f[:, 0:NT], sched_i[:, 1, 0:NT], 3.0, None, ALU.max))
            zero_row = sched[:, 7, 0:NT]
            link(dve.tensor_tensor_scan(k_sum[:, 0:NT], k_f[:, 0:NT], zero_row, 0.0, ALU.add, ALU.add))
            link(dve.tensor_tensor(t0[:, 0:NT], k_sum[:, 0:NT], k_f[:, 0:NT], ALU.subtract))
            link(dve.tensor_scalar(sched_i[:, 2, 0:1], k_sum[:, NT - 1:NT], float(RING - 1), None, ALU.add))
            link(dve.tensor_scalar(sched_i[:, 3, 0:1], sched_i[:, 2, 0:1], RING.bit_length() - 1, None, ALU.arith_shift_right))
            link(dve.tensor_copy(meta[:, 128:129], sched_i[:, 3, 0:1]))
            link(dve.tensor_scalar(tmp[:, 0:1], sched_i[:, 3, 0:1], float(RING), None, ALU.mult))
            link(dve.tensor_tensor(k_f[:, NT - 1:NT], tmp[:, 0:1], t0[:, NT - 1:NT], ALU.subtract))
            link(dve.tensor_copy(meta[:, 0:NT], t0[:, 0:NT]))
            link(dve.tensor_scalar(meta[:, 64:64 + NT], k_f[:, 0:NT], -2.0, None, ALU.add))
            base_n, dif = sched[:, 5, :], sched[:, 6, :]
            link(dve.scalar_tensor_tensor(base_n[:, 1:NT + 1], t0[:, 0:NT], -float(STEP), rp[:, 0:NT], ALU.mult, ALU.add))
            dve.tensor_tensor(dif[:, 0:NT], base_n[:, 1:NT + 1], base_n[:, 0:NT], ALU.subtract).then_inc(sched_rows, 1)
            dve.wait_ge(sched_cols, 1)
            link(dve.tensor_copy(cols[0:NT, :], small_ps[0:NT, 64:66]))
            dve.tensor_scalar(steps_f[0:NT, :], iota_f[0:NT, :], cols[0:NT, 0:1], cols[0:NT, 1:2], ALU.is_ge, ALU.mult)\
                .then_inc(steps_masked, 1)
            dve.wait_ge(steps_summed, 1)
            for i, ps in enumerate((mix_ps, tp_ps)):
                part_ = slice(i * MAX_STEPS // 2, (i + 1) * MAX_STEPS // 2)
                link(dve.scalar_tensor_tensor(steps_i[:, part_], iota_f[0:1, part_], float(STEP), ps[0:1, 0:MAX_STEPS // 2],
                                              ALU.mult, ALU.add))
            dve.wait_ge(gmax_all, 1)
            link(dve.tensor_copy(adc[:, :, 0:HEADS], asad[:, :, HEADS:2 * HEADS]))
            link(dve.tensor_tensor(small2[:, :, :], asad[:, :, HEADS:2 * HEADS],
                                   gmax[:, 1, :].unsqueeze(1).broadcast_to([P, NT, HEADS]), ALU.add))
            link(dve.scalar_tensor_tensor(adc[:, :, HEADS:2 * HEADS], small2[:, :, :], 0.2, small2[:, :, :], ALU.mult, ALU.max))
            link(dve.tensor_copy(adc3[:, :, 0, :], adc[:, :, :]))
            link(dve.tensor_tensor(adc_r[:, :, :], adc[:, :, :], adc3[:, :, 0, :], ALU.subtract))
            link(dve.tensor_copy(adc3[:, :, 1, :], adc_r[:, :, :]))
            link(dve.tensor_tensor(adc_r[:, :, :], adc_r[:, :, :], adc3[:, :, 1, :], ALU.subtract))
            link(dve.tensor_copy(adc3[:, :, 2, :], adc_r[:, :, :]))
            link(dve.tensor_tensor(small2[:, :, :], asad[:, :, 0:HEADS], asad[:, :, HEADS:2 * HEADS], ALU.add))
            link(dve.scalar_tensor_tensor(pself[:, :, :], small2[:, :, :], 0.2, small2[:, :, :], ALU.mult, ALU.max))
            link(dve.tensor_tensor(small2[:, :, :], pself[:, :, :], adc[:, :, HEADS:2 * HEADS], ALU.subtract))
            dve.tensor_scalar(small2[:, :, :], small2[:, :, :], 0.0, None, ALU.min).then_inc(self_scores, 1)
            link(dve.tensor_scalar(keep_a[:, :], rstd_n[:, :], 1.0, None, ALU.add))
            link(dve.scalar_tensor_tensor(keep_b[:, :], mean_n[:, :], -1.0, rstd_n[:, :], ALU.mult, ALU.mult))
            dve.wait_ge(self_probs, 1)
            dve.wait_ge(m_copied, 1)
            dve.wait_ge(h_stored[0], 16 * ((NT + 1) // 2))
            dve.wait_ge(h_stored[1], 16 * (NT // 2))
            link(dve.tensor_copy(small[:, 0:1], keep_a[:, 0:1]))
            link(dve.tensor_copy(small[:, 1:2], keep_b[:, 0:1]))
            mid.per = mid.n
            dve.tensor_copy(small[:, 2:3], keep_b[:, 0:1]).then_inc(phase2_ready, 1)

            def slot(s):
                return bass.ds(s % RING, 1)

            def onehot_t(n, s):
                dve.wait_ge(rows_ready, s + 1)
                src = dstrow[:, slot(s), :].rearrange("p a (e j) -> p (a j) e", j=TPS)
                dve.tensor_scalar(oht, src, node_pf[:, bass.ds(n, 1)], None, ALU.is_equal).then_inc(oht_ready, 1)

            def score(s, i):
                if i == 0:
                    dve.wait_ge(adg_ready, s + 1)
                    a_src = ring[:, slot(s), :, HEADS * HG:ROW].rearrange("p a j c -> p (a j) c")
                    dve.tensor_tensor(sc2, adg_ps[:, :, 0:HEADS], a_src, ALU.add).then_inc(score_chain, 1)
                    return
                dve.wait_ge(score_chain, s * 3 + i)
                if i == 1:
                    dve.scalar_tensor_tensor(sc, sc2, 0.2, sc2, ALU.mult, ALU.max).then_inc(score_chain, 1)
                elif i == 2:
                    dve.tensor_tensor(sc2, sc, adg_ps[:, :, HEADS:2 * HEADS], ALU.subtract).then_inc(score_chain, 1)
                else:
                    dve.tensor_scalar(sc, sc2, 0.0, None, ALU.min).then_inc(scores_ready, 1)

            def onehot(s, half):
                dve.wait_ge(half_summed[half], s + 1)
                d = idx[:, slot(s), 2 * half:2 * half + 2, 1].rearrange("p a j -> p (a j)")
                dve.tensor_tensor(oh[half], window.unsqueeze(1).broadcast_to([P, 2, P]),
                                  d.unsqueeze(2).broadcast_to([P, 2, P]), ALU.is_equal)

            def message(s, half):
                if half == 0:
                    dve.wait_ge(probs_ready, s + 1)
                js = slice(2 * half, 2 * half + 2)
                rows_ = ring[:, slot(s), js, 0:HEADS * HG].rearrange("p a j (h c) -> p (a j) h c", h=HEADS)
                w_ = prob[:, bass.ds(s % 2, 1), js, :].rearrange("p a j h -> p (a j) h")
                dve.tensor_tensor(msg[half], rows_, w_.unsqueeze(3).broadcast_to([P, 2, HEADS, HG]), ALU.mult)\
                    .then_inc(msg_ready[half], 1)

            def step(n, s, ahead):
                onehot(s, 0)
                message(s, 0)
                if ahead > 0:
                    score(s + 1, 0)
                if ahead > 1:
                    onehot_t(n, s + 2)
                if ahead > 0:
                    score(s + 1, 1)
                onehot(s, 1)
                if ahead > 0:
                    score(s + 1, 2)
                message(s, 1)
                if ahead > 0:
                    score(s + 1, 3)

            def rsqrt(c, out_, var):
                v, y, t = rsq[:, 0:1], rsq[:, 1:2], rsq[:, 2:3]
                c.link(dve.tensor_scalar(v, var, EPS, None, ALU.add))
                c.link(dve.tensor_scalar(y.bitcast(I32), v.bitcast(I32), -0.5, float(0x5f3759df), ALU.mult, ALU.add))
                for i in range(3):
                    c.link(dve.scalar_tensor_tensor(t, y, v, y, ALU.mult, ALU.mult))
                    c.link(dve.tensor_scalar(t, t, -0.5, 1.5, ALU.mult, ALU.add))
                    c.link(dve.tensor_tensor(out_ if i == 2 else y, y, t, ALU.mult))

            def late_router(n, q):
                c = Chain(dve, router_chain, n * 2, 2)
                dve.wait_ge(router_done, n + 1)
                c.link(dve.tensor_tensor(small[:, 8:16], rt_ps, rowsb[:, 2 * D:2 * D + EXPERTS], ALU.add))
                c.link(dve.tensor_reduce(small[:, 41:42], small[:, 8:16], axis=AX_X, op=ALU.max))
                c.end()
                dve.tensor_scalar(small[:, 8:16], small[:, 8:16], small[:, 41:42], None, ALU.subtract).then_inc(logits_ready, 1)
                dve.wait_ge(wexp_done, n + 1)
                dve.reciprocal(small[:, 42:43], small[:, 24:25]).then_inc(w_recip, 1)
                dve.wait_ge(w_recip, n + 1)
                dve.tensor_scalar(wgt[:, q, :], small[:, 16:24], small[:, 42:43], None, ALU.mult).then_inc(w_ready, 1)

            def late_bias(n, q):
                dve.wait_ge(bo_done, n + 1)
                dve.tensor_tensor(x1b[:, q, :], x1b[:, q, :], mix_ps[:, D:2 * D], ALU.add).then_inc(tile_done, 1)

            def section(n, q, bases=None, handoff=None, fresh=None, first_tile=False):
                par = q % 2
                late = None if first_tile else n - 1
                part_no = (q - 1) % SUP
                c = Chain(dve, tile_chain, n * 22, 22)
                col = bass.ds(n, 1)
                dve.wait_ge(xin_in[par], (n - par) * 16 + 32)
                dve.tensor_scalar(xnb, xin[par], mean_n[:, col], rstd_n[:, col], ALU.subtract, ALU.mult).then_inc(xn_ready, 1)
                c.link(dve.tensor_scalar(kept, xin[par], keep_a[:, col], keep_b[:, col], ALU.mult, ALU.add))
                dve.tensor_tensor(kept, kept, rowsb[:, D:2 * D], ALU.add)
                dve.tensor_tensor(mself.rearrange("p (h c) -> p h c", h=HEADS),
                                  hself[par][:, 0:HEADS * HG].rearrange("p (h c) -> p h c", h=HEADS),
                                  pself[:, col, :].rearrange("p a h -> p (a h)").unsqueeze(2).broadcast_to([P, HEADS, HG]),
                                  ALU.mult).then_inc(self_ready, 1)
                c.link(dve.tensor_scalar(window, iota_f[:, 0:P], base_f[:, col], None, ALU.add))
                first = dve.value_load(meta[0:1, bass.ds(n, 1)], min_val=0, max_val=MAX_STEPS)
                body = dve.value_load(meta[0:1, bass.ds(n + 64, 1)], min_val=1, max_val=MAX_STEPS)
                onehot_t(n, first)
                for i in range(4):
                    score(first, i)
                onehot_t(n, first + 1)
                if late is not None:
                    late_router(late, part_no)
                if bases is not None:
                    expert_sums(part_no, bases, SUP, handoff, fresh)
                if late is not None:
                    late_bias(late, part_no)
                    if part_no == SUP - 1:
                        hand_over(n, SUP, None if bases is None else n * 4 - 4 * SUP)

                with dve.Fori(0, body) as k:
                    step(n, first + k, 2)
                step(n, first + body, 1)
                step(n, first + (body + 1), 0)

                dve.wait_ge(tile_summed, n + 1)
                sums = acc_ps[:, 0:HEADS * HG].rearrange("p (h c) -> p h c", h=HEADS)
                c.link(dve.tensor_scalar(small[:, 0:4], sums[:, :, C], 1e-16, None, ALU.add))
                c.link(dve.reciprocal(small[:, 4:8], small[:, 0:4]))
                c.link(dve.tensor_tensor(gat.rearrange("p (h c) -> p h c", h=HEADS), sums[:, :, 0:C],
                                         small[:, 4:8].unsqueeze(2).broadcast_to([P, HEADS, C]), ALU.mult))
                c.link(dve.tensor_tensor(gat, gat, rowsb[:, 0:D], ALU.add))
                dve.tensor_scalar(neg, gat, 0.0, None, ALU.min).then_inc(neg_ready, 1)
                dve.wait_ge(mix_done, n + 1)
                c.link(dve.tensor_tensor(kept, kept, mix_ps[:, 0:D], ALU.add))
                dve.wait_ge(neg_exped, n + 1)
                c.link(dve.scalar_tensor_tensor(gat, gat, 0.0, neg, ALU.max, ALU.add))
                x1 = x1b[:, q, :]
                c.link(dve.tensor_tensor(x1, gat, kept, ALU.add))
                c.link(dve.bn_stats(stats[:, :], x1))
                dve.memset(small[:, 63:64], 0.0)
                c.link(dve.bn_aggr(mv[:, :], stats[:, :]))
                rsqrt(c, small[:, 40:41], mv[:, 1:2])
                dve.tensor_scalar(zb, x1, mv[:, 0:1], small[:, 40:41], ALU.subtract, ALU.mult).then_inc(z_ready, 1)
                c.end()

            def expert_sums(q, bases, tiles, handoff, fresh=None):
                fbase, _, abase = bases
                pairs = max(1, tiles // 2)
                for i in range(2 * pairs):
                    e = 2 * q + i // pairs
                    t0_ = 2 * (i % pairs)
                    dve.wait_ge(ff_done, fbase + (9 + i))
                    if q == 0 and i < pairs:
                        dve.wait_ge(handed, handoff)
                    else:
                        dve.wait_ge(acc_done, abase + (i - pairs + 1))
                    if e == EXPERTS - 1:
                        dve.wait_ge(out_stored, fresh)
                    for t in range(t0_, min(t0_ + 2, tiles)):
                        ins = dve.scalar_tensor_tensor((outb if e == EXPERTS - 1 else acc)[:, t, :], ff_ps[i][:, (t - t0_) * D:(t - t0_ + 1) * D],
                                                       wgf[:, t, e:e + 1], acc[:, t, :], ALU.mult, ALU.add)
                    ins.then_inc(acc_done, 1)

            def hand_over(n_done, tiles, summed):
                if summed is not None:
                    dve.wait_ge(acc_done, summed)
                dve.wait_ge(tile_done, n_done)
                dve.tensor_copy(acc[:, 0:tiles, :], x1b[:, 0:tiles, :])
                dve.tensor_copy(wgf[:, 0:tiles, :], wgt[:, 0:tiles, :])
                dve.tensor_copy(zTf[:, :, 0:tiles * P], zTb[:, :, 0:tiles * P]).then_inc(handed, 1)

            for n in range(SUP + 1):
                section(n, n % SUP, first_tile=n == 0)
            with dve.Fori(1, NSUP) as g:
                for q in range(1, SUP + 1):
                    section(g * SUP + q, q % SUP, part_bases(g, q - 1), g, fresh=16 * g)
            late_router(LAST, 0)
            expert_sums(0, part_bases(NSUP, 0), SUP, NSUP)
            late_bias(LAST, 0)
            for q in range(1, SUP):
                expert_sums(q, part_bases(NSUP, q), SUP, NSUP, fresh=16 * NSUP)
            hand_over(LAST + 1, 1, 4 * SUP * NSUP)
            for q in range(SUP):
                expert_sums(q, last_bases(q), 1, NSUP + 1, fresh=16 * (NSUP + 1))

        @block.tensor
        def _(pe):
            def product(out_, pairs, sem_=None, start=True, stop=True):
                for i, (lhsT, rhs) in enumerate(pairs):
                    ins = pe.matmul(out_, lhsT, rhs, start=start and i == 0, stop=stop and i == len(pairs) - 1)
                if sem_ is not None:
                    ins.then_inc(sem_, 1)

            pe.wait_ge(const_made, 3)
            pe.wait_ge(wgnn_in, 48)
            for k in range(KC):
                product(small_ps[:, k * 2 * HEADS:(k + 1) * 2 * HEADS],
                        [(wg[:, o, k * P:(k + 1) * P], attb[:, o, :]) for o in range(KC)],
                        was_done if k == KC - 1 else None)
            product(acc_ps[:, :], [(zeros[:, 0:P], zeros[:, :])], stop=False)

            def transpose_x(n, par):
                pe.wait_ge(normed, n + 1)
                for k in range(KC):
                    ins = pe.transpose(tp_ps[:, k * P:(k + 1) * P], xn[par][:, k * P:(k + 1) * P], ident[:, :])
                ins.then_inc(xT_done, 1)

            def sum_dt(n, par):
                pe.wait_ge(v_scaled, n + 1)
                for j in range(4):
                    ins = pe.matmul(acc_ps[:, j * P:(j + 1) * P], vsb[par][:, j * P:(j + 1) * P],
                                    ksb[par][:, j * P:(j + 1) * P], start=False, stop=False)
                ins.then_inc(dt_done, 1)

            def project(n, par):
                pe.wait_ge(xT_copied, n + 1)
                xT = [xnT[par][:, k * P:(k + 1) * P] for k in range(KC)]
                product(k_ps[par][:, :], [(xT[k], wkv[:, k, 0:INNER]) for k in range(KC)], k_done)
                product(v_ps[par][:, :], [(xT[k], wkv[:, k, INNER:2 * INNER]) for k in range(KC)], v_done)
                if not (isinstance(n, int) and n == 0):
                    pe.wait_ge(h_staged, n)
                product(mix_ps[:, 0:D + 2 * HEADS], [(xT[k], wh[:, k, :]) for k in range(KC)], h_done)

            pe.wait_ge(weights_ready, 1)
            pe.wait_ge(wh_ready, 1)
            for n in range(2):
                transpose_x(n, n)
                project(n, n)
            with pe.Fori(2, LAST, 2) as n0:
                for par in range(2):
                    transpose_x(n0 + par, par)
                    sum_dt(n0 + (par - 2), par)
                    project(n0 + par, par)
            transpose_x(LAST, 0)
            sum_dt(LAST - 2, 0)
            project(LAST, 0)
            sum_dt(LAST - 1, 1)
            sum_dt(LAST, 0)
            product(acc_ps[:, :], [(zeros[:, 0:P], zeros[:, :])], dt_done, start=False)

            product(small_ps[0:1, 0:NT], [(ones[:, 0:1], cnt[:, 0:NT])], counts_summed)
            pe.wait_ge(dt_copied, 1)
            for j in range(4):
                product(k_ps[j // 2][:, (j % 2) * D:(j % 2 + 1) * D], [(dtb[:, j * P:(j + 1) * P], wout[:, j, :])],
                        z_done if j == 3 else None)
            pe.wait_ge(sched_rows, 1)
            product(small_ps[0:NT, 64:65], [(sched[0:1, 3, 0:NT], ones[0:1, 0:1])])
            product(small_ps[0:NT, 65:66], [(sched[0:1, 6, 0:NT], ones[0:1, 0:1])], sched_cols)
            pe.wait_ge(steps_masked, 1)
            for i, ps in enumerate((mix_ps, tp_ps)):
                product(ps[0:1, 0:MAX_STEPS // 2],
                        [(ones[0:NT, 0:1], steps_f[0:NT, i * MAX_STEPS // 2:(i + 1) * MAX_STEPS // 2])],
                        steps_summed if i else None)
            pe.wait_ge(z_copied, 2)
            for f in range(KC):
                product(v_ps[0][:, f * D:(f + 1) * D],
                        [(wqt[:, j, f * P:(f + 1) * P], zsb[:, j * D:(j + 1) * D]) for j in range(4)],
                        m_done if f == KC - 1 else None)

            pe.wait_ge(phase2_ready, 1)
            for half in range(2):
                pe.sem_inc(half_summed[half], 1)

            def target_scores(n, s):
                pe.wait_ge(oht_ready, s + 1)
                for j in range(TPS):
                    for i in range(3):
                        ins = pe.matmul(adg_ps[:, j, :], oht[:, j, :],
                                        adc3[:, bass.ds(n, 1), i, :].rearrange("p a c -> p (a c)"), start=i == 0, stop=i == 2)
                ins.then_inc(adg_ready, 1)

            def sum_half(s, half):
                pe.wait_ge(msg_ready[half], s + 1)
                for j in range(2):
                    ins = pe.matmul(acc_ps[:, 0:HEADS * HG], oh[half][:, j, :],
                                    msg[half][:, j, :, :].rearrange("p h c -> p (h c)"), start=False, stop=False)
                ins.then_inc(half_summed[half], 1)

            def layer1(q, bases, width, handoff):
                _, _, abase = bases
                for i in range(4):
                    if q == 0:
                        if i == 0:
                            pe.wait_ge(handed, handoff)
                    else:
                        pe.wait_ge(acc_done, abase + ((i - 3) if width > P else min(0, i - 1)))
                    e, m = 2 * q + i // 2, i % 2
                    product(ff_ps[i][:, 0:width],
                            [(w1b[:, e, k, m * P:(m + 1) * P], zTf[:, k, 0:width]) for k in range(KC)], ff_done)

            def layer2(q, bases, width):
                _, rbase, _ = bases
                for i in range(4):
                    if i % 2 == 0:
                        pe.wait_ge(relu_done, rbase + (i + 2))
                    e, m = 2 * q + i // 2, i % 2
                    product(ff_ps[i][:, 0:width],
                            [(w2b[:, e, k, m * P:(m + 1) * P], h1[i // 2][:, k, 0:width]) for k in range(KC)], ff_done)

            def layer3(q, bases, tiles, which):
                _, rbase, _ = bases
                pairs = max(1, tiles // 2)
                pe.wait_ge(relu_done, rbase + (6 + 2 * which))
                for i in range(which * pairs, (which + 1) * pairs):
                    e = 2 * q + which
                    t0_ = 2 * (i % pairs)
                    for t in range(t0_, min(t0_ + 2, tiles)):
                        end = t == min(t0_ + 2, tiles) - 1
                        product(ff_ps[i][:, (t - t0_) * D:(t - t0_ + 1) * D],
                                [(h2[which][:, k, t * P:(t + 1) * P], wob[:, e, k, :]) for k in range(KC)],
                                ff_done if end else None)

            def transpose_pair(src, done):
                for k in range(KC):
                    ins = pe.transpose(tp_ps[:, k * P:(k + 1) * P], src[:, k * P:(k + 1) * P], ident[:, :])
                ins.then_inc(done, 1)

            def late_zT(n):
                pe.wait_ge(z_ready, n + 1)
                transpose_pair(zb, zT_done)

            def late_router(n, q):
                pe.wait_ge(zT_copied, n + 1)
                product(rt_ps, [(zTb[:, k, q * P:(q + 1) * P], wr[:, k, :]) for k in range(KC)], router_done)

            def late_wT(n, q):
                pe.wait_ge(w_ready, n + 1)
                pe.transpose(wT_ps, wgt[:, q, :], ident[:, :]).then_inc(wT_done, 1)

            def late_bo(n):
                pe.wait_ge(wT_copied, n + 1)
                product(mix_ps[:, D:2 * D], [(wT[0:EXPERTS, :], bob[:, :])], bo_done)

            def section(n, q, bases=None, handoff=None, first_tile=False):
                late = None if first_tile else n - 1
                part_no = (q - 1) % SUP
                if bases is not None:
                    layer1(part_no, bases, SUP * P, handoff)
                first = pe.value_load(meta[0:1, bass.ds(n, 1)], min_val=0, max_val=MAX_STEPS)
                body = pe.value_load(meta[0:1, bass.ds(n + 64, 1)], min_val=1, max_val=MAX_STEPS)
                if late is not None:
                    late_zT(late)
                target_scores(n, first)
                if bases is not None:
                    layer2(part_no, bases, SUP * P)
                if late is not None:
                    late_router(late, part_no)
                target_scores(n, first + 1)
                pe.wait_ge(xn_ready, n + 1)
                transpose_pair(xnb, xnT2_done)
                if bases is not None:
                    layer3(part_no, bases, SUP, 0)
                pe.wait_ge(xnT2_copied, n + 1)
                if late is not None:
                    late_wT(late, part_no)
                product(mix_ps[:, 0:D], [(xnTb[:, k * P:(k + 1) * P], msb[:, k, :]) for k in range(KC)], mix_done)
                if bases is not None:
                    layer3(part_no, bases, SUP, 1)
                if late is not None:
                    late_bo(late)
                product(acc_ps[:, 0:HEADS * HG], [(zeros[:, 0:P], zeros[:, 0:HEADS * HG])], stop=False)
                with pe.Fori(0, body) as k:
                    sum_half(first + k, 0)
                    sum_half(first + k, 1)
                    target_scores(n, first + k + 2)
                for k in range(2):
                    sum_half(first + (body + k), 0)
                    sum_half(first + (body + k), 1)
                pe.wait_ge(self_ready, n + 1)
                product(acc_ps[:, 0:HEADS * HG], [(ident[:, :], mself)], tile_summed, start=False)

            for n in range(SUP + 1):
                section(n, n % SUP, first_tile=n == 0)
            pe.wait_ge(experts_in, 48)
            with pe.Fori(1, NSUP) as g:
                for q in range(1, SUP + 1):
                    section(g * SUP + q, q % SUP, part_bases(g, q - 1), g)
            layer1(0, part_bases(NSUP, 0), SUP * P, NSUP)
            late_zT(LAST)
            layer2(0, part_bases(NSUP, 0), SUP * P)
            late_router(LAST, 0)
            layer3(0, part_bases(NSUP, 0), SUP, 0)
            late_wT(LAST, 0)
            layer3(0, part_bases(NSUP, 0), SUP, 1)
            late_bo(LAST)
            for q in range(1, SUP):
                layer1(q, part_bases(NSUP, q), SUP * P, NSUP)
                layer2(q, part_bases(NSUP, q), SUP * P)
                for which in range(2):
                    layer3(q, part_bases(NSUP, q), SUP, which)
            for q in range(SUP):
                layer1(q, last_bases(q), P, NSUP + 1)
                layer2(q, last_bases(q), P)
                for which in range(2):
                    layer3(q, last_bases(q), 1, which)


def kernel(x, src, dst, L0_gnn_W, L0_gnn_att_src, L0_gnn_att_dst, L0_gnn_bias, L0_mix_w_qkv, L0_mix_w_out, L0_mix_b_out,
           L0_ffn_Wr, L0_ffn_br, L0_ffn_W1, L0_ffn_b1, L0_ffn_g1, L0_ffn_be1, L0_ffn_m1, L0_ffn_v1, L0_ffn_W2, L0_ffn_b2,
           L0_ffn_g2, L0_ffn_be2, L0_ffn_m2, L0_ffn_v2, L0_ffn_Wo, L0_ffn_bo):
    import numpy as np
    import concourse.bacc as bacc
    from concourse.bass_utils import run_bass_kernel_spmd

    f = np.ascontiguousarray
    n, e = x.shape[0], src.shape[0]
    rows_pad = -(-n // P) * P - n
    edge_pad = -(-e // P) * P - e + STEP * (RING + 4)
    srcp = np.concatenate([np.asarray(src), np.zeros(edge_pad, np.int32)])
    dstp = np.concatenate([np.asarray(dst), np.full(edge_pad, 1 << 20, np.int32)])
    att = np.zeros((D, 2 * HEADS), np.float32)
    for h in range(HEADS):
        att[h * C:(h + 1) * C, h] = np.asarray(L0_gnn_att_src)[h]
        att[h * C:(h + 1) * C, HEADS + h] = np.asarray(L0_gnn_att_dst)[h]
    rows = np.tile(np.concatenate([np.asarray(L0_gnn_bias), np.asarray(L0_mix_b_out), np.asarray(L0_ffn_br)])[None], (P, 1))
    params = [L0_ffn_b1, L0_ffn_g1, L0_ffn_be1, L0_ffn_m1, L0_ffn_v1, L0_ffn_b2, L0_ffn_g2, L0_ffn_be2, L0_ffn_m2, L0_ffn_v2]
    bn = np.stack([np.asarray(a).reshape(2 * EXPERTS, P).T for a in params], axis=1)
    qkv = np.asarray(L0_mix_w_qkv)
    ins = {
        "in_x": f(np.pad(np.asarray(x), ((0, rows_pad), (0, 0)))),
        "in_sd": f(np.stack([srcp, dstp], axis=1)),
        "in_dst": f(dstp),
        "in_att": att,
        "in_w_gnn": f(L0_gnn_W),
        "in_w_gnn_t": f(np.asarray(L0_gnn_W).T),
        "in_rows": f(rows),
        "in_w_kv": f(qkv[:, INNER:]),
        "in_w_q_t": f(qkv[:, :INNER].T),
        "in_w_out": f(L0_mix_w_out),
        "in_w_r": f(L0_ffn_Wr),
        "in_bn": f(bn),
        "in_w1": f(L0_ffn_W1),
        "in_w2": f(L0_ffn_W2),
        "in_wo": f(L0_ffn_Wo),
        "in_bo": f(L0_ffn_bo),
    }
    nc = bacc.Bacc("TRN2", target_bir_lowering=False, num_devices=1)
    args = [nc.dram_tensor(k, a.shape, mybir.dt.from_np(a.dtype), kind="ExternalInput").ap() for k, a in ins.items()]
    out = nc.dram_tensor("out_x", (n + rows_pad, D), F32, kind="ExternalOutput").ap()
    gps_layer(nc, *args, out, n, e)
    r = run_bass_kernel_spmd(nc, [ins], core_ids=[0])
    return r.results[0]["out_x"][:n]
```

```python
from contextlib import ExitStack

import concourse.bass as bass
from concourse import mybir

F32 = mybir.dt.float32
BF16 = mybir.dt.bfloat16
I32 = mybir.dt.int32
ALU = mybir.AluOpType
ACT = mybir.ActivationFunctionType
AX_X = mybir.AxisListType.X

P = 128
D = 256
KC = D // P
HEADS = 4
C = D // HEADS
HG = C + 1
ROW = HEADS * HG + HEADS
MH = 8
MD = 64
INNER = MH * MD
EXPERTS = 8
SUP = 2
EPP = EXPERTS // SUP
TPS = 4
STEP = P * TPS
RING = 8
HEAD = 6
TAIL = 2
MAX_STEPS = 864
SPLIT = 1024
GUARD = 16.0
EPS = 1e-5
BN_EPS = 1e-3


class Chain:

    def __init__(self, eng, sem):
        self.eng, self.sem, self.n = eng, sem, 0

    def link(self, ins):
        self.n += 1
        ins.then_inc(self.sem, 1)
        self.eng.wait_ge(self.sem, self.n)


def gps_layer(nc, x, sd, dsts, att, w_gnn, w_gnn_t, rows, w_kv, w_q_t, w_out, w_r, bn, w1, w2, wo, bo, out, n_nodes, n_edges):
    NT = x.shape[0] // P
    NSUP = (NT - 1) // SUP
    LAST = NSUP * SUP
    assert NT == LAST + 1 and LAST % 2 == 0
    DCOLS = -(-n_edges // P)
    EMAX = sd.shape[0] - STEP
    h_rows = nc.dram_tensor("h_rows", [NT * P, ROW], F32).ap()

    ctx = ExitStack()
    with ctx:
        def sb(name, shape, dt=F32):
            return ctx.enter_context(nc.sbuf_tensor(name, shape, dt))

        def sem(name):
            return ctx.enter_context(nc.semaphore(name))

        bank = [ctx.enter_context(nc.psum_tensor(f"bank{i}", [P, 512], F32)) for i in range(8)]

        ident = sb("ident", [P, P])
        iota_f = sb("iota_f", [P, MAX_STEPS])
        node_i = sb("node_i", [P, NT + 1], I32)
        node_pf = sb("node_pf", [P, NT + 1])
        base_f = sb("base_f", [P, NT + 1])
        ones = sb("ones", [P, P])
        zeros = sb("zeros", [P, 512], BF16)
        wkv = sb("wkv", [P, KC, 2 * INNER])
        wh = sb("wh", [P, KC, D + 2 * HEADS])
        wg = sb("wg", [P, KC, D])
        attb = sb("attb", [P, KC, 2 * HEADS])
        wqt = sb("wqt", [P, INNER // P, D])
        wout = sb("wout", [P, INNER // P, D])
        wr = sb("wr", [P, KC, EXPERTS])
        rowsb = sb("rowsb", [P, 2 * D + EXPERTS])
        bnp = sb("bnp", [P, 10, 2 * EXPERTS])
        bns = sb("bns", [P, 2, 2 * EXPERTS])
        bnt = sb("bnt", [P, 2, 2 * EXPERTS])
        bob = sb("bob", [EXPERTS, D])
        w1b = sb("w1b", [P, EXPERTS, KC, D])
        w2b = sb("w2b", [P, EXPERTS, KC, D])
        wob = sb("wob", [P, EXPERTS, KC, D])
        mean16 = sb("mean16", [P, KC, 16])
        mean_n = sb("mean_n", [P, NT])
        rstd_n = sb("rstd_n", [P, NT])
        keep_a = sb("keep_a", [P, NT])
        keep_b = sb("keep_b", [P, NT])
        asad = sb("asad", [P, NT, 2 * HEADS])
        adc = sb("adc", [P, NT, 2 * HEADS])
        adc3 = sb("adc3", [P, NT + 1, 3, 2 * HEADS], BF16)
        adc_r = sb("adc_r", [P, NT, 2 * HEADS])
        pself = sb("pself", [P, NT, HEADS])
        gmax = sb("gmax", [P, 2, HEADS])
        shift = sb("shift", [P, NT, HEADS])
        msb = sb("msb", [P, KC, D])
        cnt = sb("cnt", [P, NT])
        sched = sb("sched", [1, 8, 64])
        sched_i = sb("sched_i", [1, 4, 64], I32)
        meta = sb("meta", [1, 65], I32)
        steps_i = sb("steps_i", [1, MAX_STEPS], I32)
        steps_f = sb("steps_f", [64, MAX_STEPS])
        cols = sb("cols", [64, 2])
        stats = sb("stats", [P, 6])
        mv = sb("mv", [P, 2])
        small = sb("small", [P, 64])
        rsq = sb("rsq", [P, 8])
        ve1 = sb("ve1", [P, 1])
        rs1 = sb("rs1", [P, 1])
        ve2 = sb("ve2", [P, MH])
        rs2 = sb("rs2", [P, MH])
        rs3 = sb("rs3", [P, MH])
        small2 = sb("small2", [P, NT, HEADS])

        big = sb("big", [P, 26400])
        at = [0]

        def part(n, dt=F32):
            words = -(-n * (2 if dt == BF16 else 4) // 4)
            view = big[:, at[0]:at[0] + words]
            at[0] += words + (-words) % 8
            return view if dt == F32 else view.bitcast(dt)

        at[0] = RING * (TPS * (ROW + 2) + STEP)
        iota_i = part(MAX_STEPS, I32)
        dst_all = part(DCOLS, I32)
        tile_i = part(DCOLS, I32)
        tile_of = part(DCOLS, BF16)
        below = part(DCOLS, BF16)
        xt = [part(D) for _ in range(2)]
        xn = [part(D) for _ in range(2)]
        xnT = [part(KC * P) for _ in range(2)]
        ksb = [part(INNER) for _ in range(2)]
        vsb = [part(INNER) for _ in range(2)]
        sq = [part(2 * INNER) for _ in range(2)]
        hst = [part(ROW) for _ in range(2)]
        dtb = part(4 * P)
        zsb = part(4 * D)
        at1 = at[0]
        at[0] = 0
        ring = part(RING * TPS * ROW).rearrange("p (u j c) -> p u j c", u=RING, j=TPS)
        idx = part(RING * TPS * 2, I32).rearrange("p (u j c) -> p u j c", u=RING, j=TPS)
        dstrow = part(RING * STEP, I32).rearrange("p (u e) -> p u e", u=RING)
        window = [part(P) for _ in range(2)]
        oh = [part(2 * 2 * P).rearrange("p (b j n) -> p b j n", b=2, j=2) for _ in range(2)]
        msg = [part(2 * 2 * HEADS * HG).rearrange("p (b j f) -> p b j f", b=2, j=2) for _ in range(2)]
        oht = part(TPS * P, BF16).rearrange("p (j e) -> p j e", j=TPS)
        prob = part(2 * TPS * HEADS).rearrange("p (b j h) -> p b j h", b=2, j=TPS)
        outb = part(SUP * D).rearrange("p (t c) -> p t c", t=SUP)
        sc, sc_a, sc_b = (part(TPS * HEADS).rearrange("p (j h) -> p j h", j=TPS) for _ in range(3))
        xin = [part(D) for _ in range(2)]
        hself = [part(ROW) for _ in range(2)]
        mself = part(HEADS * HG)
        gsum = part(HEADS * HG)
        xnb = part(D)
        xnTb = part(KC * P)
        kept = [part(D) for _ in range(2)]
        gat = part(D)
        neg = part(D)
        zb = part(D)
        zTf = part(KC * SUP * P).rearrange("p (k n) -> p k n", k=KC)
        zTb = part(KC * (SUP - 1) * P).rearrange("p (k n) -> p k n", k=KC)

        def zT_slot(q):
            return zTb[:, :, q * P:(q + 1) * P] if q < SUP - 1 else zTf[:, :, q * P:(q + 1) * P]
        x1b = part(SUP * D).rearrange("p (t c) -> p t c", t=SUP)
        acc = part(SUP * D).rearrange("p (t c) -> p t c", t=SUP)
        wgt = part(SUP * EXPERTS).rearrange("p (t e) -> p t e", t=SUP)
        wgf = part(SUP * EXPERTS).rearrange("p (t e) -> p t e", t=SUP)
        wT = part(P)
        def hidden(w):
            flat, n = w.rearrange("p j n -> p (j n)"), KC * SUP * P
            return [flat[:, i * n:(i + 1) * n].rearrange("p (k n) -> p k n", k=KC) for i in range(w.shape[1] * w.shape[2] // n)]

        h1 = hidden(wkv[:, :, :])
        h2 = hidden(wqt[:, :, :]) + hidden(wout[:, :, :])
        assert min(len(h1), len(h2)) >= EPP
        at2 = at[0]
        assert max(at1, at2) <= 26400, (at1, at2)

        acc_ps, small_ps, tp_ps, mix_ps = bank[:4]
        ff_ps = bank[4:]
        k_ps, v_ps = bank[4:6], bank[6:8]
        adg_ps = small_ps[:, 0:TPS * 2 * HEADS].rearrange("p (j c) -> p j c", j=TPS)
        rt_ps = mix_ps[:, D:D + EXPERTS]
        bo_ps = tp_ps[:, 0:D]
        wT_ps = tp_ps[0:EXPERTS, KC * P:KC * P + P]

        weights_in = sem("weights_in")
        later_in = sem("later_in")
        wgnn_in = sem("wgnn_in")
        experts_in = sem("experts_in")
        dst_in = sem("dst_in")
        const_made = sem("const_made")
        setup_chain = sem("setup_chain")
        was_done = sem("was_done")
        wh_ready = sem("wh_ready")
        weights_ready = sem("weights_ready")
        phase2_ready = sem("phase2_ready")
        x_in = [sem(f"x_in{i}") for i in range(2)]
        normed = sem("normed")
        ln_chain = sem("ln_chain")
        xT_done = sem("xT_done")
        xT_copied = sem("xT_copied")
        k_done = sem("k_done")
        v_done = sem("v_done")
        h_done = sem("h_done")
        squared = sem("squared")
        h_staged = sem("h_staged")
        h_stored = [sem(f"h_stored{i}") for i in range(2)]
        kv_chain = sem("kv_chain")
        v_scaled = sem("v_scaled")
        bn_var = sem("bn_var")
        bn_rooted = sem("bn_rooted")
        x_var = sem("x_var")
        x_rooted = sem("x_rooted")
        kv_var = sem("kv_var")
        kv_rooted = sem("kv_rooted")
        z_done = sem("z_done")
        dt_done = sem("dt_done")
        mid_chain = sem("mid_chain")
        dt_copied = sem("dt_copied")
        z_copied = sem("z_copied")
        m_done = sem("m_done")
        m_copied = sem("m_copied")
        counts_summed = sem("counts_summed")
        sched_rows = sem("sched_rows")
        sched_cols = sem("sched_cols")
        sched_ready = sem("sched_ready")
        steps_masked = sem("steps_masked")
        steps_summed = sem("steps_summed")
        gmax_local = sem("gmax_local")
        gmax_all = sem("gmax_all")
        self_scores = sem("self_scores")
        self_probs = sem("self_probs")
        idx_in = [sem(f"idx_in{i}") for i in range(RING)]
        gathered = [sem(f"gathered{i}") for i in range(RING)]
        step_begun = sem("step_begun")
        window_made = sem("window_made")
        kept_made = sem("kept_made")
        rows_ready = sem("rows_ready")
        oht_ready = sem("oht_ready")
        adg_ready = sem("adg_ready")
        score_chain = sem("score_chain")
        scores_ready = sem("scores_ready")
        probs_ready = sem("probs_ready")
        msg_ready = [sem("msg_a_ready"), sem("msg_b_ready")]
        half_summed = [sem("half_a_summed"), sem("half_b_summed")]
        xin_in = [sem(f"xin_in{i}") for i in range(2)]
        xn_ready = sem("xn_ready")
        xnT2_done = sem("xnT2_done")
        xnT2_copied = sem("xnT2_copied")
        mix_done = sem("mix_done")
        tile_chain = sem("tile_chain")
        router_chain = sem("router_chain")
        self_ready = sem("self_ready")
        tile_summed = sem("tile_summed")
        sums_read = sem("sums_read")
        neg_ready = sem("neg_ready")
        neg_exped = sem("neg_exped")
        z_ready = sem("z_ready")
        zT_done = sem("zT_done")
        zT_copied = sem("zT_copied")
        router_done = sem("router_done")
        logits_ready = sem("logits_ready")
        wexp_done = sem("wexp_done")
        w_ready = sem("w_ready")
        wT_done = sem("wT_done")
        wT_copied = sem("wT_copied")
        bo_done = sem("bo_done")
        tile_done = sem("tile_done")
        ff_done = sem("ff_done")
        relu_done = sem("relu_done")
        acc_done = sem("acc_done")
        handed = sem("handed")
        zT_handed = sem("zT_handed")
        out_stored = sem("out_stored")

        def part_bases(g, q):
            g = g - 1
            return g * (3 * EXPERTS) + 3 * EPP * q, g * (2 * EXPERTS) + 2 * EPP * q, g * EXPERTS + EPP * q

        def loop_bases(g, q):
            return part_bases(g, q) if q < SUP else part_bases(g + 1, 0)

        block = ctx.enter_context(nc.Block())

        @block.sync
        def _(sp):
            def load_x(n, par):
                sp.dma_start(xt[par], x[bass.ds(n * P, P), :]).then_inc(x_in[par], 16)

            load_x(0, 0)
            load_x(1, 1)
            sp.dma_start(dst_all, dsts[0:P * DCOLS].rearrange("(p c) -> p c", p=P)).then_inc(dst_in, 16)
            sp.dma_start(wg[:, :, :], w_gnn.rearrange("(k p) n -> p k n", p=P)).then_inc(wgnn_in, 16)
            sp.dma_start(attb[:, :, :], att.rearrange("(k p) n -> p k n", p=P)).then_inc(wgnn_in, 16)
            sp.dma_start(wh[:, :, 0:D], w_gnn_t.rearrange("(k p) n -> p k n", p=P)).then_inc(wgnn_in, 16)

            def store_h(n, par):
                sp.wait_ge(h_staged, n + 1)
                sp.dma_start(h_rows[bass.ds(n * P, P), :], hst[par]).then_inc(h_stored[par], 16)

            for n in range(2):
                sp.wait_ge(normed, n + 1)
                load_x(n + 2, n % 2)
                store_h(n, n % 2)
            with sp.Fori(2, LAST - 2, 2) as n0:
                for par in range(2):
                    sp.wait_ge(normed, n0 + (par + 1))
                    load_x(n0 + (par + 2), par)
                    store_h(n0 + par, par)
            sp.wait_ge(normed, LAST - 1)
            load_x(LAST, 0)
            for n in range(LAST - 2, NT):
                store_h(n, n % 2)

            sp.wait_ge(sched_ready, 2)

            def edges(s, u, first):
                if not first:
                    sp.wait_ge(msg_ready[1], s - (RING - 1))
                e0 = sp.value_load(steps_i[0:1, bass.ds(s, 1)], min_val=0, max_val=EMAX)
                sp.dma_start(idx[:, u, :, :], sd[bass.ds(e0, STEP), :].rearrange("(p j) c -> p j c", p=P))\
                    .then_inc(idx_in[u], 16)
                sp.dma_start(dstrow[:, u, :], dsts[bass.ds(e0, STEP)].partition_broadcast(P))\
                    .then_inc(idx_in[u], 16)

            for u in range(RING):
                edges(u, u, True)
            rounds = sp.value_load(meta[0:1, 64:65], min_val=2, max_val=MAX_STEPS // RING)
            with sp.Fori(1, rounds) as r:
                for u in range(RING):
                    edges(r * RING + u, u, False)

        @block.gpsimd
        def _(pool):
            pool.memset(ident[:, :], 0.0).then_inc(const_made, 1)
            pool.memset(ones[:, :], 1.0)
            pool.memset(zeros[:, :], 0.0)
            pool.memset(hst[0].rearrange("p (c) -> p c"), 1.0)
            pool.memset(hst[1].rearrange("p (c) -> p c"), 1.0)
            pool.iota(iota_i, [[1, MAX_STEPS]], base=0, channel_multiplier=0)
            pool.iota(node_i[:, :], [[P, NT + 1]], base=0, channel_multiplier=1).then_inc(const_made, 1)
            pool.wait_ge(const_made, 2)
            pool.affine_select(out=ident[:, :], in_=ident[:, :], compare_op=ALU.not_equal, fill=1.0, base=0,
                               pattern=[[-1, P]], channel_multiplier=1).then_inc(const_made, 1)
            pool.wait_ge(gmax_local, 1)
            pool.partition_all_reduce(gmax[:, 1, :], gmax[:, 0, :], P, bass.bass_isa.ReduceOp.max).then_inc(gmax_all, 1)

            pool.wait_ge(h_stored[0], 16 * ((NT + 1) // 2))
            pool.wait_ge(h_stored[1], 16 * (NT // 2))
            pool.wait_ge(sched_ready, 2)

            def gather(s, u, first, turn):
                if not first:
                    pool.wait_ge(msg_ready[1], s - (RING - 1))
                pool.wait_ge(idx_in[u], 32 * turn)
                pool.sem_inc(step_begun, 1)
                for j in range(TPS):
                    pool.indirect_dma_start(ring[:, u, j, :], None, h_rows[:, :],
                                            bass.IndirectOffsetOnAxis(ap=idx[:, u, j, 0:1], axis=0))\
                        .then_inc(gathered[u], 16)

            def landed(u, turn):
                pool.wait_ge(gathered[u], 16 * TPS * turn)
                pool.sem_inc(rows_ready, 1)

            for u in range(RING):
                gather(u, u, True, 1)
                if u:
                    landed(u - 1, 1)
            rounds = pool.value_load(meta[0:1, 64:65], min_val=2, max_val=MAX_STEPS // RING)
            with pool.Fori(1, rounds) as r:
                for u in range(RING):
                    gather(r * RING + u, u, False, r + 1)
                    landed((u - 1) % RING, r + 1 if u else r)
            landed(RING - 1, rounds)

        @block.scalar
        def _(act):
            act.dma_start(wkv[:, :, :], w_kv.rearrange("(k p) n -> p k n", p=P)).then_inc(weights_in, 16)
            act.dma_start(bnp[:, :, :], bn).then_inc(weights_in, 16)
            act.dma_start(rowsb[:, :], rows).then_inc(weights_in, 16)
            act.dma_start(wqt[:, :, :], w_q_t.rearrange("(k p) n -> p k n", p=P)).then_inc(later_in, 16)
            act.dma_start(wout[:, :, :], w_out.rearrange("(k p) n -> p k n", p=P)).then_inc(later_in, 16)
            act.dma_start(wr[:, :, :], w_r.rearrange("(k p) n -> p k n", p=P)).then_inc(later_in, 16)
            act.dma_start(bob[:, :], bo).then_inc(later_in, 16)
            def x_std(n):
                act.wait_ge(x_var, n + 1)
                act.activation(rs1[:, :], ve1[:, :], ACT.Sqrt).then_inc(x_rooted, 1)

            x_std(0)
            x_std(1)
            act.wait_ge(was_done, 1)
            act.wait_ge(wgnn_in, 48)
            act.activation(wh[:, :, D:D + 2 * HEADS],
                           small_ps[:, 0:KC * 2 * HEADS].rearrange("p (k c) -> p k c", k=KC), ACT.Copy)\
                .then_inc(wh_ready, 1)

            def copy_xT(n, par):
                act.wait_ge(xT_done, n + 1)
                act.activation(xnT[par], tp_ps[:, 0:KC * P], ACT.Copy).then_inc(xT_copied, 1)

            def evacuate_kv(n, par):
                act.wait_ge(k_done, n + 1)
                act.activation(ksb[par], k_ps[par][:, :], ACT.Copy)
                act.activation(sq[par][:, 0:INNER], k_ps[par][:, :], ACT.Square)
                act.wait_ge(v_done, n + 1)
                act.activation(sq[par][:, INNER:2 * INNER], v_ps[par][:, :], ACT.Square).then_inc(squared, 1)

            def evacuate_h(n, par):
                act.wait_ge(h_done, n + 1)
                if not (isinstance(n, int) and n < 2):
                    act.wait_ge(h_stored[par], (n - par) * 8)
                act.activation(hst[par][:, 0:HEADS * HG].rearrange("p (h c) -> p h c", h=HEADS)[:, :, 0:C],
                               mix_ps[:, 0:D].rearrange("p (h c) -> p h c", h=HEADS), ACT.Copy)
                act.activation(asad[:, bass.ds(n, 1), :].rearrange("p a c -> p (a c)"),
                               mix_ps[:, D:D + 2 * HEADS], ACT.Copy)
                act.activation(hst[par][:, HEADS * HG:ROW], mix_ps[:, D:D + HEADS], ACT.Copy)\
                    .then_inc(h_staged, 1)

            def kv_std(n):
                act.wait_ge(kv_var, n + 1)
                act.activation(rs2[:, :], ve2[:, :], ACT.Sqrt).then_inc(kv_rooted, 1)

            def tile1(n, par, left):
                evacuate_kv(n, par)
                if left > 0:
                    copy_xT(n + 1, 1 - par)
                evacuate_h(n, par)
                if left > 1:
                    x_std(n + 2)
                kv_std(n)


            def load_experts(dst, src):
                act.dma_start(dst[:, :, :, :], src.rearrange("e (k p) n -> p e k n", p=P)).then_inc(experts_in, 16)

            act.wait_ge(const_made, 3)
            copy_xT(0, 0)
            load_experts(w1b, w1)
            tile1(0, 0, 2)
            load_experts(w2b, w2)
            tile1(1, 1, 2)
            load_experts(wob, wo)
            with act.Fori(2, LAST - 2, 2) as n0:
                for par in range(2):
                    tile1(n0 + par, par, 2)
            for n in range(LAST - 2, NT):
                tile1(n, n % 2, LAST - n)

            act.wait_ge(bn_var, 1)
            act.activation(bns[:, :, :], bns[:, :, :], ACT.Sqrt).then_inc(bn_rooted, 1)
            act.wait_ge(z_done, 1)
            for j in range(2):
                act.activation(zsb[:, j * 512:(j + 1) * 512], k_ps[j][:, :], ACT.Copy).then_inc(z_copied, 1)
            act.wait_ge(self_scores, 1)
            act.activation(pself[:, :, :], small2[:, :, :], ACT.Exp).then_inc(self_probs, 1)
            act.wait_ge(m_done, 1)
            act.activation(msb[:, :, :], v_ps[0][:, :].rearrange("p (k n) -> p k n", k=KC), ACT.Copy,
                           scale=1.0 / n_nodes).then_inc(m_copied, 1)
            act.wait_ge(phase2_ready, 1)

            def load_tile(n, par):
                act.dma_start(xin[par], x[bass.ds(n * P, P), :]).then_inc(xin_in[par], 16)
                act.dma_start(hself[par], h_rows[bass.ds(n * P, P), :]).then_inc(xin_in[par], 16)

            def exp_step(s):
                act.wait_ge(scores_ready, s + 1)
                act.activation(prob[:, bass.ds(s % 2, 1), :, :].rearrange("p b j h -> p (b j h)"),
                               sc.rearrange("p j h -> p (j h)"), ACT.Exp).then_inc(probs_ready, 1)

            def copy_zT(n, q):
                act.wait_ge(zT_done, n + 1)
                act.activation(zT_slot(q), tp_ps[:, 0:KC * P].rearrange("p (k n) -> p k n", k=KC), ACT.Copy)\
                    .then_inc(zT_copied, 1)
                if q == SUP - 1:
                    hand_zT(n, q)

            def hand_zT(n, tiles):
                act.wait_ge(zT_copied, n + 1)
                act.activation(zTf[:, :, 0:tiles * P], zTb[:, :, 0:tiles * P], ACT.Copy).then_inc(zT_handed, 1)

            def copy_xnT(n):
                act.wait_ge(xnT2_done, n + 1)
                act.activation(xnTb, tp_ps[:, 0:KC * P], ACT.Copy).then_inc(xnT2_copied, 1)

            def exp_neg(n):
                act.wait_ge(neg_ready, n + 1)
                act.activation(neg, neg, ACT.Exp).then_inc(neg_exped, 1)

            def exp_router(n):
                act.wait_ge(logits_ready, n + 1)
                act.activation(small[:, 16:24], small[:, 8:16], ACT.Exp, accum_out=small[:, 24:25]).then_inc(wexp_done, 1)

            def copy_wT(n):
                act.wait_ge(wT_done, n + 1)
                act.activation(wT[0:EXPERTS, :], wT_ps, ACT.Copy).then_inc(wT_copied, 1)

            def section(n, q, bases=None, first_tile=False, stores=False):
                late, part_no = n - 1, (q - 1) % SUP
                if not first_tile:
                    act.wait_ge(self_ready, n)
                load_tile((n + 1) % NT, (q + 1) % 2)
                packed = act.value_load(meta[0:1, bass.ds(n, 1)], min_val=0, max_val=MAX_STEPS * SPLIT)
                first, body = act.snap(packed // SPLIT), act.snap(packed % SPLIT + 1)

                def relu(layer, *which):
                    if bases is not None:
                        for i in which:
                            expert_relu(part_no, bases, layer, i, SUP * P)

                exp_step(first + 1)
                if not first_tile:
                    exp_neg(late)
                relu(0, 0)
                exp_step(first + 2)
                if stores:
                    store_out(n)
                relu(0, 1, 2)
                exp_step(first + 3)
                relu(0, 3)
                exp_step(first + 4)
                relu(1, 0, 1)
                if not first_tile:
                    copy_zT(late, part_no)
                exp_step(first + 5)
                relu(1, 2)
                exp_step(first + 6)
                if not first_tile:
                    exp_router(late)
                relu(1, 3)
                copy_xnT(n)
                with act.Fori(0, body) as k:
                    exp_step(first + k + (HEAD + 1))
                exp_step(first + body + (HEAD + 1))
                if not first_tile:
                    copy_wT(late)
                exp_step(first + body + (HEAD + 2))

            def store_out(n):
                act.wait_ge(acc_done, n * EPP - EPP * (SUP + 1))
                act.dma_start(out[bass.ds(n * P - (2 * SUP + 1) * P, SUP * P), :].rearrange("(t p) c -> p t c", p=P),
                              outb).then_inc(out_stored, 16)

            def expert_relu(q, bases, layer, i, width):
                fbase, _, _ = bases
                act.wait_ge(ff_done, fbase + (EPP * layer + i + 1))
                for m in range(KC):
                    col = KC * (EPP * q + i) + m
                    ins = act.activation((h1, h2)[layer][i][:, m, 0:width], ff_ps[i][:, m * SUP * P:m * SUP * P + width], ACT.Relu,
                                         bias=bnt[:, layer, col:col + 1], scale=bns[:, layer, col:col + 1])
                ins.then_inc(relu_done, 1)

            act.sem_inc(out_stored, 16)
            load_tile(0, 0)
            exp_step(0)
            for n in range(SUP + 1):
                section(n, n % SUP, first_tile=n == 0)
            section(SUP + 1, 1, part_bases(1, 0))
            with act.Fori(1, NSUP - 1) as g:
                for q in range(2, SUP + 2):
                    section(g * SUP + q, q % SUP, loop_bases(g, q - 1), stores=q == SUP + 1)
            for q in range(2, SUP + 1):
                section(LAST - SUP + q, q % SUP, part_bases(NSUP - 1, q - 1))
            exp_neg(LAST)
            for i in range(4):
                expert_relu(0, part_bases(NSUP, 0), 0, i, SUP * P)
            copy_zT(LAST, 0)
            for i in range(4):
                expert_relu(0, part_bases(NSUP, 0), 1, i, SUP * P)
            exp_router(LAST)
            copy_wT(LAST)
            store_out(LAST + 1)
            for q in range(1, SUP):
                for layer in range(2):
                    for i in range(EPP):
                        expert_relu(q, part_bases(NSUP, q), layer, i, SUP * P)
                    if q == SUP - 1 and layer == 0:
                        hand_zT(LAST, 1)
            store_out(LAST + 1 + SUP)
            for q in range(SUP):
                for layer in range(2):
                    for i in range(4):
                        expert_relu(q, part_bases(NSUP + 1, q), layer, i, P)
            act.wait_ge(acc_done, (NSUP + 1) * EXPERTS)
            act.dma_start(out[LAST * P:NT * P, :], outb[:, 0, :]).then_inc(out_stored, 16)
            act.wait_ge(out_stored, 16 * (NSUP + 2))

        @block.vector
        def _(dve):
            dve.wait_ge(const_made, 3)
            prep = Chain(dve, setup_chain)
            dve.memset(base_f[:, 0:1], 0.0)
            dve.tensor_copy(node_pf[:, :], node_i[:, :])
            dve.memset(adc3[:, NT, :, :], 0.0)
            prep.link(dve.tensor_copy(iota_f[:, :], iota_i))
            prep.link(dve.tensor_scalar(base_f[:, 1:NT + 1], iota_f[:, 0:NT], 1.0, float(P), ALU.add, ALU.mult))
            dve.wait_ge(dst_in, 16)
            prep.link(dve.tensor_scalar(tile_i, dst_all, P.bit_length() - 1, None, ALU.arith_shift_right))
            prep.link(dve.tensor_copy(tile_of, tile_i))
            def norm(n, par, i, first=None):
                if i == 0:
                    dve.wait_ge(x_in[par], (n - par) * 8 + 16)
                    dve.bn_stats(stats[:, :], xt[par]).then_inc(ln_chain, 1)
                    dve.tensor_scalar(below, tile_of, iota_f[:, bass.ds(n + 1, 1)], 0.0, ALU.is_lt, ALU.add,
                                      accum_out=cnt[:, bass.ds(n, 1)])
                elif i == 1:
                    dve.wait_ge(ln_chain, n * 3 + 1)
                    dve.memset(small[:, 63:64], 0.0)
                    dve.bn_aggr(mv[:, :], stats[:, :]).then_inc(ln_chain, 1)
                elif i == 2:
                    dve.wait_ge(ln_chain, n * 3 + 2)
                    dve.tensor_scalar(ve1[:, :], mv[:, 1:2], EPS, None, ALU.add).then_inc(x_var, 1)
                    dve.tensor_copy(mean_n[:, bass.ds(n, 1)], mv[:, 0:1])
                elif i == 3:
                    dve.wait_ge(x_rooted, n + 1)
                    dve.reciprocal(rstd_n[:, bass.ds(n, 1)], rs1[:, 0:1]).then_inc(ln_chain, 1)
                else:
                    if first is None:
                        dve.wait_ge(xT_done, n - 1)
                    dve.wait_ge(ln_chain, n * 3 + 3)
                    dve.tensor_scalar(xn[par], xt[par], mv[:, 0:1], rstd_n[:, bass.ds(n, 1)], ALU.subtract, ALU.mult)\
                        .then_inc(normed, 1)

            def scale_v(n, par, i):
                if i == 0:
                    dve.wait_ge(squared, n + 1)
                    dve.tensor_reduce(small[:, 0:16], sq[par].rearrange("p (h c) -> p h c", c=MD), axis=AX_X, op=ALU.add)\
                        .then_inc(kv_chain, 1)
                elif i == 1:
                    dve.wait_ge(kv_chain, n * 3 + 1)
                    dve.tensor_scalar(small[:, 16:32], small[:, 0:16], 1.0 / MD, EPS, ALU.mult, ALU.add).then_inc(kv_chain, 1)
                elif i == 2:
                    dve.wait_ge(kv_chain, n * 3 + 2)
                    dve.tensor_tensor(ve2[:, :], small[:, 16:24], small[:, 24:32], ALU.mult).then_inc(kv_var, 1)
                elif i == 3:
                    dve.wait_ge(kv_rooted, n + 1)
                    dve.reciprocal(rs3[:, :], rs2[:, :]).then_inc(kv_chain, 1)
                else:
                    dve.wait_ge(kv_chain, n * 3 + 3)
                    dve.tensor_tensor(vsb[par].rearrange("p (h c) -> p h c", c=MD),
                                      v_ps[par][:, :].rearrange("p (h c) -> p h c", c=MD),
                                      rs3[:, :].unsqueeze(2).broadcast_to([P, MH, MD]), ALU.mult).then_inc(v_scaled, 1)

            def turn(n, par):
                norm(n + 2, par, 0)
                scale_v(n, par, 0)
                norm(n + 2, par, 1)
                scale_v(n, par, 1)
                norm(n + 2, par, 2)
                scale_v(n, par, 2)
                norm(n + 2, par, 3)
                norm(n + 2, par, 4)
                scale_v(n, par, 3)
                scale_v(n, par, 4)

            for n in range(2):
                for i in range(5):
                    norm(n, n, i, True)
            dve.wait_ge(weights_in, 48)
            for k in range(KC):
                prep.link(dve.tensor_reduce(mean16[:, k, :], wkv[:, k, :].rearrange("p (h c) -> p h c", c=MD), axis=AX_X,
                                            op=ALU.add))
            prep.link(dve.tensor_scalar(mean16[:, :, :], mean16[:, :, :], 1.0 / MD, None, ALU.mult))
            for k in range(KC):
                dve.tensor_tensor(wkv[:, k, :].rearrange("p (h c) -> p h c", c=MD),
                                  wkv[:, k, :].rearrange("p (h c) -> p h c", c=MD),
                                  mean16[:, k, :].unsqueeze(2).broadcast_to([P, 16, MD]), ALU.subtract)
            par10 = bnp[:, :, :].rearrange("p (l f) c -> p l f c", l=2)
            dve.tensor_scalar(bns[:, :, :], par10[:, :, 4, :], BN_EPS, None, ALU.add).then_inc(bn_var, 1)
            dve.tensor_scalar(rowsb[:, D:2 * D], rowsb[:, D:2 * D], -1.0, None, ALU.add).then_inc(weights_ready, 1)
            dve.wait_ge(weights_ready, 1)

            with dve.Fori(0, LAST - 2, 2) as n0:
                turn(n0, 0)
                turn(n0 + 1, 1)
            turn(LAST - 2, 0)
            link = Chain(dve, mid_chain).link
            dve.wait_ge(counts_summed, 1)
            rp, k_f, k_sum, t0, tmp = (sched[:, i, :] for i in range(5))
            link(dve.memset(sched[:, :, :], 0.0))
            link(dve.tensor_copy(rp[:, 1:NT + 1], small_ps[0:1, 0:NT]))
            link(dve.tensor_tensor(tmp[:, 0:NT], rp[:, 1:NT + 1], rp[:, 0:NT], ALU.subtract))
            link(dve.tensor_scalar(sched_i[:, 0, 0:NT], tmp[:, 0:NT], float(STEP - 1), None, ALU.add))
            link(dve.tensor_scalar(sched_i[:, 1, 0:NT], sched_i[:, 0, 0:NT], STEP.bit_length() - 1, None, ALU.arith_shift_right))
            link(dve.tensor_scalar(k_f[:, 0:NT], sched_i[:, 1, 0:NT], float(HEAD + 1 + TAIL), None, ALU.max))
            zero_row = sched[:, 7, 0:NT]
            link(dve.tensor_tensor_scan(k_sum[:, 0:NT], k_f[:, 0:NT], zero_row, 0.0, ALU.add, ALU.add))
            link(dve.tensor_tensor(t0[:, 0:NT], k_sum[:, 0:NT], k_f[:, 0:NT], ALU.subtract))
            link(dve.tensor_scalar(sched_i[:, 2, 0:1], k_sum[:, NT - 1:NT], float(RING + 1), None, ALU.add))
            link(dve.tensor_scalar(sched_i[:, 3, 0:1], sched_i[:, 2, 0:1], RING.bit_length() - 1, None, ALU.arith_shift_right))
            link(dve.tensor_copy(meta[:, 64:65], sched_i[:, 3, 0:1]))
            link(dve.tensor_scalar(tmp[:, 0:1], sched_i[:, 3, 0:1], float(RING), -2.0, ALU.mult, ALU.add))
            link(dve.tensor_tensor(k_f[:, NT - 1:NT], tmp[:, 0:1], t0[:, NT - 1:NT], ALU.subtract))
            link(dve.tensor_scalar(tmp[:, 0:NT], k_f[:, 0:NT], -float(HEAD + 1 + TAIL), None, ALU.add))
            link(dve.scalar_tensor_tensor(meta[:, 0:NT], t0[:, 0:NT], float(SPLIT), tmp[:, 0:NT], ALU.mult, ALU.add))
            base_n, dif = sched[:, 5, :], sched[:, 6, :]
            link(dve.scalar_tensor_tensor(base_n[:, 1:NT + 1], t0[:, 0:NT], -float(STEP), rp[:, 0:NT], ALU.mult, ALU.add))
            dve.tensor_tensor(dif[:, 0:NT], base_n[:, 1:NT + 1], base_n[:, 0:NT], ALU.subtract).then_inc(sched_rows, 1)
            dve.wait_ge(sched_cols, 1)
            link(dve.tensor_copy(cols[0:NT, :], small_ps[0:NT, 64:66]))
            dve.tensor_scalar(steps_f[0:NT, :], iota_f[0:NT, :], cols[0:NT, 0:1], cols[0:NT, 1:2], ALU.is_ge, ALU.mult)\
                .then_inc(steps_masked, 1)
            for i in range(5):
                scale_v(LAST - 1, 1, i)
            dve.wait_ge(steps_summed, 1)
            for i, ps in enumerate((mix_ps, tp_ps)):
                part_ = slice(i * MAX_STEPS // 2, (i + 1) * MAX_STEPS // 2)
                dve.scalar_tensor_tensor(steps_i[:, part_], iota_f[0:1, part_], float(STEP), ps[0:1, 0:MAX_STEPS // 2],
                                         ALU.mult, ALU.add).then_inc(sched_ready, 1)
            dve.wait_ge(h_staged, NT)
            dve.tensor_reduce(gmax[:, 0, :], asad[:, :, 0:HEADS].rearrange("p n h -> p h n"), axis=AX_X, op=ALU.max)\
                .then_inc(gmax_local, 1)
            for i in range(5):
                scale_v(LAST, 0, i)
            dve.wait_ge(bn_rooted, 1)
            link(dve.reciprocal(bns[:, :, :], bns[:, :, :]))
            link(dve.tensor_tensor(bns[:, :, :], bns[:, :, :], par10[:, :, 1, :], ALU.mult))
            link(dve.tensor_tensor(bnt[:, :, :], par10[:, :, 0, :], par10[:, :, 3, :], ALU.subtract))
            link(dve.tensor_tensor(bnt[:, :, :], bnt[:, :, :], bns[:, :, :], ALU.mult))
            dve.tensor_tensor(bnt[:, :, :], bnt[:, :, :], par10[:, :, 2, :], ALU.add)
            link(dve.tensor_scalar(keep_a[:, :], rstd_n[:, :], 1.0, None, ALU.add))
            link(dve.scalar_tensor_tensor(keep_b[:, :], mean_n[:, :], -1.0, rstd_n[:, :], ALU.mult, ALU.mult))
            link(dve.memset(dtb, 0.0))
            dve.wait_ge(dt_done, NT + 1)
            dt_v = acc_ps[:, :].rearrange("p (j c) -> p j c", j=4)
            dt_b = dtb.rearrange("p (j c) -> p j c", j=4)
            dve.tensor_copy(dt_b[0:MD, :, 0:MD], dt_v[0:MD, :, 0:MD])
            dve.tensor_copy(dt_b[MD:P, :, MD:P], dt_v[MD:P, :, MD:P]).then_inc(dt_copied, 1)
            dve.wait_ge(gmax_all, 1)
            tgt = asad[:, :, HEADS:2 * HEADS]
            link(dve.tensor_tensor(small2[:, :, :], tgt, gmax[:, 1, :].unsqueeze(1).broadcast_to([P, NT, HEADS]), ALU.add))
            link(dve.scalar_tensor_tensor(shift[:, :, :], small2[:, :, :], 0.2, small2[:, :, :], ALU.mult, ALU.max))
            link(dve.tensor_scalar(shift[:, :, :], shift[:, :, :], -GUARD, None, ALU.add))
            link(dve.tensor_tensor(small2[:, :, :], asad[:, :, 0:HEADS], tgt, ALU.add))
            link(dve.scalar_tensor_tensor(pself[:, :, :], small2[:, :, :], 0.2, small2[:, :, :], ALU.mult, ALU.max))
            link(dve.tensor_tensor(small2[:, :, :], pself[:, :, :], shift[:, :, :], ALU.subtract))
            dve.tensor_scalar(small2[:, :, :], small2[:, :, :], GUARD, None, ALU.min).then_inc(self_scores, 1)
            link(dve.tensor_tensor(adc[:, :, 0:HEADS], tgt, shift[:, :, :], ALU.subtract))
            link(dve.scalar_tensor_tensor(adc[:, :, HEADS:2 * HEADS], tgt, 0.2, shift[:, :, :], ALU.mult, ALU.subtract))
            link(dve.tensor_copy(adc3[:, 0:NT, 0, :], adc[:, :, :]))
            link(dve.tensor_tensor(adc_r[:, :, :], adc[:, :, :], adc3[:, 0:NT, 0, :], ALU.subtract))
            link(dve.tensor_copy(adc3[:, 0:NT, 1, :], adc_r[:, :, :]))
            link(dve.tensor_tensor(adc_r[:, :, :], adc_r[:, :, :], adc3[:, 0:NT, 1, :], ALU.subtract))
            link(dve.tensor_copy(adc3[:, 0:NT, 2, :], adc_r[:, :, :]))
            dve.wait_ge(self_probs, 1)
            dve.wait_ge(h_stored[0], 16 * ((NT + 1) // 2))
            dve.wait_ge(h_stored[1], 16 * (NT // 2))
            link(dve.tensor_copy(small[:, 0:1], keep_a[:, 0:1]))
            link(dve.tensor_copy(small[:, 1:2], keep_b[:, 0:1]))
            dve.tensor_copy(small[:, 2:3], keep_b[:, 0:1]).then_inc(phase2_ready, 1)

            def slot(s):
                return bass.ds(s % RING, 1)

            def onehot_t(n, s):
                dve.wait_ge(rows_ready, s + 1)
                src = dstrow[:, slot(s), :].rearrange("p a (e j) -> p (a j) e", j=TPS)
                dve.tensor_scalar(oht, src, node_pf[:, bass.ds(n, 1)], None, ALU.is_equal).then_inc(oht_ready, 1)

            def scores_read(s):
                dve.wait_ge(adg_ready, s + 1)
                a_src = ring[:, slot(s), :, HEADS * HG:ROW].rearrange("p a j c -> p (a j) c")
                dve.tensor_tensor(sc_a, adg_ps[:, :, 0:HEADS], a_src, ALU.add)
                dve.scalar_tensor_tensor(sc_b, a_src, 0.2, adg_ps[:, :, HEADS:2 * HEADS], ALU.mult, ALU.add)\
                    .then_inc(score_chain, 1)

            def scores_leaky(s):
                dve.wait_ge(score_chain, s * 2 + 1)
                dve.tensor_tensor(sc_a, sc_a, sc_b, ALU.max).then_inc(score_chain, 1)

            def scores_bound(s):
                dve.wait_ge(score_chain, s * 2 + 2)
                dve.tensor_scalar(sc, sc_a, GUARD, None, ALU.min).then_inc(scores_ready, 1)

            def onehot(s, half, par, turn, again):
                dve.wait_ge(half_summed[half], s + (2 if again else 1))
                d = idx[:, slot(s), 2 * half:2 * half + 2, 1].rearrange("p a j -> p (a j)")
                dve.tensor_tensor(oh[half][:, turn, :, :], window[par].unsqueeze(1).broadcast_to([P, 2, P]),
                                  d.unsqueeze(2).broadcast_to([P, 2, P]), ALU.is_equal)

            def message(s, half, turn):
                if half == 0:
                    dve.wait_ge(probs_ready, s + 1)
                js = slice(2 * half, 2 * half + 2)
                rows_ = ring[:, slot(s), js, 0:HEADS * HG].rearrange("p a j (h c) -> p (a j) h c", h=HEADS)
                w_ = prob[:, bass.ds(s % 2, 1), js, :].rearrange("p a j h -> p (a j) h")
                m_ = msg[half][:, turn, :, :].rearrange("p j (h c) -> p j h c", h=HEADS)
                dve.tensor_tensor(m_, rows_, w_.unsqueeze(3).broadcast_to([P, 2, HEADS, HG]), ALU.mult)\
                    .then_inc(msg_ready[half], 1)

            def late(n, q, i):
                par = q % 2
                links = n * 20

                def after(k):
                    dve.wait_ge(tile_chain, links + k)

                sums = gsum.rearrange("p (h c) -> p h c", h=HEADS)
                x1 = x1b[:, q, :]
                v, y, t = rsq[:, 0:1], rsq[:, 1:2], rsq[:, 2:3]
                if i == 0:
                    dve.wait_ge(tile_summed, n + 1)
                    dve.tensor_tensor(gsum, acc_ps[:, 0:HEADS * HG], mself, ALU.add).then_inc(sums_read, 1)
                elif i == 1:
                    dve.wait_ge(sums_read, n + 1)
                    dve.tensor_scalar(small[:, 0:4], sums[:, :, C], 1e-16, None, ALU.add).then_inc(tile_chain, 1)
                elif i == 2:
                    after(1)
                    dve.reciprocal(small[:, 4:8], small[:, 0:4]).then_inc(tile_chain, 1)
                elif i == 3:
                    after(2)
                    dve.tensor_tensor(gat.rearrange("p (h c) -> p h c", h=HEADS), sums[:, :, 0:C],
                                      small[:, 4:8].unsqueeze(2).broadcast_to([P, HEADS, C]), ALU.mult).then_inc(tile_chain, 1)
                elif i == 4:
                    after(3)
                    dve.tensor_tensor(gat, gat, rowsb[:, 0:D], ALU.add).then_inc(tile_chain, 1)
                elif i == 5:
                    after(4)
                    dve.tensor_scalar(neg, gat, 0.0, None, ALU.min).then_inc(neg_ready, 1)
                elif i == 6:
                    dve.wait_ge(mix_done, n + 1)
                    dve.tensor_tensor(kept[par], kept[par], mix_ps[:, 0:D], ALU.add).then_inc(tile_chain, 1)
                elif i == 7:
                    dve.wait_ge(neg_exped, n + 1)
                    dve.scalar_tensor_tensor(gat, gat, 0.0, neg, ALU.max, ALU.add).then_inc(tile_chain, 1)
                elif i == 8:
                    after(6)
                    dve.tensor_tensor(x1, gat, kept[par], ALU.add).then_inc(tile_chain, 1)
                elif i == 9:
                    after(7)
                    dve.bn_stats(stats[:, :], x1).then_inc(tile_chain, 1)
                elif i == 10:
                    after(8)
                    dve.memset(small[:, 63:64], 0.0)
                    dve.bn_aggr(mv[:, :], stats[:, :]).then_inc(tile_chain, 1)
                elif i == 11:
                    after(9)
                    dve.tensor_scalar(v, mv[:, 1:2], EPS, None, ALU.add).then_inc(tile_chain, 1)
                elif i == 12:
                    after(10)
                    dve.tensor_scalar(y.bitcast(I32), v.bitcast(I32), -0.5, float(0x5f3759df), ALU.mult, ALU.add)\
                        .then_inc(tile_chain, 1)
                elif i <= 21:
                    after(i - 2)
                    if i % 3 == 1:
                        ins = dve.scalar_tensor_tensor(t, y, v, y, ALU.mult, ALU.mult)
                    elif i % 3 == 2:
                        ins = dve.tensor_scalar(t, t, -0.5, 1.5, ALU.mult, ALU.add)
                    else:
                        ins = dve.tensor_tensor(y, y, t, ALU.mult)
                    ins.then_inc(tile_chain, 1)
                else:
                    after(20)
                    dve.tensor_scalar(zb, x1, mv[:, 0:1], y, ALU.subtract, ALU.mult).then_inc(z_ready, 1)

            def router(n, q, i):
                if i == 0:
                    dve.wait_ge(router_done, n + 1)
                    dve.tensor_tensor(small[:, 8:16], rt_ps, rowsb[:, 2 * D:2 * D + EXPERTS], ALU.add)\
                        .then_inc(router_chain, 1)
                elif i == 1:
                    dve.wait_ge(router_chain, n * 3 + 1)
                    dve.tensor_reduce(small[:, 41:42], small[:, 8:16], axis=AX_X, op=ALU.max).then_inc(router_chain, 1)
                elif i == 2:
                    dve.wait_ge(router_chain, n * 3 + 2)
                    dve.tensor_scalar(small[:, 8:16], small[:, 8:16], small[:, 41:42], None, ALU.subtract)\
                        .then_inc(logits_ready, 1)
                elif i == 3:
                    dve.wait_ge(wexp_done, n + 1)
                    dve.reciprocal(small[:, 42:43], small[:, 24:25]).then_inc(router_chain, 1)
                else:
                    dve.wait_ge(router_chain, n * 3 + 3)
                    dve.tensor_scalar(wgt[:, q, :], small[:, 16:24], small[:, 42:43], None, ALU.mult).then_inc(w_ready, 1)

            def late_bias(n, q):
                dve.wait_ge(bo_done, n + 1)
                dve.tensor_tensor(x1b[:, q, :], x1b[:, q, :], bo_ps, ALU.add).then_inc(tile_done, 1)

            def own(n, q, i):
                par, col = q % 2, bass.ds(n, 1)
                if i == 0:
                    dve.wait_ge(xin_in[par], (n - par) * 16 + 32)
                    dve.tensor_scalar(xnb, xin[par], mean_n[:, col], rstd_n[:, col], ALU.subtract, ALU.mult)\
                        .then_inc(xn_ready, 1)
                elif i == 1:
                    dve.tensor_scalar(kept[par], xin[par], keep_a[:, col], keep_b[:, col], ALU.mult, ALU.add)\
                        .then_inc(kept_made, 1)
                elif i == 2:
                    dve.tensor_tensor(mself.rearrange("p (h c) -> p h c", h=HEADS),
                                      hself[par][:, 0:HEADS * HG].rearrange("p (h c) -> p h c", h=HEADS),
                                      pself[:, col, :].rearrange("p a h -> p (a h)").unsqueeze(2)
                                      .broadcast_to([P, HEADS, HG]), ALU.mult).then_inc(self_ready, 1)
                elif i == 3:
                    dve.wait_ge(kept_made, n + 1)
                    dve.tensor_tensor(kept[par], kept[par], rowsb[:, D:2 * D], ALU.add)
                else:
                    set_window(n + 1, 1 - par)

            def set_window(n, par):
                dve.tensor_scalar(window[par], iota_f[:, 0:P], base_f[:, bass.ds(n, 1)], None, ALU.add)\
                    .then_inc(window_made, 1)

            def section(n, q, now=None, before=None, handoff=None, fresh=None, first_tile=False,
                        second_tile=False):
                par, part_no = q % 2, (q - 1) % SUP
                last_q, q2 = (q - 1) % SUP, (q - 2) % SUP
                packed = dve.value_load(meta[0:1, bass.ds(n, 1)], min_val=0, max_val=MAX_STEPS * SPLIT)
                first, body = dve.snap(packed // SPLIT), dve.snap(packed % SPLIT + 1)

                def rest(*pieces):
                    if not first_tile:
                        for i in pieces:
                            late(n - 1, last_q, i)

                def route(*pieces):
                    if not first_tile:
                        for i in pieces:
                            router(n - 1, last_q, i)

                def step(s, ahead, turn, again=False, p1=(), p2=(), p3=(), p4=(), p5=(), p6=(), p7=(), do=rest):
                    scores_read(s + 1)
                    do(*p1)
                    onehot(s, 0, par, turn, again)
                    do(*p2)
                    scores_leaky(s + 1)
                    do(*p3)
                    message(s, 0, turn)
                    do(*p4)
                    scores_bound(s + 1)
                    onehot_t(ahead, s + 2)
                    do(*p5)
                    onehot(s, 1, par, turn, again)
                    do(*p6)
                    message(s, 1, turn)
                    do(*p7)

                dve.wait_ge(window_made, n + 1)
                step(first, n, 0, True, (), (), (), (0,), (1,), (2, 3), (4,))
                if before is not None:
                    expert_sum((part_no - 1) % SUP, before, EPP - 2, SUP, None, fresh)
                rest(5)
                step(first + 1, n, 1, False, (), (), (), (6,), (), (7,))
                if before is not None:
                    expert_sum((part_no - 1) % SUP, before, EPP - 1, SUP, None, fresh)
                if not (first_tile or second_tile):
                    late_bias(n - 2, q2)
                if handoff is not None and part_no == 0:
                    hand_over(n - 1, SUP, None if before is None else n * EPP - EPP * (SUP + 1))
                    dve.wait_ge(handed, handoff)
                step(first + 2, n, 0, False, (8,), (9,), (10,), (11,), (12,), (13,), (14,))
                step(first + 3, n, 1, False, (15,), (16,), (17, 18), (19,), (20,), (21,), (22,))
                own(n, q, 0)
                step(first + 4, n, 0)
                for i in range(1, 5):
                    own(n, q, i)
                step(first + 5, n, 1, False, (), (0,), (), (1,), (2,), do=route)
                with dve.Fori(0, body) as k:
                    step(first + k + HEAD, n, 0, True)
                step(first + body + HEAD, n + 1, 1, False, (), (3,), (), (4,), do=route)
                if now is not None:
                    expert_sum(part_no, now, 0, SUP, handoff)
                step(first + body + (HEAD + 1), n + 1, 0)
                if now is not None:
                    expert_sum(part_no, now, 1, SUP, handoff)

            def expert_sum(q, bases, i, tiles, handoff, fresh=None):
                fbase, _, abase = bases
                e = EPP * q + i
                dve.wait_ge(ff_done, fbase + (2 * EPP + 1 + i))
                if e == 0:
                    dve.wait_ge(handed, handoff)
                else:
                    dve.wait_ge(acc_done, abase + i)
                last = e == EXPERTS - 1
                if last:
                    dve.wait_ge(out_stored, fresh)
                for t in range(tiles):
                    ins = dve.scalar_tensor_tensor((outb if last else acc)[:, t, :], ff_ps[i][:, t * D:(t + 1) * D],
                                                   wgf[:, t, e:e + 1], acc[:, t, :], ALU.mult, ALU.add)
                ins.then_inc(acc_done, 1)

            def hand_over(n_done, tiles, summed):
                if summed is not None:
                    dve.wait_ge(acc_done, summed)
                dve.wait_ge(tile_done, n_done)
                dve.tensor_copy(acc[:, 0:tiles, :], x1b[:, 0:tiles, :])
                dve.tensor_copy(wgf[:, 0:tiles, :], wgt[:, 0:tiles, :]).then_inc(handed, 1)

            set_window(0, 0)
            onehot_t(0, 0)
            scores_read(0)
            scores_leaky(0)
            scores_bound(0)
            onehot_t(0, 1)
            for n in range(SUP + 1):
                section(n, n % SUP, first_tile=n == 0, second_tile=n == 1)
            section(SUP + 1, 1, part_bases(1, 0), handoff=1)
            with dve.Fori(1, NSUP - 1) as g:
                for q in range(2, SUP + 2):
                    section(g * SUP + q, q % SUP, loop_bases(g, q - 1), part_bases(g, q - 2),
                            g + (1 if q > SUP else 0), 16 * g)
            for q in range(2, SUP + 1):
                section(LAST - SUP + q, q % SUP, part_bases(NSUP - 1, q - 1), part_bases(NSUP - 1, q - 2), NSUP - 1)
            for i in range(2, 4):
                expert_sum(SUP - 1, part_bases(NSUP - 1, SUP - 1), i, SUP, None, 16 * (NSUP - 1))
            late_bias(LAST - 1, SUP - 1)
            late(LAST, 0, 0)
            late(LAST, 0, 1)
            hand_over(LAST, SUP, EXPERTS * (NSUP - 1))
            for i in range(2, 23):
                late(LAST, 0, i)
            for i in range(5):
                router(LAST, 0, i)
            for q in range(SUP):
                for i in range(4):
                    expert_sum(q, part_bases(NSUP, q), i, SUP, NSUP, 16 * NSUP)
                if q == 0:
                    late_bias(LAST, 0)
            hand_over(LAST + 1, 1, EXPERTS * NSUP)
            for q in range(SUP):
                for i in range(EPP):
                    expert_sum(q, part_bases(NSUP + 1, q), i, 1, NSUP + 1, 16 * (NSUP + 1))

        @block.tensor
        def _(pe):
            def product(out_, pairs, sem_=None, start=True, stop=True):
                for i, (lhsT, rhs) in enumerate(pairs):
                    ins = pe.matmul(out_, lhsT, rhs, start=start and i == 0, stop=stop and i == len(pairs) - 1)
                if sem_ is not None:
                    ins.then_inc(sem_, 1)

            pe.wait_ge(const_made, 3)
            pe.wait_ge(wgnn_in, 48)
            for k in range(KC):
                product(small_ps[:, k * 2 * HEADS:(k + 1) * 2 * HEADS],
                        [(wg[:, o, k * P:(k + 1) * P], attb[:, o, :]) for o in range(KC)],
                        was_done if k == KC - 1 else None)
            product(acc_ps[:, :], [(zeros[:, 0:P], zeros[:, :])], stop=False)

            def transpose_x(n, par):
                pe.wait_ge(normed, n + 1)
                for k in range(KC):
                    ins = pe.transpose(tp_ps[:, k * P:(k + 1) * P], xn[par][:, k * P:(k + 1) * P], ident[:, :])
                ins.then_inc(xT_done, 1)

            def sum_dt(n, par):
                pe.wait_ge(v_scaled, n + 1)
                for j in range(4):
                    ins = pe.matmul(acc_ps[:, j * P:(j + 1) * P], vsb[par][:, j * P:(j + 1) * P],
                                    ksb[par][:, j * P:(j + 1) * P], start=False, stop=False)
                ins.then_inc(dt_done, 1)

            def project(n, par):
                pe.wait_ge(xT_copied, n + 1)
                xT = [xnT[par][:, k * P:(k + 1) * P] for k in range(KC)]
                product(k_ps[par][:, :], [(xT[k], wkv[:, k, 0:INNER]) for k in range(KC)], k_done)
                product(v_ps[par][:, :], [(xT[k], wkv[:, k, INNER:2 * INNER]) for k in range(KC)], v_done)
                if not (isinstance(n, int) and n == 0):
                    pe.wait_ge(h_staged, n)
                product(mix_ps[:, 0:D + 2 * HEADS], [(xT[k], wh[:, k, :]) for k in range(KC)], h_done)

            pe.wait_ge(weights_ready, 1)
            pe.wait_ge(wh_ready, 1)
            for n in range(2):
                transpose_x(n, n)
                project(n, n)
            with pe.Fori(2, LAST, 2) as n0:
                for par in range(2):
                    transpose_x(n0 + par, par)
                    sum_dt(n0 + (par - 2), par)
                    project(n0 + par, par)
            transpose_x(LAST, 0)
            product(small_ps[0:1, 0:NT], [(ones[:, 0:1], cnt[:, 0:NT])], counts_summed)
            sum_dt(LAST - 2, 0)
            project(LAST, 0)
            pe.wait_ge(sched_rows, 1)
            product(small_ps[0:NT, 64:65], [(sched[0:1, 3, 0:NT], ones[0:1, 0:1])])
            product(small_ps[0:NT, 65:66], [(sched[0:1, 6, 0:NT], ones[0:1, 0:1])], sched_cols)
            pe.wait_ge(steps_masked, 1)
            pe.wait_ge(h_staged, NT)
            for i, ps in enumerate((mix_ps, tp_ps)):
                product(ps[0:1, 0:MAX_STEPS // 2],
                        [(ones[0:NT, 0:1], steps_f[0:NT, i * MAX_STEPS // 2:(i + 1) * MAX_STEPS // 2])],
                        steps_summed if i else None)
            sum_dt(LAST - 1, 1)
            sum_dt(LAST, 0)
            product(acc_ps[:, :], [(zeros[:, 0:P], zeros[:, :])], dt_done, start=False)

            pe.wait_ge(dt_copied, 1)
            pe.wait_ge(later_in, 64)
            for j in range(4):
                product(k_ps[j // 2][:, (j % 2) * D:(j % 2 + 1) * D], [(dtb[:, j * P:(j + 1) * P], wout[:, j, :])],
                        z_done if j == 3 else None)
            pe.wait_ge(z_copied, 2)
            for f in range(KC):
                product(v_ps[0][:, f * D:(f + 1) * D],
                        [(wqt[:, j, f * P:(f + 1) * P], zsb[:, j * D:(j + 1) * D]) for j in range(4)],
                        m_done if f == KC - 1 else None)

            pe.wait_ge(phase2_ready, 1)
            for half in range(2):
                pe.sem_inc(half_summed[half], 2)

            def target_scores(n, s):
                pe.wait_ge(oht_ready, s + 1)
                for j in range(TPS):
                    for i in range(3):
                        ins = pe.matmul(adg_ps[:, j, :], oht[:, j, :],
                                        adc3[:, bass.ds(n, 1), i, :].rearrange("p a c -> p (a c)"), start=i == 0, stop=i == 2)
                ins.then_inc(adg_ready, 1)

            def sum_half(s, half, turn, opens=False, closes=False):
                pe.wait_ge(msg_ready[half], s + 1)
                for j in range(2):
                    ins = pe.matmul(acc_ps[:, 0:HEADS * HG], oh[half][:, turn, j, :],
                                    msg[half][:, turn, j, :],
                                    start=opens and j == 0, stop=closes and j == 1)
                if closes:
                    ins.then_inc(tile_summed, 1)
                    pe.sem_inc(half_summed[half], 1)
                else:
                    ins.then_inc(half_summed[half], 1)

            def layer1(q, bases, width, handoff, i):
                _, _, abase = bases
                if not (isinstance(abase, int) and abase == 0):
                    pe.wait_ge(acc_done, abase + (i - (EPP - 1)))
                if q == 0 and i == 0:
                    pe.wait_ge(zT_handed, handoff)
                for m in range(KC):
                    product(ff_ps[i][:, m * SUP * P:m * SUP * P + width],
                            [(w1b[:, EPP * q + i, k, m * P:(m + 1) * P], zTf[:, k, 0:width]) for k in range(KC)],
                            ff_done if m == KC - 1 else None)

            def layer2(q, bases, width, i):
                _, rbase, _ = bases
                pe.wait_ge(relu_done, rbase + (i + 1))
                for m in range(KC):
                    product(ff_ps[i][:, m * SUP * P:m * SUP * P + width],
                            [(w2b[:, EPP * q + i, k, m * P:(m + 1) * P], h1[i][:, k, 0:width]) for k in range(KC)],
                            ff_done if m == KC - 1 else None)

            def layer3(q, bases, tiles, i):
                _, rbase, _ = bases
                pe.wait_ge(relu_done, rbase + (EPP + i + 1))
                for t in range(tiles):
                    product(ff_ps[i][:, t * D:(t + 1) * D],
                            [(h2[i][:, k, t * P:(t + 1) * P], wob[:, EPP * q + i, k, :]) for k in range(KC)],
                            ff_done if t == tiles - 1 else None)

            def transpose_pair(src, done):
                for k in range(KC):
                    ins = pe.transpose(tp_ps[:, k * P:(k + 1) * P], src[:, k * P:(k + 1) * P], ident[:, :])
                ins.then_inc(done, 1)

            def late_zT(n):
                pe.wait_ge(z_ready, n + 1)
                transpose_pair(zb, zT_done)

            def late_router(n, q):
                pe.wait_ge(zT_copied, n + 1)
                product(rt_ps, [(zT_slot(q)[:, k, :], wr[:, k, :]) for k in range(KC)], router_done)

            def late_wT(n, q):
                pe.wait_ge(w_ready, n + 1)
                pe.transpose(wT_ps, wgt[:, q, :], ident[:, :]).then_inc(wT_done, 1)

            def late_bo(n):
                pe.wait_ge(wT_copied, n + 1)
                product(bo_ps, [(wT[0:EXPERTS, :], bob[:, :])], bo_done)

            def section(n, q, bases=None, handoff=None, first_tile=False, last_tile=False):
                part_no = (q - 1) % SUP
                packed = pe.value_load(meta[0:1, bass.ds(n, 1)], min_val=0, max_val=MAX_STEPS * SPLIT)
                first, body = pe.snap(packed // SPLIT), pe.snap(packed % SPLIT + 1)

                def step(s, turn, ahead=None, opens=False, closes=False):
                    sum_half(s, 0, turn, opens)
                    if ahead is not None:
                        target_scores(ahead, s + 2)
                    sum_half(s, 1, turn, closes=closes)

                def experts(layer, *which):
                    if bases is not None:
                        for i in which:
                            if layer == 1:
                                layer1(part_no, bases, SUP * P, handoff, i)
                            elif layer == 2:
                                layer2(part_no, bases, SUP * P, i)
                            else:
                                layer3(part_no, bases, SUP, i)

                if not first_tile:
                    pe.wait_ge(sums_read, n)
                step(first, 0, opens=True)
                experts(1, 0)
                step(first + 1, 1, n)
                experts(1, 1)
                target_scores(n, first + 4)
                experts(1, 2)
                step(first + 2, 0)
                experts(1, 3)
                step(first + 3, 1, n)
                experts(2, 0)
                target_scores(n, first + 6)
                experts(2, 1)
                if not first_tile:
                    late_zT(n - 1)
                step(first + 4, 0)
                if not first_tile:
                    late_router(n - 1, part_no)
                experts(2, 2)
                step(first + 5, 1, n)
                experts(2, 3)
                experts(3, 0)
                pe.wait_ge(xn_ready, n + 1)
                transpose_pair(xnb, xnT2_done)
                with pe.Fori(0, body) as k:
                    target_scores(n, first + k + (HEAD + 2))
                    sum_half(first + k + HEAD, 0, 0)
                    sum_half(first + k + HEAD, 1, 0)
                experts(3, 1)
                step(first + body + HEAD, 1, n + 1)
                pe.wait_ge(xnT2_copied, n + 1)
                if not first_tile:
                    late_wT(n - 1, part_no)
                if first_tile:
                    pe.wait_ge(m_copied, 1)
                product(mix_ps[:, 0:D], [(xnTb[:, k * P:(k + 1) * P], msb[:, k, :]) for k in range(KC)], mix_done)
                step(first + body + (HEAD + 1), 0, n + 1, closes=True)
                if not first_tile:
                    late_bo(n - 1)
                experts(3, 2)
                if not last_tile:
                    target_scores(n + 1, first + body + (HEAD + TAIL + 2))
                experts(3, 3)

            target_scores(0, 0)
            target_scores(0, 1)
            target_scores(0, 2)
            for n in range(SUP + 1):
                section(n, n % SUP, first_tile=n == 0)
            pe.wait_ge(experts_in, 48)
            section(SUP + 1, 1, part_bases(1, 0), 1)
            with pe.Fori(1, NSUP - 1) as g:
                for q in range(2, SUP + 2):
                    section(g * SUP + q, q % SUP, loop_bases(g, q - 1), g + (1 if q > SUP else 0))
            for q in range(2, SUP + 1):
                section(LAST - SUP + q, q % SUP, part_bases(NSUP - 1, q - 1), NSUP - 1, last_tile=q == SUP)
            for q in range(SUP):
                for i in range(4):
                    layer1(q, part_bases(NSUP, q), SUP * P, NSUP, i)
                if q == 0:
                    late_zT(LAST)
                for i in range(4):
                    layer2(q, part_bases(NSUP, q), SUP * P, i)
                if q == 0:
                    late_router(LAST, 0)
                    late_wT(LAST, 0)
                    late_bo(LAST)
                for i in range(4):
                    layer3(q, part_bases(NSUP, q), SUP, i)
            for q in range(SUP):
                for i in range(4):
                    layer1(q, part_bases(NSUP + 1, q), P, NSUP + 1, i)
                for i in range(4):
                    layer2(q, part_bases(NSUP + 1, q), P, i)
                for i in range(4):
                    layer3(q, part_bases(NSUP + 1, q), 1, i)


def kernel(x, src, dst, L0_gnn_W, L0_gnn_att_src, L0_gnn_att_dst, L0_gnn_bias, L0_mix_w_qkv, L0_mix_w_out, L0_mix_b_out,
           L0_ffn_Wr, L0_ffn_br, L0_ffn_W1, L0_ffn_b1, L0_ffn_g1, L0_ffn_be1, L0_ffn_m1, L0_ffn_v1, L0_ffn_W2, L0_ffn_b2,
           L0_ffn_g2, L0_ffn_be2, L0_ffn_m2, L0_ffn_v2, L0_ffn_Wo, L0_ffn_bo):
    import numpy as np
    import concourse.bacc as bacc
    from concourse.bass_utils import run_bass_kernel_spmd

    f = np.ascontiguousarray
    n, e = x.shape[0], src.shape[0]
    rows_pad = -(-n // P) * P - n
    edge_pad = -(-e // P) * P - e + STEP * (RING + HEAD + 1 + TAIL + 4)
    srcp = np.concatenate([np.asarray(src), np.zeros(edge_pad, np.int32)])
    dstp = np.concatenate([np.asarray(dst), np.full(edge_pad, 1 << 20, np.int32)])
    att = np.zeros((D, 2 * HEADS), np.float32)
    for h in range(HEADS):
        att[h * C:(h + 1) * C, h] = np.asarray(L0_gnn_att_src)[h]
        att[h * C:(h + 1) * C, HEADS + h] = np.asarray(L0_gnn_att_dst)[h]
    rows = np.tile(np.concatenate([np.asarray(L0_gnn_bias), np.asarray(L0_mix_b_out), np.asarray(L0_ffn_br)])[None], (P, 1))
    params = [L0_ffn_b1, L0_ffn_g1, L0_ffn_be1, L0_ffn_m1, L0_ffn_v1, L0_ffn_b2, L0_ffn_g2, L0_ffn_be2, L0_ffn_m2, L0_ffn_v2]
    bn = np.stack([np.asarray(a).reshape(2 * EXPERTS, P).T for a in params], axis=1)
    qkv = np.asarray(L0_mix_w_qkv)
    ins = {
        "in_x": f(np.pad(np.asarray(x), ((0, rows_pad), (0, 0)))),
        "in_sd": f(np.stack([srcp, dstp], axis=1)),
        "in_dst": f(dstp),
        "in_att": att,
        "in_w_gnn": f(L0_gnn_W),
        "in_w_gnn_t": f(np.asarray(L0_gnn_W).T),
        "in_rows": f(rows),
        "in_w_kv": f(qkv[:, INNER:]),
        "in_w_q_t": f(qkv[:, :INNER].T),
        "in_w_out": f(L0_mix_w_out),
        "in_w_r": f(L0_ffn_Wr),
        "in_bn": f(bn),
        "in_w1": f(L0_ffn_W1),
        "in_w2": f(L0_ffn_W2),
        "in_wo": f(L0_ffn_Wo),
        "in_bo": f(L0_ffn_bo),
    }
    nc = bacc.Bacc("TRN2", target_bir_lowering=False, num_devices=1)
    args = [nc.dram_tensor(k, a.shape, mybir.dt.from_np(a.dtype), kind="ExternalInput").ap() for k, a in ins.items()]
    out = nc.dram_tensor("out_x", (n + rows_pad, D), F32, kind="ExternalOutput").ap()
    gps_layer(nc, *args, out, n, e)
    r = run_bass_kernel_spmd(nc, [ins], core_ids=[0])
    return r.results[0]["out_x"][:n]
```
